# Optimizing a Trainium2 kernel written in Bass

```python
import numpy as np
import jax
import jax.numpy as jnp

def _softmax(x, axis=-1):
    return jax.nn.softmax(x, axis=axis)

def _gelu(x):
    return jax.nn.gelu(x, approximate=True)

def _silu(x):
    return jax.nn.silu(x)

def _sigmoid(x):
    return jax.nn.sigmoid(x)

def _layernorm(x, axis=-1, eps=1e-05):
    m = jnp.mean(x, axis=axis, keepdims=True)
    v = jnp.var(x, axis=axis, keepdims=True)
    return (x - m) / jnp.sqrt(v + eps)

def _scatter_add(tgt, idx, src, axis=0):
    return tgt.at[idx].add(src)

def _segment_sum(src, seg, n):
    return jax.ops.segment_sum(src, seg, n)
kernel_name = 'mk_seq_postln_d2_jaxref_r4_2fa0f6'

def setup_inputs(seed: int=0):
    np.random.seed(seed)
    _w = jnp.asarray

    def _L0_attn_setup():
        import jax, jax.numpy as jnp
        import numpy as np
        D_MODEL = 256
        D_STATE = 16
        DT_RANK = 64
        DT_MIN = 0.001
        DT_MAX = 0.1
        key = jax.random.key(seed)
        ks = jax.random.split(key, 7)
        B, S = (2, 512)
        return {'x': jax.random.normal(ks[0], (B, S, D_MODEL), jnp.float32), 'w_in': jax.random.normal(ks[1], (D_MODEL, D_MODEL), jnp.float32) / np.sqrt(D_MODEL).astype(np.float32), 'w_x': jax.random.normal(ks[2], (D_MODEL, DT_RANK + 2 * D_STATE), jnp.float32) / np.sqrt(D_MODEL).astype(np.float32), 'w_dt': jax.random.normal(ks[3], (DT_RANK, D_MODEL), jnp.float32) / np.sqrt(DT_RANK).astype(np.float32), 'b_dt': jnp.zeros((D_MODEL,), jnp.float32), 'A_log': jax.random.normal(ks[5], (D_MODEL, D_STATE), jnp.float32) * 0.5, 'Dp': jax.random.normal(ks[6], (D_MODEL,), jnp.float32)}
    _L0_attn_in = _L0_attn_setup()

    def _L0_ffn_setup():
        import jax, jax.numpy as jnp
        import numpy as np
        B, S, D = (8, 1024, 256)
        E, R, K = (6, 16, 2)
        key = jax.random.key(seed)
        ks = jax.random.split(key, 9)
        sc = 0.02
        return {'x': jax.random.normal(ks[0], (B, S, D), jnp.float32), 'base_W': jax.random.normal(ks[1], (D, D), jnp.float32) * sc, 'base_b': jax.random.normal(ks[2], (D,), jnp.float32) * sc, 'shared_A': jax.random.normal(ks[3], (R, D), jnp.float32) * sc, 'shared_B': jax.random.normal(ks[4], (D, R), jnp.float32) * sc, 'routed_A': jax.random.normal(ks[5], (E, R, D), jnp.float32) * sc, 'routed_B': jax.random.normal(ks[6], (E, D, R), jnp.float32) * sc, 'router_W': jax.random.normal(ks[7], (E, D), jnp.float32) * sc, 'router_b': jax.random.normal(ks[8], (E,), jnp.float32) * sc}
    _L0_ffn_in = _L0_ffn_setup()

    def _L1_attn_setup():
        import math
        import jax, jax.numpy as jnp
        import numpy as np
        N_HEAD = 16
        N_EMBD = 256
        HEAD_DIM = N_EMBD // N_HEAD
        SHARED = 16
        PRIV = HEAD_DIM - SHARED
        B, T = (4, 512)
        STD = 0.02
        key = jax.random.key(seed)
        ks = jax.random.split(key, 6)
        x = jax.random.normal(ks[0], (B, T, N_EMBD), dtype=jnp.float32)
        W_share = jax.random.normal(ks[1], (N_EMBD, SHARED), dtype=jnp.float32) * STD
        Wq = jax.random.normal(ks[2], (N_EMBD, N_HEAD * PRIV), dtype=jnp.float32) * STD
        Wk = jax.random.normal(ks[3], (N_EMBD, N_HEAD * PRIV), dtype=jnp.float32) * STD
        Wv = jax.random.normal(ks[4], (N_EMBD, N_EMBD), dtype=jnp.float32) * STD
        Wo = jax.random.normal(ks[5], (N_EMBD, N_EMBD), dtype=jnp.float32) * STD
        return {'hidden_states': x, 'W_share': W_share, 'b_share': jnp.zeros((SHARED,), jnp.float32), 'Wq': Wq, 'bq': jnp.zeros((N_HEAD * PRIV,), jnp.float32), 'Wk': Wk, 'bk': jnp.zeros((N_HEAD * PRIV,), jnp.float32), 'Wv': Wv, 'bv': jnp.zeros((N_EMBD,), jnp.float32), 'Wo': Wo, 'bo': jnp.zeros((N_EMBD,), jnp.float32)}
    _L1_attn_in = _L1_attn_setup()

    def _L1_ffn_setup():
        import jax, jax.numpy as jnp
        import numpy as np
        D_MODEL, D_FF, NUM_EXPERTS, RANK, TOP_K = (256, 1024, 8, 16, 2)
        B, S = (8, 512)

        def _expert_ffn(h, wi_w, wo_w, A, Bm):
            inter = jnp.einsum('bsd,fd->bsf', h, wi_w)
            lora = jnp.einsum('bsr,fr->bsf', jnp.einsum('bsd,rd->bsr', h, A), Bm)
            inter = jax.nn.relu(inter + lora)
            return jnp.einsum('bsf,df->bsd', inter, wo_w)
        key = jax.random.key(seed)
        ks = jax.random.split(key, 8)
        hidden_states = jax.random.normal(ks[0], (B, S, D_MODEL), dtype=jnp.float32)
        wi_w = jax.random.normal(ks[1], (D_FF, D_MODEL), dtype=jnp.float32) * (1.0 / np.sqrt(D_MODEL))
        wo_w = jax.random.normal(ks[2], (D_MODEL, D_FF), dtype=jnp.float32) * (1.0 / np.sqrt(D_FF))
        lora_As = jax.random.uniform(ks[3], (NUM_EXPERTS, RANK, D_MODEL), dtype=jnp.float32, minval=-1.0, maxval=1.0) / np.sqrt(D_MODEL)
        lora_Bs = jax.random.normal(ks[4], (NUM_EXPERTS, D_FF, RANK), dtype=jnp.float32) * 0.02
        top_k_indices = jnp.arange(TOP_K, dtype=jnp.int32)
        top_k_values = jax.random.uniform(ks[5], (TOP_K,), dtype=jnp.float32)
        return {'hidden_states': hidden_states, 'wi_w': wi_w, 'wo_w': wo_w, 'lora_As': lora_As, 'lora_Bs': lora_Bs, 'top_k_indices': top_k_indices, 'top_k_values': top_k_values}
    _L1_ffn_in = _L1_ffn_setup()
    _d = {'L0_attn_x': _L0_attn_in['x'], 'L0_attn_w_in': _L0_attn_in['w_in'], 'L0_attn_w_x': _L0_attn_in['w_x'], 'L0_attn_w_dt': _L0_attn_in['w_dt'], 'L0_attn_b_dt': _L0_attn_in['b_dt'], 'L0_attn_A_log': _L0_attn_in['A_log'], 'L0_attn_Dp': _L0_attn_in['Dp'], 'L0_ffn_base_W': _L0_ffn_in['base_W'], 'L0_ffn_base_b': _L0_ffn_in['base_b'], 'L0_ffn_shared_A': _L0_ffn_in['shared_A'], 'L0_ffn_shared_B': _L0_ffn_in['shared_B'], 'L0_ffn_routed_A': _L0_ffn_in['routed_A'], 'L0_ffn_routed_B': _L0_ffn_in['routed_B'], 'L0_ffn_router_W': _L0_ffn_in['router_W'], 'L0_ffn_router_b': _L0_ffn_in['router_b'], 'L1_attn_W_share': _L1_attn_in['W_share'], 'L1_attn_b_share': _L1_attn_in['b_share'], 'L1_attn_Wq': _L1_attn_in['Wq'], 'L1_attn_bq': _L1_attn_in['bq'], 'L1_attn_Wk': _L1_attn_in['Wk'], 'L1_attn_bk': _L1_attn_in['bk'], 'L1_attn_Wv': _L1_attn_in['Wv'], 'L1_attn_bv': _L1_attn_in['bv'], 'L1_attn_Wo': _L1_attn_in['Wo'], 'L1_attn_bo': _L1_attn_in['bo'], 'L1_ffn_wi_w': _L1_ffn_in['wi_w'], 'L1_ffn_wo_w': _L1_ffn_in['wo_w'], 'L1_ffn_lora_As': _L1_ffn_in['lora_As'], 'L1_ffn_lora_Bs': _L1_ffn_in['lora_Bs'], 'L1_ffn_top_k_indices': _L1_ffn_in['top_k_indices'], 'L1_ffn_top_k_values': _L1_ffn_in['top_k_values']}
    _x0 = _d['L0_attn_x']
    _d['L0_attn_x'] = jax.random.normal(jax.random.fold_in(jax.random.key(seed), 1), (2, 2048, 256), dtype=_x0.dtype)
    del _x0
    return _d

def reference(L0_attn_x, L0_attn_w_in, L0_attn_w_x, L0_attn_w_dt, L0_attn_b_dt, L0_attn_A_log, L0_attn_Dp, L0_ffn_base_W, L0_ffn_base_b, L0_ffn_shared_A, L0_ffn_shared_B, L0_ffn_routed_A, L0_ffn_routed_B, L0_ffn_router_W, L0_ffn_router_b, L1_attn_W_share, L1_attn_b_share, L1_attn_Wq, L1_attn_bq, L1_attn_Wk, L1_attn_bk, L1_attn_Wv, L1_attn_bv, L1_attn_Wo, L1_attn_bo, L1_ffn_wi_w, L1_ffn_wo_w, L1_ffn_lora_As, L1_ffn_lora_Bs, L1_ffn_top_k_indices, L1_ffn_top_k_values):

    def _L0_attn_ref(x, w_in, w_x, w_dt, b_dt, A_log, Dp):
        import jax, jax.numpy as jnp
        import numpy as np
        D_MODEL = 256
        D_STATE = 16
        DT_RANK = 64
        DT_MIN = 0.001
        DT_MAX = 0.1
        x_in = jnp.einsum('bsd,de->bse', x, w_in)
        proj = jnp.einsum('bsd,dp->bsp', x_in, w_x)
        dt_low, Bm, Cm = jnp.split(proj, [DT_RANK, DT_RANK + D_STATE], axis=-1)
        dt = jax.nn.softplus(jnp.einsum('bsr,rd->bsd', dt_low, w_dt) + b_dt) * (DT_MAX - DT_MIN) + DT_MIN
        A = -jnp.exp(A_log)
        b, s, d = x.shape
        h0 = jnp.zeros((b, d, D_STATE), x.dtype)
        dt_tm = jnp.swapaxes(dt, 0, 1)
        u_tm = jnp.swapaxes(x_in, 0, 1)
        B_tm = jnp.swapaxes(Bm, 0, 1)
        C_tm = jnp.swapaxes(Cm, 0, 1)

        def step(h, inp):
            dtt, ut, bt, ct = inp
            dA = dtt[:, :, None] * A
            barA = jnp.exp(dA)
            inp_term = jnp.einsum('bdn,bn,bd->bn', dA, bt, ut)
            h = barA * h + inp_term[:, None, :]
            y = jnp.einsum('bdn,bn->bd', h, ct) + Dp * ut
            return (h, y)
        _, ys = jax.lax.scan(step, h0, (dt_tm, u_tm, B_tm, C_tm))
        return jnp.swapaxes(ys, 0, 1)

    def _L0_ffn_ref(x, base_W, base_b, shared_A, shared_B, routed_A, routed_B, router_W, router_b):
        import jax, jax.numpy as jnp
        import numpy as np
        B, S, D = (8, 1024, 256)
        E, R, K = (6, 16, 2)
        base_out = jax.lax.stop_gradient(jnp.einsum('bsi,oi->bso', x, base_W) + base_b)
        shared_out = jnp.einsum('bsr,or->bso', jnp.einsum('bsi,ri->bsr', x, shared_A), shared_B)
        logits = jnp.einsum('bsi,ei->bse', x, router_W) + router_b
        gate = jax.nn.softmax(logits, axis=-1)
        topk_w, topk_i = jax.lax.top_k(gate, K)
        sparse_w = jnp.sum(jax.nn.one_hot(topk_i, E, dtype=gate.dtype) * topk_w[..., None], axis=-2)
        sparse_w = sparse_w / (jnp.sum(sparse_w, axis=-1, keepdims=True) + 1e-06)
        h = jnp.einsum('bsi,eri->bser', x, routed_A)
        routed_outs = jnp.einsum('bser,eor->bseo', h, routed_B)
        routed_out = jnp.einsum('bseo,bse->bso', routed_outs, sparse_w)
        return base_out + shared_out + routed_out

    def _L1_attn_ref(hidden_states, W_share, b_share, Wq, bq, Wk, bk, Wv, bv, Wo, bo):
        import math
        import jax, jax.numpy as jnp
        import numpy as np
        N_HEAD = 16
        N_EMBD = 256
        HEAD_DIM = N_EMBD // N_HEAD
        SHARED = 16
        PRIV = HEAD_DIM - SHARED
        B, T = (4, 512)
        STD = 0.02
        x = hidden_states
        Bt, Tt, C = x.shape
        share = x @ W_share + b_share
        share_h = jnp.broadcast_to(share[:, None, :, :], (Bt, N_HEAD, Tt, SHARED))
        q_priv = (x @ Wq + bq).reshape(Bt, Tt, N_HEAD, PRIV).transpose(0, 2, 1, 3)
        k_priv = (x @ Wk + bk).reshape(Bt, Tt, N_HEAD, PRIV).transpose(0, 2, 1, 3)
        q = jnp.concatenate([share_h, q_priv], axis=-1)
        k = jnp.concatenate([share_h, k_priv], axis=-1)
        v = (x @ Wv + bv).reshape(Bt, Tt, N_HEAD, HEAD_DIM).transpose(0, 2, 1, 3)
        scale = 1.0 / math.sqrt(HEAD_DIM)
        att = jnp.einsum('bhqd,bhkd->bhqk', q, k) * scale
        causal = jnp.tril(jnp.ones((Tt, Tt), dtype=bool))
        att = jnp.where(causal[None, None, :, :], att, -jnp.inf)
        att = jax.nn.softmax(att, axis=-1)
        y = jnp.einsum('bhqk,bhkd->bhqd', att, v)
        y = y.transpose(0, 2, 1, 3).reshape(Bt, Tt, C)
        y = y @ Wo + bo
        return y

    def _L1_ffn_ref(hidden_states, wi_w, wo_w, lora_As, lora_Bs, top_k_indices, top_k_values):
        import jax, jax.numpy as jnp
        import numpy as np
        D_MODEL, D_FF, NUM_EXPERTS, RANK, TOP_K = (256, 1024, 8, 16, 2)
        B, S = (8, 512)

        def _expert_ffn(h, wi_w, wo_w, A, Bm):
            inter = jnp.einsum('bsd,fd->bsf', h, wi_w)
            lora = jnp.einsum('bsr,fr->bsf', jnp.einsum('bsd,rd->bsr', h, A), Bm)
            inter = jax.nn.relu(inter + lora)
            return jnp.einsum('bsf,df->bsd', inter, wo_w)
        out = jnp.zeros_like(hidden_states)
        for k in range(top_k_values.shape[0]):
            A = jnp.take(lora_As, top_k_indices[k], axis=0)
            Bm = jnp.take(lora_Bs, top_k_indices[k], axis=0)
            out = out + top_k_values[k] * _expert_ffn(hidden_states, wi_w, wo_w, A, Bm)
        return out
    x = L0_attn_x
    x = _layernorm(x + _L0_attn_ref(x, L0_attn_w_in, L0_attn_w_x, L0_attn_w_dt, L0_attn_b_dt, L0_attn_A_log, L0_attn_Dp), axis=-1)
    x = _layernorm(x + _L0_ffn_ref(x, L0_ffn_base_W, L0_ffn_base_b, L0_ffn_shared_A, L0_ffn_shared_B, L0_ffn_routed_A, L0_ffn_routed_B, L0_ffn_router_W, L0_ffn_router_b), axis=-1)
    x = _layernorm(x + _L1_attn_ref(x, L1_attn_W_share, L1_attn_b_share, L1_attn_Wq, L1_attn_bq, L1_attn_Wk, L1_attn_bk, L1_attn_Wv, L1_attn_bv, L1_attn_Wo, L1_attn_bo), axis=-1)
    x = _layernorm(x + _L1_ffn_ref(x, L1_ffn_wi_w, L1_ffn_wo_w, L1_ffn_lora_As, L1_ffn_lora_Bs, L1_ffn_top_k_indices, L1_ffn_top_k_values), axis=-1)
    return x

_drawn_inputs = setup_inputs


def setup_inputs(seed=0):
    import zlib

    import numpy as np

    out = dict(_drawn_inputs(seed))
    spreads = {'L0_attn_b_dt': (0.0, 0.1),
     'L1_attn_b_share': (0.0, 0.8),
     'L1_attn_bv': (0.0, 0.27),
     'L1_attn_bo': (0.0, 0.1)}
    factors = {'L0_ffn_base_b': 2.768,
     'L0_ffn_routed_A': 3.336,
     'L0_ffn_routed_B': 3.379,
     'L0_ffn_router_W': 4.0,
     'L0_ffn_router_b': 8.0,
     'L1_attn_W_share': 8.0,
     'L1_attn_Wv': 7.262,
     'L1_ffn_top_k_values': 8.0}
    for name, (base, spread) in spreads.items():
        noise = np.random.default_rng([zlib.crc32(name.encode()), seed]).standard_normal(out[name].shape)
        drawn = base * np.exp(spread * noise) if base else spread * noise
        out[name] = jnp.asarray(drawn.astype(out[name].dtype))
    for name, factor in factors.items():
        out[name] = (out[name] * factor).astype(out[name].dtype)
    return out
```

```python
from contextlib import ExitStack

import concourse.bass as bass
from concourse import mybir

F32 = mybir.dt.float32
F32R = mybir.dt.float32r
BF16 = mybir.dt.bfloat16
I32 = mybir.dt.int32
ALU = mybir.AluOpType
ACT = mybir.ActivationFunctionType
AX = mybir.AxisListType

P = 128
B, S, D = 2, 2048, 256
KD = D // P
T = 512
TT = T // P
CPB = S // T
NCH = B * CPB
N = 16
E, R = 6, 16
EP = E + 1
HR = EP * R
CAT = D + HR + E
FF = 1024
FB = FF // P
DT_MIN, DT_MAX = 0.001, 0.1
EPS = 1e-5
SCALE = 0.25
NEG = -1e38
RANKL = 96


def program(nc, a):
    with ExitStack() as ctx:
        def sb(name, shape, dt=F32):
            return ctx.enter_context(nc.sbuf_tensor(name, shape, dt))

        def sem(name):
            return ctx.enter_context(nc.semaphore(name))

        ident = sb("ident", [P, P])
        ident_bf = sb("ident_bf", [P, P], BF16)
        mask_bf = sb("mask_bf", [P, P], BF16)
        mask_t_bf = sb("mask_t_bf", [P, P], BF16)
        ones = sb("ones", [P, P])
        sel_cols = sb("sel_cols", [P, 2 * N])
        sel = sb("sel", [P, 2 * N], F32R)
        w_in_h = sb("w_in_h", [P, KD, D], F32R)
        w_in_l = sb("w_in_l", [P, KD, D], F32R)
        w_pre_h = sb("w_pre_h", [P, KD, D + P], F32R)
        w_pre_l = sb("w_pre_l", [P, KD, D + P], F32R)
        b_dt = sb("b_dt", [P, KD])
        d_skip = sb("d_skip", [P, KD])
        a_neg = sb("a_neg", [P, KD, N])
        a_rep = sb("a_rep", [P, KD, P])
        a_h = sb("a_h", [P, KD, P], F32R)
        a_l = sb("a_l", [P, KD, P], F32R)
        w_cat_h = sb("w_cat_h", [P, KD, CAT], F32R)
        w_cat_l = sb("w_cat_l", [P, KD, CAT], F32R)
        w_up_h = sb("w_up_h", [HR + 1, D], F32R)
        w_up_l = sb("w_up_l", [HR + 1, D], F32R)
        r_bias = sb("r_bias", [P, TT, E])
        tie = sb("tie", [P, E, E])
        w_sh_h = sb("w_sh_h", [P, KD, P], F32R)
        w_sh_l = sb("w_sh_l", [P, KD, P], F32R)
        b_sh = sb("b_sh", [P, 1])
        w_vo_h = sb("w_vo_h", [P, KD, D], F32R)
        w_vo_l = sb("w_vo_l", [P, KD, D], F32R)
        bv_col = sb("bv_col", [P, KD])
        bo_row = sb("bo_row", [1, D])
        att_bias = sb("att_bias", [P, D])
        pick_cols = sb("pick_cols", [P, R])
        expert_of = sb("expert_of", [P, 1])
        top_i = sb("top_i", [P, 2], I32)
        top_f = sb("top_f", [P, 2])
        top_v = sb("top_v", [P, 2])
        picked = sb("picked", [P, 2])
        minus0 = sb("minus0", [P, 1])
        sel_a128 = sb("sel_a128", [P, P])
        sel_0 = sb("sel_0", [P, RANKL])
        sel_d = sb("sel_d", [P, RANKL])
        sgn = sb("sgn", [P, 2])
        absv = sb("absv", [P, 2])
        sgn01 = sb("sgn01", [P, 1])
        w_la_h = sb("w_la_h", [P, KD, P], F32R)
        w_la_l = sb("w_la_l", [P, KD, P], F32R)
        w_z0 = sb("w_z0", [RANKL, FF], F32R)
        w_zd = sb("w_zd", [RANKL, FF], F32R)
        w_i_h = sb("w_i_h", [P, KD, FF], F32R)
        w_i_l = sb("w_i_l", [P, KD, FF], F32R)
        w_out = sb("w_out", [P, FB, D])
        x_pre = sb("x_pre", [P, TT, D])
        x_res = sb("x_res", [P, TT, D])
        xs_h = sb("xs_h", [P, KD, T], F32R)
        xs_l = sb("xs_l", [P, KD, T], F32R)
        u_sb = sb("u_sb", [P, KD, T])
        dt_sb = sb("dt_sb", [P, 2, KD, T])
        sp_a = sb("sp_a", [P, KD, T])
        dtu = sp_a
        bc_sb = sb("bc_sb", [P, T])
        parts = sb("parts", [P, 2, T], F32R)
        bar = sb("bar", [P, 3, KD, T])
        hst = sb("hst", [P, 3, KD, T])
        c_rep = sb("c_rep", [P, 2, T])
        prod = sb("prod", [P, 2, KD, T])
        state = sb("state", [P, KD, N])
        acc = sb("acc", [P, KD, T])
        res = sb("res", [P, TT, D])
        bnst = sb("bnst", [P, TT, 6])
        mv = sb("mv", [P, TT, 2])
        veps = sb("veps", [P, TT])
        rstd = sb("rstd", [P, TT])
        nbias = sb("nbias", [P, TT])
        mhalf = sb("mhalf", [P, TT])
        xl_tm = sb("xl_tm", [P, 2, TT, D])
        xt_h = sb("xt_h", [P, KD, T], F32R)
        xt_l = sb("xt_l", [P, KD, T], F32R)
        lg = sb("lg", [P, TT, E])
        lmax = sb("lmax", [P, TT])
        ls = sb("ls", [P, TT, E])
        ex = sb("ex", [P, TT, E])
        rk_gt = sb("rk_gt", [P, TT, E, E])
        rk_eq = sb("rk_eq", [P, TT, E, E])
        rank = sb("rank", [P, TT, E])
        em = sb("em", [P, TT, E])
        e_sum = sb("e_sum", [P, TT])
        k_sum = sb("k_sum", [P, TT])
        gate = sb("gate", [P, TT, EP])
        hw = sb("hw", [P, TT, HR + 1])
        q_st = sb("q_st", [P, T], F32R)
        k_st = sb("k_st", [P, S], F32R)
        vc = sb("vc", [P, S // P, D + 1])
        smax = sb("smax", [P, TT, CPB])
        m4 = sb("m4", [P, TT])
        mhl = sb("mhl", [P, TT, 2], F32R)
        rl = sb("rl", [P, TT])
        lr = sb("lr", [RANKL, T], F32R)
        mid = sb("mid", [P, 2, T])
        ring = sb("ring", [P, 3, T])
        sp_m = mid
        x13, x24 = xl_tm[:, 0, :, :], xl_tm[:, 1, :, :]
        x2b = x24
        dtu_h, dtu_l = xs_h, xs_l
        hw_h, hw_l = xt_h[0:HR + 1, 0, :], xt_h[0:HR + 1, 1, :]

        vflat = vc[:, :, :].rearrange("p a b -> p (a b)")
        w_i_r = vflat[:, 0:KD * FF].rearrange("p (k f) -> p k f", k=KD)
        w_cat_r = vflat[:, KD * FF:KD * FF + KD * CAT].rearrange("p (k f) -> p k f", k=KD)
        lora_b = vflat[:, KD * (FF + CAT):KD * (FF + CAT) + FF]
        xflat = xl_tm[:, :, :, :].rearrange("p a t d -> p (a t d)")

        def cut(flat, at, blocks, width):
            return flat[:, at:at + blocks * width].rearrange("p (k n) -> p k n", k=blocks)

        w_in_r, w_in_t = cut(xflat, 0, KD, D), cut(xflat, KD * D, KD, D)
        dt_bc_r = cut(xflat, 2 * KD * D, KD, D + P)
        w_sh_r = cut(xflat, 3 * KD * D + KD * P, KD, P)
        rflat = res[:, :, :].rearrange("p t d -> p (t d)")
        w_v_t, w_o = cut(rflat, 0, KD, D), cut(rflat, KD * D, KD, D)
        mflat = ring[:, :, :].rearrange("p a t -> p (a t)")
        lora_a = mflat[:, 0:D]
        w_up_r = mflat[0:HR + 1, D:2 * D]
        bv_rep = cut(mflat, 4 * D, KD, P)
        w_xdt_t, w_dt = mflat[0:64, 2 * D:3 * D], mflat[0:64, 3 * D:4 * D]

        bi = ctx.enter_context(nc.psum_tensor("bi", [P, 2, T], F32))
        bc = ctx.enter_context(nc.psum_tensor("bc", [P, T], F32))
        gb = ctx.enter_context(nc.psum_tensor("gb", [P, 5, T], F32))

        ld_x, ld_r = sem("ld_x"), sem("ld_r")
        ld_pre, ld_cat, ld_att, ld_ffn = sem("ld_pre"), sem("ld_cat"), sem("ld_att"), sem("ld_ffn")
        consts = sem("consts")
        pc_ready = sem("pc_ready")
        wp_pe, wp_act, wp_dve = sem("wp_pe"), sem("wp_act"), sem("wp_dve")
        wd = sem("wd")
        wa = sem("wa")
        xs_t = sem("xs_t")
        xs_hi, xs_lo = sem("xs_hi"), sem("xs_lo")
        u_ps, z_ps, bc_ps, g_ps = sem("u_ps"), sem("z_ps"), sem("bc_ps"), sem("g_ps")
        u_cp, bc_cp = sem("u_cp"), sem("bc_cp")
        sp_abs, sp_exp, sp_ln = sem("sp_abs"), sem("sp_exp"), sem("sp_ln")
        sp_max, sp_sum, dt_ok = sem("sp_max"), sem("sp_sum"), sem("dt_ok")
        dtu_ok, dtu_hi, dtu_lo = sem("dtu_ok"), sem("dtu_hi"), sem("dtu_lo")
        inp_ok, inp_hi, inp_lo = sem("inp_ok"), sem("inp_hi"), sem("inp_lo")
        c_hi, c_lo = sem("c_hi"), sem("c_lo")
        bar_ok = sem("bar_ok")
        ir_ok, cr_ps = sem("ir_ok"), sem("cr_ps")
        cr_ok = sem("cr_ok")
        scan_ok = sem("scan_ok")
        st_ok = sem("st_ok")
        pr_ok = sem("pr_ok")
        acc_ok = sem("acc_ok")
        y_t = sem("y_t")
        ln_r, ln_bn, ln_mv, ln_ve = sem("ln_r"), sem("ln_bn"), sem("ln_mv"), sem("ln_ve")
        ln_rstd, ln_nb, ln_x = sem("ln_rstd"), sem("ln_nb"), sem("ln_x")
        xt_ps, xt_hi, xt_lo = sem("xt_ps"), sem("xt_hi"), sem("xt_lo")
        lgate = sem("lgate")
        cat_ps, lg_ok, rt, ex_ok, hw_ok = sem("cat_ps"), sem("lg_ok"), sem("rt"), sem("ex_ok"), sem("hw_ok")
        hwt_ps, hw_hi, hw_lo, up_ps = sem("hwt_ps"), sem("hw_hi"), sem("hw_lo"), sem("up_ps")
        sh_ps, q_hi, k_hi, q_lo, k_lo = sem("sh_ps"), sem("q_hi"), sem("k_hi"), sem("q_lo"), sem("k_lo")
        v_ps, v_ok, x2b_ok = sem("v_ps"), sem("v_ok"), sem("x2b_ok")
        s_ps, s_mx = sem("s_ps"), sem("s_mx")
        m_ok, mhl_ok, mt_ps, mt_ok = sem("m_ok"), sem("mhl_ok"), sem("mt_ps"), sem("mt_ok")
        st_ps, p_ok, pv_ok = sem("st_ps"), sem("p_ok"), sem("pv_ok")
        o_ok, rl_ok, o_res = sem("o_ok"), sem("rl_ok"), sem("o_res")
        l_ps, l_hi, l_lo = sem("l_ps"), sem("l_hi"), sem("l_lo")
        z0_ps, zd_ps, a0_ok, a1_ok, mid_ok, mid_used, out_ps = (
            sem("z0_ps"), sem("zd_ps"), sem("a0_ok"), sem("a1_ok"), sem("mid_ok"), sem("mid_used"), sem("out_ps"))
        stored = sem("stored")

        n_s = [TT * (g % CPB + 1) for g in range(NCH)]
        n_p = [[(4 * (g % CPB) + 2 * h + 2) // 2 for h in range(2)] for g in range(NCH)]
        s_base = [sum(n_s[:g]) for g in range(NCH)]
        p_base = [[sum(sum(x) for x in n_p[:g]) + (n_p[g][0] if h else 0) for h in range(2)] for g in range(NCH)]

        def row(g, n):
            return g * N + n

        def acc_at(k):
            return k + 1 + k // N + 1

        SL_Y, SL_N1, SL_X1, SL_CAT, SL_RT, SL_UP, SL_N2, SL_X2, SL_QV = 0, 1, 2, 3, 4, 5, 6, 6, 7
        SL_S, SL_P0, SL_P1, SL_N3, SL_X3, SL_L = 8, 9, 10, 11, 11, 12
        SL_F = [12, 12, 13, 13, 14, 14, 15, 15]
        PR_T, PR_MM, PR_SP, PR_G = 0, 1, 2, 3

        block = ctx.enter_context(nc.Block())

        @block.sync
        def _(sp):
            def load_x(g, dst, loaded):
                b, c = divmod(g, CPB)
                sp.dma_start(dst[:], a["x"][b, c * T:(c + 1) * T, :].rearrange("(t p) d -> p t d", p=P)
                             ).then_inc(loaded, 16)

            def rows(w):
                return w.rearrange("(k p) n -> p k n", p=P)

            load_x(0, x_pre, ld_x)
            load_x(0, x_res, ld_r)
            for dst, src in ((w_xdt_t, a["w_xdt_t"]), (w_dt, a["w_dt"]),
                             (w_in_t, rows(a["w_in_t"])), (w_in_r, rows(a["w_in"])),
                             (dt_bc_r[:, :, D:D + P], rows(a["w_bc"])), (b_dt[:], a["b_dt"]),
                             (d_skip[:], a["d_skip"]), (a_neg[:], a["a_log"]), (sel_cols[:], a["sel_cols"])):
                sp.dma_start(dst, src).then_inc(ld_pre, 16)
            for dst, src in ((w_cat_r, rows(a["w_cat"])), (w_up_r, a["w_up"]),
                             (r_bias[:], a["r_bias"]), (tie[:], a["tie"])):
                sp.dma_start(dst, src).then_inc(ld_cat, 16)
            for dst, src in ((w_sh_r, rows(a["w_sh"])), (b_sh[:], a["b_sh"]), (w_v_t, rows(a["w_v_t"])),
                             (w_o, rows(a["w_o"])), (bv_col[:], a["bv"]), (bo_row[:], a["bo"])):
                sp.dma_start(dst, src).then_inc(ld_att, 16)
            for dst, src in ((w_i_r, rows(a["w_i_t"])), (lora_a, a["lora_a"]), (lora_b, a["lora_b"]),
                             (pick_cols[:], a["pick_cols"]), (expert_of[:], a["expert_of"]),
                             (top_i[:], a["top_i"]), (top_v[:], a["top_v"]), (w_out[:], rows(a["w_out_t"]))):
                sp.dma_start(dst, src).then_inc(ld_ffn, 16)
            for g in range(-1, NCH):
                if g + 2 < NCH:
                    sp.wait_ge(xs_t, g + 2)
                    load_x(g + 2, x_pre, ld_x)
                if g < 0:
                    continue
                if g + 1 < NCH:
                    sp.wait_ge(ln_r, 4 * g + 1)
                    load_x(g + 1, x_res, ld_r)
                b, c = divmod(g, CPB)
                sp.wait_ge(ln_x, 4 * TT * g + 4 * TT)
                sp.dma_start(a["out"][b, c * T:(c + 1) * T, :].rearrange("(t p) d -> p t d", p=P),
                             x24).then_inc(stored, 16)
            sp.wait_ge(stored, 16 * NCH)

        @block.gpsimd
        def _(pool):
            pool.memset(ident[:], 0.0).then_inc(consts, 1)
            pool.memset(ones[:], 1.0).then_inc(consts, 1)
            pool.wait_ge(consts, 2)
            pool.affine_select(out=ident[:], in_=ident[:], compare_op=ALU.not_equal, fill=1.0, base=0,
                               pattern=[[-1, P]], channel_multiplier=1).then_inc(consts, 1)
            pool.memset(ident_bf[:], 0.0).then_inc(consts, 1)
            pool.memset(mask_bf[:], 0.0).then_inc(consts, 1)
            pool.memset(mask_t_bf[:], 0.0).then_inc(consts, 1)
            pool.memset(mhalf[:], -0.5).then_inc(consts, 1)
            pool.memset(gate[:], 1.0).then_inc(consts, 1)
            pool.memset(hw[:], 1.0).then_inc(consts, 1)
            pool.wait_ge(consts, 9)
            pool.affine_select(out=ident_bf[:], in_=ident_bf[:], compare_op=ALU.not_equal, fill=1.0, base=0,
                               pattern=[[-1, P]], channel_multiplier=1).then_inc(consts, 1)
            pool.affine_select(out=mask_bf[:], in_=mask_bf[:], compare_op=ALU.is_ge, fill=NEG, base=0,
                               pattern=[[-1, P]], channel_multiplier=1).then_inc(consts, 1)
            pool.affine_select(out=mask_t_bf[:], in_=mask_t_bf[:], compare_op=ALU.is_ge, fill=NEG, base=0,
                               pattern=[[1, P]], channel_multiplier=-1).then_inc(consts, 1)

            def product(g, n):
                k = row(g, n)
                pool.wait_ge(scan_ok, 2 * k + 2)
                pool.wait_ge(cr_ok, k + 1)
                if k >= 2:
                    pool.wait_ge(acc_ok, acc_at(k - 2))
                pool.tensor_tensor(prod[:, k % 2, :, :], hst[:, k % 3, :, :],
                                   c_rep[:, k % 2, :].unsqueeze(1).to_broadcast([P, KD, T]),
                                   ALU.mult).then_inc(pr_ok, 1)

            def norm_power(q):
                pool.wait_ge(ln_ve, q + 1)
                pool.tensor_tensor(rstd[:], veps[:], mhalf[:], ALU.pow).then_inc(ln_rstd, 1)

            for s in range(NCH + 1):
                g, r = s, s - 1
                for n in range(N):
                    if g < NCH:
                        product(g, n)
                    if s == 0 and n == 4:
                        pool.wait_ge(wp_act, 9)
                        pool.wait_ge(wp_dve, 8)
                        pool.wait_ge(wp_pe, 8)
                        pool.memset(vc[:, :, D:D + 1], 1.0).then_inc(pc_ready, 1)
                    if s > 0:
                        if n == SL_Y:
                            norm_power(4 * r)
                        if n == SL_UP:
                            norm_power(4 * r + 1)
                        if n == SL_QV:
                            pool.wait_ge(xt_ps, 3 * r + 2)
                            pool.wait_ge(wp_act, 6)
                            pool.tensor_tensor(x2b, x24,
                                               att_bias[:].unsqueeze(1).to_broadcast([P, TT, D]),
                                               ALU.add).then_inc(x2b_ok, 1)
                        if n == SL_P1:
                            norm_power(4 * r + 2)
                if s > 0:
                    norm_power(4 * r + 3)

        @block.scalar
        def _(act):
            def copy(out, in_):
                return nc.scalar.activation(out, in_, ACT.Copy)

            act.wait_ge(ld_pre, 9 * 16)
            nc.scalar.activation(a_neg[:], a_neg[:], ACT.Exp).then_inc(wa, 1)
            copy(w_in_h[:], w_in_r).then_inc(wp_act, 1)
            act.wait_ge(wp_pe, 1)
            copy(dt_bc_r[:, :, 0:D], gb[:, 0, :].rearrange("p (k n) -> p k n", k=KD)).then_inc(wp_act, 1)
            act.wait_ge(wp_pe, 2)
            copy(w_pre_h[:], gb[:, 1:3, 0:D + P]).then_inc(wp_act, 1)
            act.wait_ge(wd, 2)
            copy(a_h[:], a_rep[:]).then_inc(wp_act, 1)

            def pre_x(g):
                act.wait_ge(xs_t, g + 1)
                if g >= 1:
                    act.wait_ge(g_ps, g)
                copy(xs_h[:].rearrange("p k t -> p (k t)"),
                     gb[:, 2:4, :].rearrange("p k t -> p (k t)")).then_inc(xs_hi, 1)

            def pre_u(g):
                act.wait_ge(u_ps, g + 1)
                if g >= 1:
                    act.wait_ge(dtu_ok, g)
                    act.wait_ge(acc_ok, acc_at(row(g - 1, 0)))
                copy(u_sb[:, 0, :], gb[:, 4, :]).then_inc(u_cp, 1)
                copy(u_sb[:, 1, :], gb[:, 0, :]).then_inc(u_cp, 1)
                if g >= 1:
                    act.wait_ge(dtu_lo, g)
                    act.wait_ge(inp_lo, g)
                    act.wait_ge(c_lo, g)
                act.wait_ge(z_ps, g + 1)
                for j in range(KD):
                    nc.scalar.activation(sp_a[:, j, :], gb[:, 1 + j, :], ACT.Abs,
                                         bias=b_dt[:, j:j + 1]).then_inc(sp_abs, 1)
                act.wait_ge(bc_ps, g + 1)
                copy(bc_sb[:], gb[:, 3, :]).then_inc(bc_cp, 1)
                act.wait_ge(bc_cp, g + 1)
                if g >= 2:
                    act.wait_ge(ir_ok, row(g - 1, 0))
                    act.wait_ge(cr_ps, row(g - 1, 0))
                copy(parts[64:128, g % 2, :], bc_sb[64:128, :]).then_inc(c_hi, 1)

            def pre_softplus(g):
                act.wait_ge(sp_abs, 2 * g + 2)
                nc.scalar.activation(sp_a[:], sp_a[:], ACT.Exp, scale=-1.0).then_inc(sp_exp, 1)
                act.wait_ge(sp_exp, g + 1)
                nc.scalar.activation(sp_a[:], sp_a[:], ACT.Ln, bias=ones[:, 0:1]).then_inc(sp_ln, 1)

            def pre_dtu(g):
                act.wait_ge(dtu_ok, g + 1)
                act.wait_ge(bc_ps, g + 1)
                copy(dtu_h[:], dtu[:]).then_inc(dtu_hi, 1)

            def decay(g, n):
                k = row(g, n)
                act.wait_ge(dt_ok, g + 1)
                if k >= 3:
                    act.wait_ge(scan_ok, 2 * (k - 3) + 2)
                for j in range(KD):
                    nc.scalar.activation(bar[:, k % 3, j, :], dt_sb[:, g % 2, j, :], ACT.Exp,
                                         scale=a_neg[:, j, n:n + 1]).then_inc(bar_ok, 1)

            def c_copy(g, n):
                k = row(g, n)
                act.wait_ge(cr_ps, k + 1)
                if k >= 2:
                    act.wait_ge(pr_ok, k - 1)
                copy(c_rep[:, k % 2, :], bc[:]).then_inc(cr_ok, 1)

            def normalize(q, out):
                act.wait_ge(ln_nb, q + 1)
                if q % 4 == 1 and q > 4:
                    act.wait_ge(stored, 16 * (q // 4))
                for t in range(TT):
                    nc.scalar.activation(out[:, t, :], res[:, t, :], ACT.Identity, scale=rstd[:, t:t + 1],
                                         bias=nbias[:, t:t + 1]).then_inc(ln_x, 1)

            def xt_high(i, b0):
                act.wait_ge(xt_ps, i + 1)
                copy(xt_h[:].rearrange("p k t -> p (k t)"),
                     gb[:, b0:b0 + 2, :].rearrange("p k t -> p (k t)")).then_inc(xt_hi, 1)

            def keys(g):
                b, c = divmod(g, CPB)
                act.wait_ge(sh_ps, g + 1)
                nc.scalar.activation(q_st[0:96, :], gb[0:96, 0, :], ACT.Identity,
                                     bias=b_sh[0:96, :]).then_inc(q_hi, 1)
                nc.scalar.activation(k_st[0:96, c * T:(c + 1) * T], gb[0:96, 0, :], ACT.Identity,
                                     bias=b_sh[0:96, :]).then_inc(k_hi, 1)
                act.wait_ge(v_ps, g + 1)
                act.wait_ge(pc_ready, 1)
                for h in range(2):
                    copy(vc[:, 4 * c + 2 * h:4 * c + 2 * h + 2, 0:D],
                         gb[:, 3 + h, :].rearrange("p (t d) -> p t d", t=2)).then_inc(v_ok, 1)

            def max_rows(g):
                act.wait_ge(mt_ps, g + 1)
                copy(q_st[96:98, :], gb[0:2, 3, :]).then_inc(mt_ok, 1)

            def exps(g, h):
                for i in range(n_p[g][h]):
                    k = p_base[g][h] + i
                    act.wait_ge(st_ps, k + 1)
                    if k >= 3:
                        act.wait_ge(pv_ok, k - 2)
                    nc.scalar.activation(ring[:, k % 3, :],
                                         gb[:, 1 + k % 2, :], ACT.Exp, scale=SCALE).then_inc(p_ok, 1)

            def relus(g, m):
                k = g * FB + m
                bank = gb[:, (0, 4, 3)[m % 3], :]
                if m >= 2:
                    act.wait_ge(mid_ok, k - 1)
                if m == 0:
                    act.wait_ge(pv_ok, p_base[g][1] + n_p[g][1])
                act.wait_ge(z0_ps, k + 1)
                nc.scalar.activation(ring[:, 2 * k % 3, :], bank, ACT.Relu, scale=absv[:, 0:1]).then_inc(a0_ok, 1)
                act.wait_ge(zd_ps, k + 1)
                if m >= 1:
                    act.wait_ge(mid_ok, k)
                nc.scalar.activation(ring[:, (2 * k + 1) % 3, :], bank, ACT.Relu, scale=absv[:, 1:2]).then_inc(a1_ok, 1)

            pre_x(0)
            pre_u(0)
            pre_softplus(0)
            pre_dtu(0)
            act.wait_ge(ld_cat, 4 * 16)
            copy(w_cat_h[:], w_cat_r).then_inc(wa, 1)
            copy(w_up_h[:], w_up_r).then_inc(wp_act, 1)
            decay(0, 0)
            c_copy(0, 0)
            act.wait_ge(wp_pe, 4)
            copy(att_bias[:], gb[:, 4, 0:D]).then_inc(wp_act, 1)
            copy(w_vo_h[:], gb[:, 1, :].rearrange("p (k n) -> p k n", k=KD)).then_inc(wa, 1)
            act.wait_ge(ld_att, 6 * 16)
            copy(w_sh_h[:], w_sh_r).then_inc(wa, 1)
            act.wait_ge(wp_pe, 5)
            act.wait_ge(ld_ffn, 8 * 16)
            copy(w_i_h[:], w_i_r).then_inc(wa, 1)
            copy(w_la_h[:], gb[:, 2, 0:2 * P].rearrange("p (k n) -> p k n", k=KD)).then_inc(wp_act, 1)
            act.wait_ge(wp_pe, 6)
            copy(w_z0[:].rearrange("p n -> p n"),
                 gb[0:RANKL, 0:2, :].rearrange("p k t -> p (k t)")).then_inc(wp_act, 1)
            act.wait_ge(wp_pe, 7)
            copy(w_zd[:].rearrange("p n -> p n"),
                 gb[0:RANKL, 3:5, :].rearrange("p k t -> p (k t)")).then_inc(wp_act, 1)

            for s in range(NCH + 1):
                g, r, p = s, s - 1, s + 1
                for n in range(N):
                    if g < NCH:
                        if n + 1 < N:
                            decay(g, n + 1)
                            c_copy(g, n + 1)
                        elif g + 1 < NCH:
                            decay(g + 1, 0)
                            c_copy(g + 1, 0)
                    if s > 0:
                        if n == SL_N1:
                            normalize(4 * r, x13)
                    if p < NCH:
                        if n == PR_MM:
                            pre_x(p)
                        if n == PR_SP:
                            pre_u(p)
                            pre_softplus(p)
                        if n == PR_G:
                            pre_dtu(p)
                    if s > 0:
                        if n == SL_X1 + 1:
                            xt_high(3 * r, 0)
                        if n == SL_RT:
                            act.wait_ge(lg_ok, r + 1)
                            nc.scalar.activation(ex[:], ls[:], ACT.Exp).then_inc(ex_ok, 1)
                        if n == SL_UP:
                            act.wait_ge(hwt_ps, r + 1)
                            copy(hw_h, gb[0:HR + 1, 4, :]).then_inc(hw_hi, 1)
                        if n == SL_N2:
                            normalize(4 * r + 1, x24)
                            xt_high(3 * r + 1, 1)
                        if n == SL_QV:
                            keys(r)
                        if n == SL_S:
                            max_rows(r)
                        if n == SL_P0:
                            exps(r, 0)
                        if n == SL_P1:
                            exps(r, 1)
                        if n == SL_N3:
                            normalize(4 * r + 2, x13)
                            xt_high(3 * r + 2, 1)
                        if n == SL_L:
                            act.wait_ge(l_ps, r + 1)
                            copy(lr[:], gb[0:RANKL, 3, :]).then_inc(l_hi, 1)
                        for m in range(FB):
                            if n == SL_F[m]:
                                relus(r, m)
                if s > 0:
                    normalize(4 * r + 3, x24)

        @block.tensor
        def _(pe):
            def mm3(out, lh, ll, rh, rl_, start, stop, skip=False):
                nc.tensor.matmul(out, lh, rh, start=start, stop=False, skip_group_check=skip)
                nc.tensor.matmul(out, ll, rh, start=False, stop=False, skip_group_check=skip)
                return nc.tensor.matmul(out, lh, rl_, start=False, stop=stop, skip_group_check=skip)

            pe.wait_ge(ld_pre, 9 * 16)
            for k in range(KD):
                mm = nc.tensor.matmul(gb[:, 0, k * D:(k + 1) * D], w_xdt_t[:, k * P:(k + 1) * P], w_dt,
                                      start=(k == 0), stop=True, skip_group_check=True)
            mm.then_inc(wp_pe, 1)
            pe.wait_ge(wp_act, 2)
            for m in range(KD):
                for k in range(KD):
                    mm = nc.tensor.matmul(gb[:, 1 + m, 0:D + P], w_in_t[:, k, m * P:(m + 1) * P],
                                          dt_bc_r[:, k, :], start=(k == 0), stop=(k == KD - 1))
            mm.then_inc(wp_pe, 1)

            def pre_transpose(g):
                pe.wait_ge(ld_x, 16 * (g + 1))
                if g >= 3:
                    pe.wait_ge(a1_ok, (g - 2) * FB)
                    pe.wait_ge(ln_r, 4 * (g - 2))
                for k in range(KD):
                    for t in range(TT):
                        mm = nc.tensor.transpose(gb[:, 2 + k, t * P:(t + 1) * P],
                                                 x_pre[:, t, k * P:(k + 1) * P], ident[:])
                mm.then_inc(xs_t, 1)

            def pre_products(g):
                pe.wait_ge(xs_hi, g + 1)
                pe.wait_ge(xs_lo, g + 1)
                if g >= 2:
                    pe.wait_ge(ln_r, 4 * (g - 2) + 1)
                for j in range(KD):
                    for k in range(KD):
                        mm = mm3(gb[:, (4, 0)[j], :], w_in_h[:, k, j * P:(j + 1) * P],
                                 w_in_l[:, k, j * P:(j + 1) * P], xs_h[:, k, :], xs_l[:, k, :],
                                 k == 0, k == KD - 1)
                mm.then_inc(u_ps, 1)
                for j in range(KD):
                    for k in range(KD):
                        mm = mm3(gb[:, 1 + j, :], w_pre_h[:, k, j * P:(j + 1) * P],
                                 w_pre_l[:, k, j * P:(j + 1) * P], xs_h[:, k, :], xs_l[:, k, :],
                                 k == 0, k == KD - 1)
                mm.then_inc(z_ps, 1)
                for k in range(KD):
                    mm = mm3(gb[:, 3, :], w_pre_h[:, k, D:D + P], w_pre_l[:, k, D:D + P],
                             xs_h[:, k, :], xs_l[:, k, :], k == 0, k == KD - 1)
                mm.then_inc(bc_ps, 1)

            def pre_input(g):
                pe.wait_ge(dtu_hi, g + 1)
                pe.wait_ge(dtu_lo, g + 1)
                pe.wait_ge(u_cp, 2 * g + 2)
                for k in range(KD):
                    mm = mm3(gb[:, 4, :], a_h[:, k, :], a_l[:, k, :], dtu_h[:, k, :], dtu_l[:, k, :],
                             k == 0, k == KD - 1)
                mm.then_inc(g_ps, 1)

            def spread(g, n):
                k = row(g, n)
                if n == 0:
                    pe.wait_ge(inp_lo, g + 1)
                    pe.wait_ge(c_lo, g + 1)
                if k >= 2:
                    pe.wait_ge(scan_ok, 2 * (k - 2) + 2)
                nc.tensor.matmul(bi[:, k % 2, :], sel[:, n:n + 1].to_broadcast([P, P]), parts[:, g % 2, :],
                                 start=True, stop=True).then_inc(ir_ok, 1)
                if k >= 1:
                    pe.wait_ge(cr_ok, k)
                nc.tensor.matmul(bc[:], sel[:, N + n:N + n + 1].to_broadcast([P, P]), parts[:, g % 2, :],
                                 start=True, stop=True).then_inc(cr_ps, 1)

            def xt_transpose(i, src, b0):
                pe.wait_ge(ln_x, TT * (4 * (i // 3) + i % 3 + 1))
                for k in range(KD):
                    for t in range(TT):
                        mm = nc.tensor.transpose(gb[:, b0 + k, t * P:(t + 1) * P],
                                                 src[:, t, k * P:(k + 1) * P], ident[:])
                mm.then_inc(xt_ps, 1)

            def y_transpose(g):
                pe.wait_ge(acc_ok, acc_at(row(g, N - 1)))
                if g >= 1:
                    pe.wait_ge(a1_ok, g * FB)
                    pe.wait_ge(ln_r, 4 * g)
                for t in range(TT):
                    for k in range(KD):
                        mm = nc.tensor.transpose(gb[:, t // 2, (t % 2) * D + k * P:(t % 2) * D + (k + 1) * P],
                                                 acc[:, k, t * P:(t + 1) * P], ident[:])
                mm.then_inc(y_t, 1)

            def cat(g):
                pe.wait_ge(xt_hi, 3 * g + 1)
                pe.wait_ge(xt_lo, 3 * g + 1)
                for t in range(TT):
                    for k in range(KD):
                        mm = mm3(gb[:, t, 0:CAT], xt_h[:, k, t * P:(t + 1) * P], xt_l[:, k, t * P:(t + 1) * P],
                                 w_cat_h[:, k, :], w_cat_l[:, k, :], k == 0, k == KD - 1)
                mm.then_inc(cat_ps, 1)

            def up(g):
                pe.wait_ge(hw_ok, g + 1)
                for t in range(TT):
                    mm = nc.tensor.transpose(gb[0:HR + 1, 4, t * P:(t + 1) * P], hw[:, t, :], ident[:])
                mm.then_inc(hwt_ps, 1)
                pe.wait_ge(hw_hi, g + 1)
                pe.wait_ge(hw_lo, g + 1)
                for t in range(TT):
                    ts = slice(t * P, (t + 1) * P)
                    mm = mm3(gb[:, t, 0:D], hw_h[:, ts], hw_l[:, ts], w_up_h[:], w_up_l[:], False, True, True)
                mm.then_inc(up_ps, 1)

            def share_values(g):
                pe.wait_ge(xt_hi, 3 * g + 2)
                pe.wait_ge(xt_lo, 3 * g + 2)
                for k in range(KD):
                    mm = mm3(gb[:, 0, :], w_sh_h[:, k, :], w_sh_l[:, k, :], xt_h[:, k, :], xt_l[:, k, :],
                             k == 0, k == KD - 1)
                mm.then_inc(sh_ps, 1)
                for t in range(TT):
                    for k in range(KD):
                        ts = slice(t * P, (t + 1) * P)
                        mm = mm3(gb[:, 3 + t // 2, (t % 2) * D:(t % 2 + 1) * D], xt_h[:, k, ts], xt_l[:, k, ts],
                                 w_vo_h[:, k, :], w_vo_l[:, k, :], k == 0 and t % 2 == 0, k == KD - 1, True)
                mm.then_inc(v_ps, 1)

            def scores(g):
                c = g % CPB
                pe.wait_ge(q_lo, g + 1)
                pe.wait_ge(k_lo, g + 1)
                for i in range(TT):
                    for kk in range(c + 1):
                        k = s_base[g] + i * (c + 1) + kk
                        j = i * (c + 1) + kk
                        w = T if kk < c else (i + 1) * P
                        if j >= 3:
                            pe.wait_ge(s_mx, k - 2)
                        out = gb[:, (1, 2, 0)[j % 3], 0:w]
                        diag = kk == c
                        mm = nc.tensor.matmul(out, q_st[0:96, i * P:(i + 1) * P], k_st[0:96, kk * T:kk * T + w],
                                              start=True, stop=True)
                        if diag:
                            mm = nc.tensor.matmul(gb[:, (1, 2, 0)[j % 3], w - P:w], ident_bf[:], mask_bf[:],
                                                  start=False, stop=True, skip_group_check=True)
                        mm.then_inc(s_ps, 1)
                pe.wait_ge(mhl_ok, 2 * g + 2)
                pe.wait_ge(v_ok, 2 * g + 2)
                for i in range(TT):
                    mm = nc.tensor.transpose(gb[0:2, 3, i * P:(i + 1) * P], mhl[:, i, :].bitcast(F32), ident[:])
                mm.then_inc(mt_ps, 1)

            def attend(g, h):
                c = g % CPB
                if h == 0:
                    pe.wait_ge(mt_ok, g + 1)
                banks = ((0, 3), (4, 0))[h]

                def scores_t(i):
                    k = p_base[g][h] + i
                    if k >= 2:
                        pe.wait_ge(p_ok, k - 1)
                    last = i == n_p[g][h] - 1
                    for e in range(2):
                        kt = 2 * i + e
                        mm = nc.tensor.matmul(gb[:, 1 + k % 2, e * D:(e + 1) * D], k_st[:, kt * P:(kt + 1) * P],
                                              q_st[:, 2 * h * P:(2 * h + 2) * P], start=(e == 0),
                                              stop=True, skip_group_check=True)
                        if last:
                            mm = nc.tensor.matmul(gb[:, 1 + k % 2, e * D + e * P:e * D + (e + 1) * P],
                                                  ident_bf[:], mask_t_bf[:], start=False, stop=True,
                                                  skip_group_check=True)
                    mm.then_inc(st_ps, 1)

                def values(i):
                    k = p_base[g][h] + i
                    pe.wait_ge(p_ok, k + 1)
                    last = i == n_p[g][h] - 1
                    for e in range(2):
                        kt = 2 * i + e
                        for ql in range(2):
                            if last and e == 1 and ql == 0:
                                continue
                            if h == 1 and ql == 1 and kt == 0:
                                pe.wait_ge(o_res, TT * g + 1)
                            end = last and (e == 1 or ql == 0)
                            mm = nc.tensor.matmul(gb[:, banks[ql], 0:D + 1],
                                                  ring[:, k % 3, e * D + ql * P:e * D + (ql + 1) * P], vc[:, kt, :],
                                                  start=(kt == 0), stop=end)
                    mm.then_inc(pv_ok, 1)

                scores_t(0)
                for i in range(n_p[g][h]):
                    if i + 1 < n_p[g][h]:
                        scores_t(i + 1)
                    values(i)

            def low_rank(g):
                pe.wait_ge(xt_hi, 3 * g + 3)
                pe.wait_ge(xt_lo, 3 * g + 3)
                for k in range(KD):
                    mm = mm3(gb[:, 3, :], w_la_h[:, k, :], w_la_l[:, k, :], xt_h[:, k, :], xt_l[:, k, :],
                             k == 0, k == KD - 1)
                mm.then_inc(l_ps, 1)

            def inner(g, m):
                k = g * FB + m
                bank = gb[:, (0, 4, 3)[m % 3], :]
                ms = slice(m * P, (m + 1) * P)
                if m >= 3:
                    pe.wait_ge(a1_ok, k - 2)
                if m == 2:
                    pe.wait_ge(l_lo, g + 1)
                    pe.wait_ge(l_hi, g + 1)
                for kk in range(KD):
                    mm3(bank, w_i_h[:, kk, ms], w_i_l[:, kk, ms], xt_h[:, kk, :], xt_l[:, kk, :], kk == 0, False)
                pe.wait_ge(l_hi, g + 1)
                pe.wait_ge(l_lo, g + 1)
                nc.tensor.matmul(bank, w_z0[:, ms], lr[:], start=False, stop=True).then_inc(z0_ps, 1)

            def inner_other(g, m):
                k = g * FB + m
                pe.wait_ge(a0_ok, k + 1)
                nc.tensor.matmul(gb[:, (0, 4, 3)[m % 3], :], w_zd[:, m * P:(m + 1) * P], lr[:],
                                 start=False, stop=True, skip_group_check=True).then_inc(zd_ps, 1)

            def outer(g, m):
                k = g * FB + m
                pe.wait_ge(mid_ok, k + 1)
                for t in range(TT):
                    mm = nc.tensor.matmul(gb[:, 1 + t // 2, (t % 2) * D:(t % 2 + 1) * D],
                                          mid[:, k % 2, t * P:(t + 1) * P], w_out[:, m, :],
                                          start=(m == 0 and t % 2 == 0), stop=(m == FB - 1),
                                          skip_group_check=True)
                mm.then_inc(mid_used, 1)

            pe.wait_ge(consts, 3)
            pe.wait_ge(wp_dve, 1)
            pe.wait_ge(wp_act, 3)
            pre_transpose(0)
            pre_products(0)
            pe.wait_ge(ld_att, 6 * 16)
            pe.wait_ge(ld_ffn, 8 * 16)
            pe.wait_ge(wp_dve, 3)
            pre_input(0)
            pe.wait_ge(inp_ok, 1)
            spread(0, 0)
            pe.wait_ge(sp_max, 2)
            pe.wait_ge(sp_abs, 2)
            for k in range(KD):
                nc.tensor.matmul(gb[:, 4, 0:D], bv_rep[:, k, :], w_o[:, k, :], start=(k == 0), stop=False)
            nc.tensor.matmul(gb[:, 4, 0:D], ones[0:1, :], bo_row[:], start=False, stop=True).then_inc(wp_pe, 1)
            for m in range(KD):
                for k in range(KD):
                    mm = nc.tensor.matmul(gb[:, 1, m * D:(m + 1) * D], w_v_t[:, k, m * P:(m + 1) * P],
                                          w_o[:, k, :], start=(k == 0 and m == 0), stop=(k == KD - 1),
                                          skip_group_check=True)
            mm.then_inc(wp_pe, 1)
            for m in range(KD):
                mm = nc.tensor.matmul(gb[:, 2, m * P:m * P + P], lora_a[:, m * P:(m + 1) * P], sel_a128[:],
                                      start=(m == 0), stop=True, skip_group_check=True)
            mm.then_inc(wp_pe, 1)
            pe.wait_ge(wa, 3)
            pe.wait_ge(wp_dve, 5)
            for h in range(2):
                mm = nc.tensor.matmul(gb[0:RANKL, h, :], sel_0[:], lora_b[:, h * T:(h + 1) * T],
                                      start=True, stop=True)
            mm.then_inc(wp_pe, 1)
            pe.wait_ge(wp_act, 6)
            pe.wait_ge(bc_cp, 1)
            for h in range(2):
                mm = nc.tensor.matmul(gb[0:RANKL, 3 + h, :], sel_d[:], lora_b[:, h * T:(h + 1) * T],
                                      start=True, stop=True)
            mm.then_inc(wp_pe, 2)

            for s in range(NCH + 1):
                g, r, p = s, s - 1, s + 1
                for n in range(N):
                    if g < NCH:
                        if n + 1 < N:
                            spread(g, n + 1)
                        elif g + 1 < NCH:
                            spread(g + 1, 0)
                    if s > 0 and n == SL_Y:
                        y_transpose(r)
                    if p < NCH:
                        if n == PR_T:
                            if s == 0:
                                pe.wait_ge(wp_act, 9)
                                pe.wait_ge(wp_dve, 8)
                            pre_transpose(p)
                        if n == PR_MM:
                            pre_products(p)
                        if n == PR_G:
                            pre_input(p)
                    if s > 0:
                        if n == SL_X1:
                            if p < NCH:
                                pe.wait_ge(u_cp, 2 * p + 2)
                                pe.wait_ge(sp_abs, 2 * p + 2)
                                pe.wait_ge(sp_max, 2 * p + 2)
                            xt_transpose(3 * r, x13, 0)
                        if n == SL_CAT:
                            if p < NCH:
                                pe.wait_ge(bc_cp, p + 1)
                            cat(r)
                        if n == SL_UP:
                            if p < NCH:
                                pe.wait_ge(inp_ok, p + 1)
                            up(r)
                        if n == SL_X2:
                            xt_transpose(3 * r + 1, x24, 1)
                        if n == SL_QV:
                            share_values(r)
                        if n == SL_S:
                            scores(r)
                        if n == SL_P0:
                            attend(r, 0)
                        if n == SL_P1:
                            attend(r, 1)
                        if n == SL_X3:
                            xt_transpose(3 * r + 2, x13, 1)
                        if n == SL_L:
                            low_rank(r)
                            inner(r, 0)
                        for m in range(FB):
                            if n == SL_F[m]:
                                inner_other(r, m)
                                if m + 1 < FB:
                                    inner(r, m + 1)
                                outer(r, m)

        @block.vector
        def _(dve):
            V = nc.vector

            def small(ins, s_, v):
                ins.then_inc(s_, 1)
                dve.wait_ge(s_, v)

            dve.wait_ge(consts, 3)
            dve.wait_ge(ld_pre, 9 * 16)
            small(V.memset(a_rep[:], 0.0), wd, 1)
            dve.wait_ge(wa, 1)
            for c0 in (0, 32):
                V.tensor_scalar(a_rep[:, :, c0:c0 + N], a_neg[:], -1.0, None, ALU.mult)
            V.tensor_scalar(a_neg[:], a_neg[:], -1.0, None, ALU.mult).then_inc(wd, 1)
            V.tensor_copy(sel[:], sel_cols[:]).then_inc(wd, 1)
            dve.wait_ge(wp_act, 1)
            V.tensor_tensor(w_in_l[:], w_in_r, w_in_h[:].bitcast(F32), ALU.subtract)
            dve.wait_ge(wp_act, 3)
            V.tensor_tensor(w_pre_l[:], gb[:, 1:3, 0:D + P], w_pre_h[:].bitcast(F32),
                            ALU.subtract).then_inc(wp_dve, 1)

            def pre_x(g):
                dve.wait_ge(xs_hi, g + 1)
                V.tensor_tensor(xs_l[:].rearrange("p k t -> p (k t)"),
                                gb[:, 2:4, :].rearrange("p k t -> p (k t)"),
                                xs_h[:].bitcast(F32).rearrange("p k t -> p (k t)"),
                                ALU.subtract).then_inc(xs_lo, 1)

            def pre_max(g):
                dve.wait_ge(z_ps, g + 1)
                dve.wait_ge(sp_abs, 2 * g + 2)
                for j in range(KD):
                    V.tensor_scalar(sp_m[:, j, :], gb[:, 1 + j, :], b_dt[:, j:j + 1], 0.0,
                                    ALU.add, ALU.max).then_inc(sp_max, 1)

            def pre_dt(g):
                dve.wait_ge(sp_ln, g + 1)
                dve.wait_ge(sp_max, 2 * g + 2)
                V.tensor_tensor(sp_m[:], sp_m[:], sp_a[:], ALU.add).then_inc(sp_sum, 1)
                dve.wait_ge(sp_sum, g + 1)
                if g >= 2:
                    dve.wait_ge(bar_ok, 2 * row(g - 1, 0))
                V.tensor_scalar(dt_sb[:, g % 2, :, :], sp_m[:], DT_MAX - DT_MIN, DT_MIN,
                                ALU.mult, ALU.add).then_inc(dt_ok, 1)
                dve.wait_ge(dt_ok, g + 1)
                dve.wait_ge(u_cp, 2 * g + 2)
                V.tensor_tensor(dtu[:], dt_sb[:, g % 2, :, :], u_sb[:],
                                ALU.mult).then_inc(dtu_ok, 1)

            def pre_low(g):
                dve.wait_ge(dtu_hi, g + 1)
                V.tensor_tensor(dtu_l[:], dtu[:], dtu_h[:].bitcast(F32), ALU.subtract).then_inc(dtu_lo, 1)
                dve.wait_ge(c_hi, g + 1)
                V.tensor_tensor(parts[96:128, g % 2, :], bc_sb[96:128, :],
                                parts[96:128, g % 2, :].bitcast(F32), ALU.subtract).then_inc(c_lo, 1)

            def pre_input(g):
                dve.wait_ge(g_ps, g + 1)
                dve.wait_ge(bc_cp, g + 1)
                V.tensor_tensor(bc_sb[0:64, :], gb[0:64, 4, :], bc_sb[0:64, :], ALU.mult).then_inc(inp_ok, 1)
                dve.wait_ge(inp_ok, g + 1)
                V.tensor_copy(parts[0:64, g % 2, :], bc_sb[0:64, :]).then_inc(inp_hi, 1)
                dve.wait_ge(inp_hi, g + 1)
                V.tensor_tensor(parts[32:64, g % 2, :], bc_sb[32:64, :],
                                parts[32:64, g % 2, :].bitcast(F32), ALU.subtract).then_inc(inp_lo, 1)

            def scan(g, n):
                k = row(g, n)
                dve.wait_ge(ir_ok, k + 1)
                if k >= 3:
                    dve.wait_ge(pr_ok, k - 2)
                if g % CPB:
                    dve.wait_ge(st_ok, (g - 1 - (g - 1) // CPB) * N + n + 1)
                for j in range(KD):
                    dve.wait_ge(bar_ok, 2 * k + j + 1)
                    V.tensor_tensor_scan(hst[:, k % 3, j, :], bar[:, k % 3, j, :], bi[:, k % 2, :],
                                         state[:, j, n:n + 1] if g % CPB else 0.0,
                                         ALU.mult, ALU.add).then_inc(scan_ok, 1)

            def keep_state(g, n):
                k = row(g, n)
                dve.wait_ge(scan_ok, 2 * k + 2)
                V.tensor_copy(state[:, :, n:n + 1], hst[:, k % 3, :, T - 1:T]).then_inc(st_ok, 1)

            def accumulate(g, n):
                k = row(g, n)
                dve.wait_ge(pr_ok, k + 1)
                if n == 0:
                    if g >= 1:
                        dve.wait_ge(y_t, g)
                    for j in range(KD):
                        V.scalar_tensor_tensor(out=acc[:, j, :], in0=u_sb[:, j, :],
                                               scalar=d_skip[:, j:j + 1], in1=prod[:, k % 2, j, :],
                                               op0=ALU.mult, op1=ALU.add).then_inc(acc_ok, 1)
                else:
                    dve.wait_ge(acc_ok, acc_at(k - 1))
                    V.tensor_tensor(acc[:], acc[:], prod[:, k % 2, :, :], ALU.add).then_inc(acc_ok, 1)

            def stats(q):
                dve.wait_ge(ln_r, q + 1)
                for t in range(TT):
                    V.bn_stats(bnst[:, t, :], res[:, t, :]).then_inc(ln_bn, 1)
                dve.wait_ge(ln_bn, TT * (q + 1))
                for t in range(TT):
                    V.bn_aggr(mv[:, t, :], bnst[:, t, :]).then_inc(ln_mv, 1)
                dve.wait_ge(ln_mv, TT * (q + 1))
                V.tensor_scalar(veps[:], mv[:, :, 1], EPS, None, ALU.add).then_inc(ln_ve, 1)

            def norm_bias(q):
                dve.wait_ge(ln_rstd, q + 1)
                V.scalar_tensor_tensor(out=nbias[:], in0=mv[:, :, 0], scalar=-1.0, in1=rstd[:],
                                       op0=ALU.mult, op1=ALU.mult).then_inc(ln_nb, 1)

            def xt_low(i, b0):
                dve.wait_ge(xt_hi, i + 1)
                V.tensor_tensor(xt_l[:].rearrange("p k t -> p (k t)"),
                                gb[:, b0:b0 + 2, :].rearrange("p k t -> p (k t)"),
                                xt_h[:].bitcast(F32).rearrange("p k t -> p (k t)"),
                                ALU.subtract).then_inc(xt_lo, 1)

            def residual(q, banks, scalar=None):
                g, l = divmod(q, 4)
                src = x_res[:] if l == 0 else x13
                if q:
                    dve.wait_ge(ln_x, TT * q)
                if l == 0:
                    dve.wait_ge(ld_r, 16 * (g + 1))
                if scalar is None:
                    V.tensor_tensor(res[:], banks, src, ALU.add).then_inc(ln_r, 1)
                else:
                    V.scalar_tensor_tensor(out=res[:].rearrange("p t d -> p (t d)"),
                                           in0=banks, scalar=scalar,
                                           in1=src.rearrange("p t d -> p (t d)"),
                                           op0=ALU.mult, op1=ALU.add).then_inc(ln_r, 1)

            def two_banks(b0):
                return gb[:, b0:b0 + 2, :].rearrange("p a (t d) -> p (a t) d", d=D)

            def router(g):
                v = 11 * g
                dve.wait_ge(cat_ps, g + 1)
                small(V.tensor_tensor(lg[:], gb[:, 0:TT, CAT - E:CAT], r_bias[:], ALU.add), rt, v + 1)
                small(V.tensor_reduce(lmax[:], lg[:], AX.X, ALU.max), rt, v + 2)
                V.tensor_tensor(ls[:], lg[:], lmax[:].unsqueeze(2).to_broadcast([P, TT, E]),
                                ALU.subtract).then_inc(lg_ok, 1)
                of_j = lg[:].unsqueeze(2).to_broadcast([P, TT, E, E])
                of_i = lg[:].unsqueeze(3).to_broadcast([P, TT, E, E])
                V.tensor_tensor(rk_gt[:], of_j, of_i, ALU.is_gt).then_inc(rt, 1)
                small(V.tensor_tensor(rk_eq[:], of_j, of_i, ALU.is_equal), rt, v + 4)
                small(V.tensor_tensor(rk_eq[:].rearrange("p t i j -> p t (i j)"),
                                      rk_eq[:].rearrange("p t i j -> p t (i j)"),
                                      tie[:].rearrange("p i j -> p (i j)").unsqueeze(1).to_broadcast([P, TT, E * E]),
                                      ALU.mult), rt, v + 5)
                small(V.tensor_tensor(rk_gt[:], rk_gt[:], rk_eq[:], ALU.add), rt, v + 6)
                small(V.tensor_reduce(rank[:], rk_gt[:], AX.X, ALU.add), rt, v + 7)
                dve.wait_ge(ex_ok, g + 1)
                small(V.scalar_tensor_tensor(out=em[:], in0=rank[:], scalar=1.5, in1=ex[:],
                                             op0=ALU.is_lt, op1=ALU.mult), rt, v + 8)
                V.tensor_reduce(e_sum[:], ex[:], AX.X, ALU.add)
                small(V.tensor_reduce(k_sum[:], em[:], AX.X, ALU.add), rt, v + 9)
                small(V.scalar_tensor_tensor(out=e_sum[:], in0=e_sum[:], scalar=1e-6, in1=k_sum[:],
                                             op0=ALU.mult, op1=ALU.add), rt, v + 10)
                small(V.reciprocal(k_sum[:], e_sum[:]), rt, v + 11)
                dve.wait_ge(consts, 12)
                V.tensor_tensor(gate[:, :, 0:E], em[:], k_sum[:].unsqueeze(2).to_broadcast([P, TT, E]),
                                ALU.mult).then_inc(lgate, 1)
                dve.wait_ge(lgate, g + 1)
                V.tensor_tensor(hw[:, :, 0:HR].rearrange("p t (e r) -> p t e r", r=R),
                                gb[:, 0:TT, D:D + HR].rearrange("p t (e r) -> p t e r", r=R),
                                gate[:].unsqueeze(3).to_broadcast([P, TT, EP, R]), ALU.mult).then_inc(hw_ok, 1)

            def keys(g):
                c = g % CPB
                dve.wait_ge(q_hi, g + 1)
                dve.wait_ge(k_hi, g + 1)
                V.scalar_tensor_tensor(out=q_st[64:96, :], in0=gb[64:96, 0, :], scalar=b_sh[64:96, :],
                                       in1=q_st[64:96, :].bitcast(F32), op0=ALU.add,
                                       op1=ALU.subtract).then_inc(q_lo, 1)
                ks = k_st[32:64, c * T:(c + 1) * T]
                V.scalar_tensor_tensor(out=ks, in0=gb[32:64, 0, :], scalar=b_sh[32:64, :],
                                       in1=ks.bitcast(F32), op0=ALU.add, op1=ALU.subtract).then_inc(k_lo, 1)

            def maxima(g):
                c = g % CPB
                for i in range(TT):
                    for kk in range(c + 1):
                        j = i * (c + 1) + kk
                        dve.wait_ge(s_ps, s_base[g] + j + 1)
                        w = T if kk < c else (i + 1) * P
                        V.tensor_reduce(smax[:, i, kk:kk + 1], gb[:, (1, 2, 0)[j % 3], 0:w], AX.X,
                                        ALU.max).then_inc(s_mx, 1)
                dve.wait_ge(s_mx, s_base[g] + n_s[g])
                small(V.tensor_reduce(m4[:], smax[:, :, 0:c + 1], AX.X, ALU.max), m_ok, g + 1)
                small(V.tensor_scalar(mhl[:, :, 0], m4[:], -1.0, None, ALU.mult), mhl_ok, 2 * g + 1)
                V.scalar_tensor_tensor(out=mhl[:, :, 1], in0=m4[:], scalar=-1.0, in1=mhl[:, :, 0].bitcast(F32),
                                       op0=ALU.mult, op1=ALU.subtract).then_inc(mhl_ok, 1)

            def finish_attention(g, h):
                banks = ((0, 3), (4, 0))[h]
                dve.wait_ge(pv_ok, p_base[g][h] + n_p[g][h])
                dve.wait_ge(x2b_ok, g + 1)
                for ql in range(2):
                    V.reciprocal(rl[:, 2 * h + ql:2 * h + ql + 1],
                                 gb[:, banks[ql], D:D + 1]).then_inc(rl_ok, 1)
                dve.wait_ge(rl_ok, TT * g + 2 * h + 2)
                if h == 0:
                    dve.wait_ge(ln_x, TT * (4 * g + 2))
                for ql in range(2):
                    i = 2 * h + ql
                    ins = V.scalar_tensor_tensor(out=res[:, i, :], in0=gb[:, banks[ql], 0:D],
                                                 scalar=rl[:, i:i + 1], in1=x2b[:, i, :],
                                                 op0=ALU.mult, op1=ALU.add)
                    ins.then_inc(o_res, 1)

            def mix(g, m):
                k = g * FB + m
                dve.wait_ge(a1_ok, k + 1)
                dve.wait_ge(a0_ok, k + 1)
                if k >= 2:
                    dve.wait_ge(mid_used, k - 1)
                V.scalar_tensor_tensor(out=mid[:, k % 2, :], in0=ring[:, 2 * k % 3, :], scalar=sgn01[:, 0:1],
                                       in1=ring[:, (2 * k + 1) % 3, :], op0=ALU.mult, op1=ALU.add).then_inc(mid_ok, 1)

            pre_x(0)
            dve.wait_ge(wd, 2)
            dve.wait_ge(wp_act, 4)
            V.tensor_tensor(a_l[:], a_rep[:], a_h[:].bitcast(F32), ALU.subtract).then_inc(wp_dve, 1)
            pre_max(0)
            pre_dt(0)
            pre_low(0)
            dve.wait_ge(ld_att, 6 * 16)
            dve.wait_ge(ld_ffn, 8 * 16)
            V.tensor_copy(bv_rep, bv_col[:].unsqueeze(2).to_broadcast([P, KD, P]))
            V.memset(sel_a128[:], 0.0)
            V.memset(sel_0[:], 0.0)
            V.tensor_scalar(sgn[:], top_v[:], 0.0, None, ALU.is_ge)
            small(V.tensor_copy(top_f[:], top_i[:]), wd, 4)
            V.tensor_scalar(sgn[:], sgn[:], 2.0, -1.0, ALU.mult, ALU.add)
            small(V.tensor_scalar(picked[:], top_f[:], expert_of[:, 0:1], None, ALU.is_equal), wd, 5)
            V.tensor_tensor(absv[:], top_v[:], sgn[:], ALU.mult)
            V.tensor_tensor(sgn01[:], sgn[:, 0:1], sgn[:, 1:2], ALU.mult)
            small(V.tensor_scalar(minus0[:], picked[:, 0:1], -1.0, None, ALU.mult), wd, 6)
            for q in range(3):
                c0 = 32 * q
                V.tensor_scalar(sel_a128[:, c0:c0 + R], pick_cols[:], picked[:, 0:1], None, ALU.mult)
                V.tensor_scalar(sel_a128[:, c0 + R:c0 + 2 * R], pick_cols[:], picked[:, 1:2], None, ALU.mult)
                V.tensor_scalar(sel_0[:, c0:c0 + R], pick_cols[:], picked[:, 0:1], None, ALU.mult)
                V.tensor_scalar(sel_d[:, c0:c0 + R], pick_cols[:], minus0[:, 0:1], None, ALU.mult)
                ins = V.tensor_scalar(sel_d[:, c0 + R:c0 + 2 * R], pick_cols[:], picked[:, 1:2], None, ALU.mult)
            ins.then_inc(wp_dve, 1)
            pre_input(0)
            V.memset(q_st[96:128, :].bitcast(F32), 0.0)
            V.memset(k_st[96:128, :].bitcast(F32), 0.0).then_inc(wd, 1)
            dve.wait_ge(wd, 7)
            V.memset(k_st[96:98, :].bitcast(F32), 1.0)
            dve.wait_ge(wa, 2)
            V.tensor_tensor(w_cat_l[:], w_cat_r, w_cat_h[:].bitcast(F32), ALU.subtract)
            dve.wait_ge(wp_act, 5)
            V.tensor_tensor(w_up_l[:], w_up_r, w_up_h[:].bitcast(F32), ALU.subtract).then_inc(wp_dve, 1)
            dve.wait_ge(wa, 3)
            V.tensor_tensor(w_vo_l[:], gb[:, 1, :].rearrange("p (k n) -> p k n", k=KD),
                            w_vo_h[:].bitcast(F32), ALU.subtract).then_inc(wp_dve, 1)
            dve.wait_ge(wa, 4)
            V.tensor_tensor(w_sh_l[:], w_sh_r, w_sh_h[:].bitcast(F32), ALU.subtract)
            dve.wait_ge(wa, 5)
            V.tensor_tensor(w_i_l[:], w_i_r, w_i_h[:].bitcast(F32), ALU.subtract)
            dve.wait_ge(wp_act, 7)
            V.tensor_tensor(w_la_l[:], gb[:, 2, 0:2 * P].rearrange("p (k n) -> p k n", k=KD),
                            w_la_h[:].bitcast(F32), ALU.subtract).then_inc(wp_dve, 1)
            dve.wait_ge(wp_act, 8)
            V.tensor_tensor(w_z0[32:64, :], gb[32:64, 0:2, :].rearrange("p k t -> p (k t)"),
                            w_z0[32:64, :].bitcast(F32), ALU.subtract).then_inc(wp_dve, 1)
            dve.wait_ge(wp_act, 9)
            V.tensor_tensor(w_zd[32:64, :], gb[32:64, 3:5, :].rearrange("p k t -> p (k t)"),
                            w_zd[32:64, :].bitcast(F32), ALU.subtract).then_inc(wp_dve, 1)

            for s in range(NCH + 1):
                g, r, p = s, s - 1, s + 1
                for n in range(N):
                    if g < NCH:
                        scan(g, n)
                        if n >= 2:
                            accumulate(g, n - 2)
                        if g % CPB != CPB - 1:
                            keep_state(g, n)
                    if s > 0:
                        if n == SL_Y:
                            dve.wait_ge(y_t, r + 1)
                            residual(4 * r, two_banks(0))
                            stats(4 * r)
                        if n == SL_N1:
                            norm_bias(4 * r)
                    if p < NCH:
                        if n == PR_MM:
                            pre_x(p)
                        if n == PR_SP:
                            pre_max(p)
                        if n == PR_G:
                            pre_dt(p)
                            pre_low(p)
                        if n == PR_G + 1:
                            pre_input(p)
                    if s > 0:
                        if n == SL_X1 + 1:
                            xt_low(3 * r, 0)
                        if n == SL_RT:
                            router(r)
                        if n == SL_UP:
                            dve.wait_ge(hwt_ps, r + 1)
                            dve.wait_ge(hw_hi, r + 1)
                            V.tensor_tensor(hw_l, gb[0:HR + 1, 4, :], hw_h.bitcast(F32),
                                            ALU.subtract).then_inc(hw_lo, 1)
                            dve.wait_ge(up_ps, r + 1)
                            residual(4 * r + 1, gb[:, 0:TT, 0:D])
                            stats(4 * r + 1)
                        if n == SL_N2:
                            norm_bias(4 * r + 1)
                            xt_low(3 * r + 1, 1)
                        if n == SL_QV:
                            keys(r)
                        if n == SL_S:
                            maxima(r)
                        if n == SL_P0:
                            finish_attention(r, 0)
                        if n == SL_P1:
                            finish_attention(r, 1)
                            dve.wait_ge(o_res, TT * (r + 1))
                            small(V.tensor_copy(rl[:, 0:1], rl[:, 0:1]), ln_r, 4 * r + 3)
                            stats(4 * r + 2)
                        if n == SL_N3:
                            norm_bias(4 * r + 2)
                            xt_low(3 * r + 2, 1)
                        if n == SL_L:
                            dve.wait_ge(l_hi, r + 1)
                            V.tensor_tensor(lr[64:96, :], gb[64:96, 3, :], lr[64:96, :].bitcast(F32),
                                            ALU.subtract).then_inc(l_lo, 1)
                        for m in range(FB):
                            if n == SL_F[m]:
                                mix(r, m)
                if g < NCH:
                    accumulate(g, N - 2)
                    accumulate(g, N - 1)
                if s > 0:
                    dve.wait_ge(mid_used, FB * (r + 1))
                    residual(4 * r + 3, gb[:, 1:3, :].rearrange("p a t -> p (a t)"), sgn[:, 1:2])
                    stats(4 * r + 3)
                    norm_bias(4 * r + 3)


def _layout(i):
    import numpy as np

    f = {k: np.ascontiguousarray(v) for k, v in i.items() if np.asarray(v).size}

    def pad(w, at, width):
        out = np.zeros((w.shape[0], width), w.dtype)
        for c in at:
            out[:, c:c + w.shape[1]] = w
        return out

    def by_partition(v):
        return np.ascontiguousarray(v.reshape(KD, P, -1).transpose(1, 0, 2)).reshape(P, KD, -1)

    w_x = f["L0_attn_w_x"]
    idx = np.arange(P)
    eye = np.eye(R, dtype=np.float32)
    sel = np.zeros((P, 2 * N), np.float32)
    for n in range(N):
        sel[[n, 32 + n], n] = 1
        sel[[64 + n, 96 + n], N + n] = 1
    w_bc = pad(w_x[:, 64:80], (0, 32), P) + 0
    w_bc[:, 64:80] = w_x[:, 80:96]
    w_bc[:, 96:112] = w_x[:, 80:96]
    sh = f["L1_attn_b_share"]
    b_sh = np.zeros((P, 1), sh.dtype)
    for c in (0, 32, 64):
        b_sh[c:c + 16, 0] = sh
    return {
        "x": f["L0_attn_x"],
        "w_in": f["L0_attn_w_in"], "w_in_t": f["L0_attn_w_in"].T,
        "w_xdt_t": w_x[:, :64].T, "w_dt": f["L0_attn_w_dt"], "w_bc": w_bc,
        "b_dt": by_partition(f["L0_attn_b_dt"])[:, :, 0], "d_skip": by_partition(f["L0_attn_Dp"])[:, :, 0],
        "a_log": by_partition(f["L0_attn_A_log"]), "sel_cols": sel,
        "w_cat": np.concatenate([f["L0_ffn_base_W"].T, f["L0_ffn_routed_A"].reshape(E * R, D).T,
                                 f["L0_ffn_shared_A"].T, f["L0_ffn_router_W"].T], 1),
        "w_up": np.concatenate([f["L0_ffn_routed_B"].transpose(0, 2, 1).reshape(E * R, D),
                                f["L0_ffn_shared_B"].T, f["L0_ffn_base_b"][None]], 0),
        "r_bias": np.broadcast_to(f["L0_ffn_router_b"], (P, TT, E)),
        "tie": np.broadcast_to(np.tril(np.ones((E, E), np.float32), -1), (P, E, E)),
        "w_sh": pad(f["L1_attn_W_share"], (0, 32, 64), P), "b_sh": b_sh,
        "w_v_t": f["L1_attn_Wv"].T, "w_o": f["L1_attn_Wo"],
        "bv": by_partition(f["L1_attn_bv"])[:, :, 0], "bo": f["L1_attn_bo"][None],
        "w_i_t": f["L1_ffn_wi_w"].T, "w_out_t": f["L1_ffn_wo_w"].T,
        "lora_a": f["L1_ffn_lora_As"].reshape(P, D),
        "lora_b": f["L1_ffn_lora_Bs"].transpose(0, 2, 1).reshape(P, FF),
        "pick_cols": eye[idx % R], "expert_of": (idx // R).astype(np.float32)[:, None],
        "top_i": np.broadcast_to(f["L1_ffn_top_k_indices"], (P, 2)),
        "top_v": np.broadcast_to(f["L1_ffn_top_k_values"], (P, 2)),
    }


def kernel(**inputs):
    import numpy as np
    import concourse.bacc as bacc
    from concourse.bass_utils import run_bass_kernel_spmd

    nc = bacc.Bacc("TRN2", target_bir_lowering=False, num_devices=1)
    arrays, args = {}, {}
    for name, v in _layout(inputs).items():
        v = np.ascontiguousarray(v)
        arrays[f"in_{name}"] = v
        args[name] = nc.dram_tensor(f"in_{name}", v.shape, mybir.dt.from_np(v.dtype), kind="ExternalInput").ap()
    args["out"] = nc.dram_tensor("out_x", (B, S, D), F32, kind="ExternalOutput").ap()
    program(nc, args)
    return run_bass_kernel_spmd(nc, [arrays], core_ids=[0]).results[0]["out_x"]
```

```python
from contextlib import ExitStack

import concourse.bass as bass
from concourse import mybir

F32 = mybir.dt.float32
F32R = mybir.dt.float32r
BF16 = mybir.dt.bfloat16
I32 = mybir.dt.int32
ALU = mybir.AluOpType
ACT = mybir.ActivationFunctionType
AX = mybir.AxisListType

P = 128
B, S, D = 2, 2048, 256
KD = D // P
T = 512
TT = T // P
CPB = S // T
NCH = B * CPB
N = 16
E, R = 6, 16
EP = E + 1
HR = EP * R
CAT = D + HR + E
FF = 1024
FB = FF // P
DT_MIN, DT_MAX = 0.001, 0.1
EPS = 1e-5
SCALE = 0.25
NEG = -1e38
RANKL = 96


def program(nc, a):
    with ExitStack() as ctx:
        def sb(name, shape, dt=F32):
            return ctx.enter_context(nc.sbuf_tensor(name, shape, dt))

        def sem(name):
            return ctx.enter_context(nc.semaphore(name))

        ident = sb("ident", [P, P])
        ident_bf = sb("ident_bf", [P, P], BF16)
        mask_bf = sb("mask_bf", [P, P], BF16)
        mask_t_bf = sb("mask_t_bf", [P, P], BF16)
        ones = sb("ones", [P, P])
        sel_cols = sb("sel_cols", [64, N])
        sel = sb("sel", [64, N], F32R)
        w_in_h = sb("w_in_h", [P, KD, D], F32R)
        w_in_l = sb("w_in_l", [P, KD, D], F32R)
        w_pre_h = sb("w_pre_h", [P, KD, D + P], F32R)
        w_pre_l = sb("w_pre_l", [P, KD, D + P], F32R)
        b_dt = sb("b_dt", [P, KD])
        d_skip = sb("d_skip", [P, KD])
        a_neg = sb("a_neg", [P, KD, N])
        a_h = sb("a_h", [P, KD, P], F32R)
        a_l = sb("a_l", [P, KD, P], F32R)
        w_cat_h = sb("w_cat_h", [P, KD, CAT], F32R)
        w_cat_l = sb("w_cat_l", [P, KD, CAT], F32R)
        w_up_h = sb("w_up_h", [HR + 1, D], F32R)
        w_up_l = sb("w_up_l", [HR + 1, D], F32R)
        r_bias = sb("r_bias", [P, TT, E])
        tie = sb("tie", [P, E, E])
        w_sh_h = sb("w_sh_h", [P, KD, P], F32R)
        w_sh_l = sb("w_sh_l", [P, KD, P], F32R)
        b_sh = sb("b_sh", [P, 1])
        w_vo_h = sb("w_vo_h", [P, KD, D], F32R)
        w_vo_l = sb("w_vo_l", [P, KD, D], F32R)
        bv_col = sb("bv_col", [P, KD])
        att_bias = sb("att_bias", [P, D])
        pick_cols = sb("pick_cols", [P, R])
        expert_of = sb("expert_of", [P, 1])
        top_i = sb("top_i", [P, 2], I32)
        top_f = sb("top_f", [P, 2])
        top_v = sb("top_v", [P, 2])
        picked = sb("picked", [P, 2])
        minus0 = sb("minus0", [P, 1])
        sgn = sb("sgn", [P, 2])
        absv = sb("absv", [P, 2])
        sgn01 = sb("sgn01", [P, 1])
        w_la_h = sb("w_la_h", [P, KD, P], F32R)
        w_la_l = sb("w_la_l", [P, KD, P], F32R)
        w_z0 = sb("w_z0", [RANKL, FF], F32R)
        w_zd = sb("w_zd", [RANKL, FF], F32R)
        w_i_h = sb("w_i_h", [P, KD, FF], F32R)
        w_i_l = sb("w_i_l", [P, KD, FF], F32R)
        w_out = sb("w_out", [P, FB, D])
        xs_h = sb("xs_h", [P, KD, T], F32R)
        xs_l = sb("xs_l", [P, KD, T], F32R)
        u_sb = sb("u_sb", [P, KD, T])
        dt_sb = sb("dt_sb", [P, 2, KD, T])
        sp_a = sb("sp_a", [P, KD, T])
        dtu = sp_a
        bc_sb = sb("bc_sb", [P, T])
        parts = sb("parts", [64, 2, T], F32R)
        bar = sb("bar", [P, 2, KD, T])
        hst = sb("hst", [P, 4, KD, T])
        c_rep = sb("c_rep", [P, 3, T])
        state = sb("state", [P, KD, N])
        acc = sb("acc", [P, KD, T])
        bnst = sb("bnst", [P, TT, 6])
        mv = sb("mv", [P, TT, 2])
        veps = sb("veps", [P, TT])
        rstd = sb("rstd", [P, TT])
        nbias = sb("nbias", [P, TT])
        bnst_f = sb("bnst_f", [P, TT, 6])
        mv_f = sb("mv_f", [P, TT, 2])
        veps_f = sb("veps_f", [P, TT])
        rstd_f = sb("rstd_f", [P, TT])
        nbias_f = sb("nbias_f", [P, TT])
        mhalf = sb("mhalf", [P, TT])
        rows_tm = sb("rows_tm", [P, 3, TT, D])
        xt_h = sb("xt_h", [P, KD, T], F32R)
        xt_l = sb("xt_l", [P, KD, T], F32R)
        xf_h = sb("xf_h", [P, KD, T], F32R)
        xf_l = sb("xf_l", [P, KD, T], F32R)
        lg = sb("lg", [P, TT, E])
        lmax = sb("lmax", [P, TT])
        ls = sb("ls", [P, TT, E])
        ex = sb("ex", [P, TT, E])
        rk_gt = sb("rk_gt", [P, TT, E, E])
        rk_eq = sb("rk_eq", [P, TT, E, E])
        rank = sb("rank", [P, TT, E])
        em = sb("em", [P, TT, E])
        e_sum = sb("e_sum", [P, TT])
        k_sum = sb("k_sum", [P, TT])
        gate = sb("gate", [P, TT, EP])
        hw = sb("hw", [P, TT, HR + 1])
        q_st = sb("q_st", [P, T], F32R)
        k_st = sb("k_st", [P, S], F32R)
        vc = sb("vc", [P, S // P, D + 1])
        smax = sb("smax", [P, TT, CPB])
        m4 = sb("m4", [P, TT])
        mhl = sb("mhl", [P, TT, 2], F32R)
        rl = sb("rl", [P, TT])
        lr = sb("lr", [RANKL, T], F32R)
        mid = sb("mid", [P, 2, T])
        aring = sb("aring", [P, 3, T])
        pring = sb("pring", [P, 2, T])
        sp_m = sb("sp_m", [P, KD, T])
        x_pre = sp_m[:, :, :].rearrange("p k (a d) -> p (k a) d", d=D)
        x2 = rows_tm[:, 2, :, :]

        def x13(g):
            return rows_tm[:, g % 2, :, :]

        dtu_h, dtu_l = xs_h, xs_l
        hw_h, hw_l = xt_h[0:HR + 1, 0, :], xt_h[0:HR + 1, 1, :]

        vflat = vc[:, :, :].rearrange("p a b -> p (a b)")
        w_i_r = vflat[:, 0:KD * FF].rearrange("p (k f) -> p k f", k=KD)
        w_cat_r = vflat[:, KD * FF:KD * FF + KD * CAT].rearrange("p (k f) -> p k f", k=KD)
        lora_b = vflat[:, KD * (FF + CAT):KD * (FF + CAT) + FF]
        xflat = rows_tm[:, :, :, :].rearrange("p a t d -> p (a t d)")

        def cut(flat, at, blocks, width):
            return flat[:, at:at + blocks * width].rearrange("p (k n) -> p k n", k=blocks)

        w_in_r, w_in_t = cut(xflat, 0, KD, D), cut(xflat, KD * D, KD, D)
        dt_bc_r = cut(xflat, 2 * KD * D, KD, D + P)
        w_sh_r = cut(xflat, 3 * KD * D + KD * P, KD, P)
        w_v_t, w_o = cut(xflat, 4 * KD * D, KD, D), cut(xflat, 5 * KD * D, KD, D)
        mflat = aring[:, :, :].rearrange("p a t -> p (a t)")
        lora_a = mflat[:, 0:D]
        w_up_r = mflat[0:HR + 1, D:2 * D]
        bv_rep = cut(mflat, 4 * D, KD, P)
        a_rep = cut(mflat, 5 * D, KD, P)
        prflat = pring[:, :, :].rearrange("p a t -> p (a t)")
        bo_row = prflat[0:1, 0:D]
        sel_a128 = prflat[:, D:D + P]
        sel_0, sel_d = prflat[:, 2 * D:2 * D + RANKL], prflat[:, 2 * D + P:2 * D + P + RANKL]
        w_xdt_t, w_dt = mflat[0:64, 2 * D:3 * D], mflat[0:64, 3 * D:4 * D]

        bi = ctx.enter_context(nc.psum_tensor("bi", [P, 2, T], F32))
        gb = ctx.enter_context(nc.psum_tensor("gb", [P, 6, T], F32))

        ld_x = sem("ld_x")
        c_kept = sem("c_kept")
        c_in = [sem(f"c_in{i}") for i in range(3)]
        ld_pre, ld_cat, ld_att, ld_ffn = sem("ld_pre"), sem("ld_cat"), sem("ld_att"), sem("ld_ffn")
        consts = sem("consts")
        pc_ready = sem("pc_ready")
        wp_pe, wp_act, wp_dve = sem("wp_pe"), sem("wp_act"), sem("wp_dve")
        wd = sem("wd")
        wa = sem("wa")
        xs_t = sem("xs_t")
        xs_hi, xs_lo = sem("xs_hi"), sem("xs_lo")
        u_ps, z_ps, bc_ps, g_ps = sem("u_ps"), sem("z_ps"), sem("bc_ps"), sem("g_ps")
        u_cp, bc_cp = sem("u_cp"), sem("bc_cp")
        sp_abs, sp_exp, sp_ln = sem("sp_abs"), sem("sp_exp"), sem("sp_ln")
        sp_max, sp_sum, dt_ok = sem("sp_max"), sem("sp_sum"), sem("dt_ok")
        dtu_ok, dtu_hi, dtu_lo = sem("dtu_ok"), sem("dtu_hi"), sem("dtu_lo")
        inp_ok, inp_hi, inp_lo = sem("inp_ok"), sem("inp_hi"), sem("inp_lo")
        bar_ok = sem("bar_ok")
        ir_ok = sem("ir_ok")
        ux_h, ux_l = sem("ux_h"), sem("ux_l")
        scan_ok = sem("scan_ok")
        st_ok = sem("st_ok")
        pr_ok = sem("pr_ok")
        acc_ok = sem("acc_ok")
        y_t = sem("y_t")
        ln_r, ln_bn, ln_mv, ln_ve = sem("ln_r"), sem("ln_bn"), sem("ln_mv"), sem("ln_ve")
        ln_rstd, ln_nb, ln_x = sem("ln_rstd"), sem("ln_nb"), sem("ln_x")
        lf_r, lf_bn, lf_mv, lf_ve = sem("lf_r"), sem("lf_bn"), sem("lf_mv"), sem("lf_ve")
        lf_rstd, lf_nb, lf_x = sem("lf_rstd"), sem("lf_nb"), sem("lf_x")
        xt_ps, xt_hi, xt_lo = sem("xt_ps"), sem("xt_hi"), sem("xt_lo")
        lgate = sem("lgate")
        base_ps = sem("base_ps")
        cat_ps, lg_ok, rt, ex_ok, hw_ok = sem("cat_ps"), sem("lg_ok"), sem("rt"), sem("ex_ok"), sem("hw_ok")
        hwt_ps, hw_hi, hw_lo, up_ps = sem("hwt_ps"), sem("hw_hi"), sem("hw_lo"), sem("up_ps")
        sh_ps, q_hi, k_hi, q_lo, k_lo = sem("sh_ps"), sem("q_hi"), sem("k_hi"), sem("q_lo"), sem("k_lo")
        v_ps, v_ok, x2b_ok = sem("v_ps"), sem("v_ok"), sem("x2b_ok")
        s_ps, s_mx = sem("s_ps"), sem("s_mx")
        m_ok, mhl_ok, mt_ps, mt_ok = sem("m_ok"), sem("mhl_ok"), sem("mt_ps"), sem("mt_ok")
        st_ps, p_ok, pv_ok = sem("st_ps"), sem("p_ok"), sem("pv_ok")
        o_ok, rl_ok, o_res = sem("o_ok"), sem("rl_ok"), sem("o_res")
        l_ps, l_hi, l_lo = sem("l_ps"), sem("l_hi"), sem("l_lo")
        z0_ps, zd_ps, a0_ok, a1_ok, mid_ok, mid_used, out_ps = (
            sem("z0_ps"), sem("zd_ps"), sem("a0_ok"), sem("a1_ok"), sem("mid_ok"), sem("mid_used"), sem("out_ps"))
        stored = sem("stored")

        n_s = [TT * (g % CPB + 1) for g in range(NCH)]
        n_p = [[(4 * (g % CPB) + 2 * h + 2) // 2 for h in range(2)] for g in range(NCH)]
        s_base = [sum(n_s[:g]) for g in range(NCH)]
        p_base = [[sum(sum(x) for x in n_p[:g]) + (n_p[g][0] if h else 0) for h in range(2)] for g in range(NCH)]

        def row(g, n):
            return g * N + n

        def kept(g, n):
            return (g - g // CPB) * N + n + 1

        UNITS = 8

        def timeline(s):
            c = (s - 1) % CPB
            score = 44 + 2.4 * (c + 1)
            p0 = score + 4
            p1 = p0 + 2.15 * (2 * c + 1)
            end = p1 + 2.15 * (2 * c + 2)
            return score, p0, p1, end, end + 11.5

        def pacer(s, emit):
            total = timeline(s)[-1] if 1 <= s <= NCH else 40.0
            done = [0]

            def until(t):
                while done[0] < N and done[0] * total / N <= t:
                    emit(done[0])
                    done[0] += 1
            return until

        block = ctx.enter_context(nc.Block())

        @block.sync
        def _(sp):
            def rows(w):
                return w.rearrange("(k p) n -> p k n", p=P)

            for dst, src in ((w_xdt_t, a["w_xdt_t"]), (w_dt, a["w_dt"]),
                             (w_in_t, rows(a["w_in_t"])), (w_in_r, rows(a["w_in"])),
                             (dt_bc_r[:, :, D:D + P], rows(a["w_bc"])), (b_dt[:], a["b_dt"]),
                             (d_skip[:], a["d_skip"]), (a_neg[:], a["a_log"]), (sel_cols[:], a["sel_cols"])):
                sp.dma_start(dst, src).then_inc(ld_pre, 16)
            for dst, src in ((w_cat_r, rows(a["w_cat"])), (w_up_r, a["w_up"]),
                             (r_bias[:], a["r_bias"]), (tie[:], a["tie"])):
                sp.dma_start(dst, src).then_inc(ld_cat, 16)
            for dst, src in ((w_sh_r, rows(a["w_sh"])), (b_sh[:], a["b_sh"]), (w_v_t, rows(a["w_v_t"])),
                             (w_o, rows(a["w_o"])), (bv_col[:], a["bv"]), (bo_row, a["bo"])):
                sp.dma_start(dst, src).then_inc(ld_att, 16)
            for dst, src in ((w_i_r, rows(a["w_i_t"])), (lora_a, a["lora_a"]), (lora_b, a["lora_b"]),
                             (pick_cols[:], a["pick_cols"]), (expert_of[:], a["expert_of"]),
                             (top_i[:], a["top_i"]), (top_v[:], a["top_v"]), (w_out[:], rows(a["w_out_t"]))):
                sp.dma_start(dst, src).then_inc(ld_ffn, 16)
            for k in range(NCH * N):
                g, n = divmod(k, N)
                if n == 0:
                    sp.wait_ge(bc_cp, g + 1)
                    sp.dma_start(a["c_rows"][g % 2], bc_sb[64:64 + N, :]).then_inc(c_kept, 16)
                    sp.wait_ge(c_kept, 16 * (g + 1))
                if k >= 3:
                    sp.wait_ge(pr_ok, k - 2)
                sp.dma_start(c_rep[:, k % 3, :], a["c_rows"][g % 2, n, :].partition_broadcast(P)
                             ).then_inc(c_in[k % 3], 16)

        @block.gpsimd
        def _(pool):
            pool.memset(ident[:], 0.0).then_inc(consts, 1)
            pool.memset(ones[:], 1.0).then_inc(consts, 1)
            pool.wait_ge(consts, 2)
            pool.affine_select(out=ident[:], in_=ident[:], compare_op=ALU.not_equal, fill=1.0, base=0,
                               pattern=[[-1, P]], channel_multiplier=1).then_inc(consts, 1)
            pool.memset(ident_bf[:], 0.0).then_inc(consts, 1)
            pool.memset(mask_bf[:], 0.0).then_inc(consts, 1)
            pool.memset(mask_t_bf[:], 0.0).then_inc(consts, 1)
            pool.memset(mhalf[:], -0.5).then_inc(consts, 1)
            pool.memset(gate[:], 1.0).then_inc(consts, 1)
            pool.memset(hw[:], 1.0).then_inc(consts, 1)
            pool.wait_ge(consts, 9)
            pool.affine_select(out=ident_bf[:], in_=ident_bf[:], compare_op=ALU.not_equal, fill=1.0, base=0,
                               pattern=[[-1, P]], channel_multiplier=1).then_inc(consts, 1)
            pool.affine_select(out=mask_bf[:], in_=mask_bf[:], compare_op=ALU.is_ge, fill=NEG, base=0,
                               pattern=[[-1, P]], channel_multiplier=1).then_inc(consts, 1)
            pool.affine_select(out=mask_t_bf[:], in_=mask_t_bf[:], compare_op=ALU.is_ge, fill=NEG, base=0,
                               pattern=[[1, P]], channel_multiplier=-1).then_inc(consts, 1)

            def product(g, n):
                k = row(g, n)
                if g % CPB != CPB - 1:
                    pool.wait_ge(st_ok, kept(g, n))
                else:
                    pool.wait_ge(scan_ok, 2 * k + 2)
                pool.wait_ge(c_in[k % 3], 16 * (k // 3 + 1))
                h = hst[:, k % 4, :, :]
                pool.tensor_tensor(h, h, c_rep[:, k % 3, :].unsqueeze(1).to_broadcast([P, KD, T]),
                                   ALU.mult).then_inc(pr_ok, 1)

            def norm_power(q):
                pool.wait_ge(ln_ve, q + 1)
                pool.tensor_tensor(rstd[:], veps[:], mhalf[:], ALU.pow).then_inc(ln_rstd, 1)

            for s in range(NCH + 2):
                r, f = s - 1, s - 2
                until = pacer(s, lambda n: product(s, n) if s < NCH else None)
                if s == 0:
                    until(12)
                    pool.wait_ge(wp_act, 9)
                    pool.wait_ge(wp_dve, 8)
                    pool.wait_ge(wp_pe, 8)
                    pool.memset(vc[:, :, D:D + 1], 1.0).then_inc(pc_ready, 1)
                if 0 <= r < NCH:
                    score, p0, p1, end, total = timeline(s)
                    until(1)
                    norm_power(3 * r)
                    until(27)
                    norm_power(3 * r + 1)
                    until(39)
                    pool.wait_ge(xt_ps, 3 * r + 2)
                    pool.wait_ge(wp_act, 6)
                    pool.tensor_tensor(x2, x2, att_bias[:].unsqueeze(1).to_broadcast([P, TT, D]),
                                       ALU.add).then_inc(x2b_ok, 1)
                    until(end + 1)
                    norm_power(3 * r + 2)
                until(1e9)
                if 0 <= f:
                    pool.wait_ge(lf_ve, f + 1)
                    pool.tensor_tensor(rstd_f[:], veps_f[:], mhalf[:], ALU.pow).then_inc(lf_rstd, 1)

        @block.scalar
        def _(act):
            def copy(out, in_):
                return nc.scalar.activation(out, in_, ACT.Copy)

            act.wait_ge(ld_pre, 9 * 16)
            nc.scalar.activation(a_neg[:], a_neg[:], ACT.Exp).then_inc(wa, 1)
            copy(w_in_h[:], w_in_r).then_inc(wp_act, 1)
            act.wait_ge(wp_pe, 1)
            copy(dt_bc_r[:, :, 0:D], gb[:, 0, :].rearrange("p (k n) -> p k n", k=KD)).then_inc(wp_act, 1)
            act.wait_ge(wp_pe, 2)
            copy(w_pre_h[:], gb[:, 1:3, 0:D + P]).then_inc(wp_act, 1)
            act.wait_ge(wd, 2)
            copy(a_h[:], a_rep).then_inc(wp_act, 1)

            def load_x(g):
                b, c = divmod(g, CPB)
                if g >= 1:
                    act.wait_ge(sp_sum, g)
                act.dma_start(x_pre, a["x"][b, c * T:(c + 1) * T, :].rearrange("(t p) d -> p t d", p=P)
                              ).then_inc(ld_x, 16)

            def store(g):
                b, c = divmod(g, CPB)
                act.wait_ge(lf_x, TT * (g + 1))
                act.dma_start(a["out"][b, c * T:(c + 1) * T, :].rearrange("(t p) d -> p t d", p=P),
                              x13(g)).then_inc(stored, 16)

            def pre_x(g):
                act.wait_ge(xs_t, g + 1)
                if g >= 1:
                    act.wait_ge(g_ps, g)
                copy(xs_h[:].rearrange("p k t -> p (k t)"),
                     gb[:, 0:2, :].rearrange("p k t -> p (k t)")).then_inc(xs_hi, 1)

            def pre_u(g):
                act.wait_ge(u_ps, g + 1)
                if g >= 1:
                    act.wait_ge(acc_ok, row(g - 1, 0) + 1)
                copy(u_sb[:, 0, :], gb[:, 2, :]).then_inc(u_cp, 1)
                copy(u_sb[:, 1, :], gb[:, 0, :]).then_inc(u_cp, 1)

            def pre_z(g):
                if g >= 1:
                    act.wait_ge(dtu_lo, g)
                act.wait_ge(z_ps, g + 1)
                for j in range(KD):
                    nc.scalar.activation(sp_a[:, j, :], gb[:, 1 + j, :], ACT.Abs,
                                         bias=b_dt[:, j:j + 1]).then_inc(sp_abs, 1)
                act.wait_ge(bc_ps, g + 1)
                if g >= 1:
                    act.wait_ge(inp_lo, g)
                    act.wait_ge(c_kept, 16 * g)
                copy(bc_sb[:], gb[:, 0, :]).then_inc(bc_cp, 1)

            def pre_softplus(g):
                act.wait_ge(sp_abs, 2 * g + 2)
                nc.scalar.activation(sp_a[:], sp_a[:], ACT.Exp, scale=-1.0).then_inc(sp_exp, 1)
                act.wait_ge(sp_exp, g + 1)
                nc.scalar.activation(sp_a[:], sp_a[:], ACT.Ln, bias=ones[:, 0:1]).then_inc(sp_ln, 1)

            def pre_dtu(g):
                act.wait_ge(dtu_ok, g + 1)
                act.wait_ge(bc_ps, g + 1)
                act.wait_ge(ux_l, g + 1)
                copy(dtu_h[:], dtu[:]).then_inc(dtu_hi, 1)

            def decay(g, n):
                k = row(g, n)
                act.wait_ge(dt_ok, g + 1)
                if k >= 2:
                    act.wait_ge(scan_ok, 2 * (k - 2) + 2)
                for j in range(KD):
                    nc.scalar.activation(bar[:, k % 2, j, :], dt_sb[:, g % 2, j, :], ACT.Exp,
                                         scale=a_neg[:, j, n:n + 1]).then_inc(bar_ok, 1)

            def normalize(q, out, src):
                act.wait_ge(ln_nb, q + 1)
                if q % 3 == 0 and q >= 6:
                    act.wait_ge(stored, 16 * (q // 3 - 1))
                for t in range(TT):
                    nc.scalar.activation(out[:, t, :], src[:, t, :], ACT.Identity, scale=rstd[:, t:t + 1],
                                         bias=nbias[:, t:t + 1]).then_inc(ln_x, 1)

            def normalize_last(g):
                act.wait_ge(lf_nb, g + 1)
                for t in range(TT):
                    nc.scalar.activation(x13(g)[:, t, :], x13(g)[:, t, :], ACT.Identity,
                                         scale=rstd_f[:, t:t + 1], bias=nbias_f[:, t:t + 1]).then_inc(lf_x, 1)

            def xt_high(i, out):
                act.wait_ge(xt_ps, i + 1)
                copy(out[:].rearrange("p k t -> p (k t)"),
                     gb[:, 0:2, :].rearrange("p k t -> p (k t)")).then_inc(xt_hi, 1)

            def keys(g):
                b, c = divmod(g, CPB)
                act.wait_ge(sh_ps, g + 1)
                nc.scalar.activation(q_st[0:96, :], gb[0:96, 2, :], ACT.Identity,
                                     bias=b_sh[0:96, :]).then_inc(q_hi, 1)
                nc.scalar.activation(k_st[0:96, c * T:(c + 1) * T], gb[0:96, 2, :], ACT.Identity,
                                     bias=b_sh[0:96, :]).then_inc(k_hi, 1)
                act.wait_ge(v_ps, g + 1)
                act.wait_ge(pc_ready, 1)
                for h in range(2):
                    copy(vc[:, 4 * c + 2 * h:4 * c + 2 * h + 2, 0:D],
                         gb[:, h, :].rearrange("p (t d) -> p t d", t=2)).then_inc(v_ok, 1)

            def max_rows(g):
                act.wait_ge(mt_ps, g + 1)
                copy(q_st[96:98, :], gb[0:2, 2, :]).then_inc(mt_ok, 1)

            def exp_pair(g, h, i):
                k = p_base[g][h] + i
                act.wait_ge(st_ps, k + 1)
                if k >= 2:
                    act.wait_ge(pv_ok, k - 1)
                nc.scalar.activation(pring[:, k % 2, :], gb[:, 2, :], ACT.Exp, scale=SCALE).then_inc(p_ok, 1)

            def relus(g, j):
                if j < UNITS:
                    k = g * UNITS + j
                    if k >= 2:
                        act.wait_ge(mid_ok, k - 1)
                    act.wait_ge(z0_ps, k + 1)
                    nc.scalar.activation(aring[:, 2 * k % 3, :], gb[:, 3 + k % 2, :], ACT.Relu,
                                         scale=absv[:, 0:1]).then_inc(a0_ok, 1)
                if 1 <= j <= UNITS:
                    k = g * UNITS + j - 1
                    if k >= 1:
                        act.wait_ge(mid_ok, k)
                    act.wait_ge(zd_ps, k + 1)
                    nc.scalar.activation(aring[:, (2 * k + 1) % 3, :], gb[:, 3 + k % 2, :], ACT.Relu,
                                         scale=absv[:, 1:2]).then_inc(a1_ok, 1)

            load_x(0)
            pre_x(0)
            pre_u(0)
            pre_z(0)
            pre_softplus(0)
            pre_dtu(0)
            act.wait_ge(ld_cat, 4 * 16)
            copy(w_cat_h[:], w_cat_r).then_inc(wa, 1)
            copy(w_up_h[:], w_up_r).then_inc(wp_act, 1)
            decay(0, 0)
            act.wait_ge(wp_pe, 4)
            copy(att_bias[:], gb[:, 4, 0:D]).then_inc(wp_act, 1)
            copy(w_vo_h[:], gb[:, 1, :].rearrange("p (k n) -> p k n", k=KD)).then_inc(wa, 1)
            act.wait_ge(ld_att, 6 * 16)
            copy(w_sh_h[:], w_sh_r).then_inc(wa, 1)
            act.wait_ge(wp_pe, 5)
            act.wait_ge(ld_ffn, 8 * 16)
            copy(w_i_h[:], w_i_r).then_inc(wa, 1)
            copy(w_la_h[:], gb[:, 2, 0:2 * P].rearrange("p (k n) -> p k n", k=KD)).then_inc(wp_act, 1)
            decay(0, 1)
            act.wait_ge(wp_pe, 6)
            copy(w_z0[:], gb[0:RANKL, 0:2, :].rearrange("p k t -> p (k t)")).then_inc(wp_act, 1)
            act.wait_ge(wp_pe, 7)
            copy(w_zd[:], gb[0:RANKL, 4:6, :].rearrange("p k t -> p (k t)")).then_inc(wp_act, 1)

            for s in range(NCH + 2):
                g, r, f, p = s, s - 1, s - 2, s + 1

                def ahead(n):
                    if g < NCH and n + 1 < N and (g or n):
                        decay(g, n + 1)
                    elif n + 1 == N and g + 1 < NCH:
                        decay(g + 1, 0)

                until = pacer(s, ahead)
                main, ffn = 0 <= r < NCH, 0 <= f
                score, p0, p1, end, total = timeline(s)
                if p < NCH:
                    load_x(p)
                if s == 0:
                    for t, part in ((10, pre_x), (14, pre_u), (17, pre_z), (19, pre_softplus), (24, pre_dtu)):
                        until(t)
                        part(p)
                if main:
                    until(1)
                    if ffn:
                        relus(f, 0)
                        relus(f, 1)
                    until(6)
                    normalize(3 * r, x13(r), gb[:, 0:2, :].rearrange("p a (t d) -> p (a t) d", d=D))
                    until(9)
                    xt_high(3 * r, xt_h)
                    until(12)
                    if ffn:
                        relus(f, 2)
                    until(16)
                    act.wait_ge(lg_ok, r + 1)
                    nc.scalar.activation(ex[:], ls[:], ACT.Exp).then_inc(ex_ok, 1)
                    if ffn:
                        relus(f, 3)
                    until(21.5)
                    act.wait_ge(hwt_ps, r + 1)
                    copy(hw_h, gb[0:HR + 1, 2, :]).then_inc(hw_hi, 1)
                    if ffn:
                        relus(f, 4)
                    if p < NCH:
                        until(28)
                        pre_x(p)
                        until(31)
                        pre_u(p)
                    until(32)
                    normalize(3 * r + 1, x2, x13(r))
                    if p < NCH:
                        until(34)
                        pre_z(p)
                        pre_softplus(p)
                    until(37)
                    xt_high(3 * r + 1, xt_h)
                    if ffn:
                        relus(f, 5)
                    until(42)
                    keys(r)
                    if p < NCH:
                        pre_dtu(p)
                    until(score)
                    max_rows(r)
                    if ffn:
                        relus(f, 6)
                    for i in range(n_p[r][0]):
                        until(p0 + 2.15 * i)
                        exp_pair(r, 0, i)
                    if ffn:
                        relus(f, 7)
                    for i in range(n_p[r][1]):
                        until(p1 + 2.15 * i)
                        exp_pair(r, 1, i)
                    until(end)
                    if ffn:
                        relus(f, 8)
                    until(end + 5)
                    normalize(3 * r + 2, x13(r), x2)
                    until(end + 9)
                    xt_high(3 * r + 2, xf_h)
                    until(total - 1)
                    act.wait_ge(l_ps, r + 1)
                    copy(lr[:], gb[0:RANKL, 2, :]).then_inc(l_hi, 1)
                elif ffn:
                    for j in range(UNITS + 1):
                        relus(f, j)
                until(1e9)
                if ffn:
                    normalize_last(f)
                    store(f)
            act.wait_ge(stored, 16 * NCH)

        @block.tensor
        def _(pe):
            def mm3(out, lh, ll, rh, rl_, start, stop, skip=False):
                nc.tensor.matmul(out, lh, rh, start=start, stop=False, skip_group_check=skip)
                nc.tensor.matmul(out, ll, rh, start=False, stop=False, skip_group_check=skip)
                return nc.tensor.matmul(out, lh, rl_, start=False, stop=stop, skip_group_check=skip)

            pe.wait_ge(ld_pre, 9 * 16)
            for k in range(KD):
                mm = nc.tensor.matmul(gb[:, 0, k * D:(k + 1) * D], w_xdt_t[:, k * P:(k + 1) * P], w_dt,
                                      start=(k == 0), stop=True, skip_group_check=True)
            mm.then_inc(wp_pe, 1)
            pe.wait_ge(wp_act, 2)
            for m in range(KD):
                for k in range(KD):
                    mm = nc.tensor.matmul(gb[:, 1 + m, 0:D + P], w_in_t[:, k, m * P:(m + 1) * P],
                                          dt_bc_r[:, k, :], start=(k == 0), stop=(k == KD - 1))
            mm.then_inc(wp_pe, 1)

            def pre_transpose(g):
                pe.wait_ge(ld_x, 16 * (g + 1))
                for k in range(KD):
                    for t in range(TT):
                        mm = nc.tensor.transpose(gb[:, k, t * P:(t + 1) * P],
                                                 x_pre[:, t, k * P:(k + 1) * P], ident[:])
                mm.then_inc(xs_t, 1)

            def project(out, w_h, w_l, cols):
                for k in range(KD):
                    mm = mm3(out, w_h[:, k, cols], w_l[:, k, cols], xs_h[:, k, :], xs_l[:, k, :],
                             k == 0, k == KD - 1)
                return mm

            def pre_u(g):
                pe.wait_ge(xs_hi, g + 1)
                pe.wait_ge(xs_lo, g + 1)
                project(gb[:, 2, :], w_in_h, w_in_l, slice(0, P))
                project(gb[:, 0, :], w_in_h, w_in_l, slice(P, D)).then_inc(u_ps, 1)

            def pre_z(g):
                pe.wait_ge(u_cp, 2 * g + 1)
                project(gb[:, 1, :], w_pre_h, w_pre_l, slice(0, P))
                project(gb[:, 2, :], w_pre_h, w_pre_l, slice(P, D)).then_inc(z_ps, 1)
                pe.wait_ge(u_cp, 2 * g + 2)
                project(gb[:, 0, :], w_pre_h, w_pre_l, slice(D, D + P)).then_inc(bc_ps, 1)

            def pre_input(g):
                pe.wait_ge(dtu_hi, g + 1)
                pe.wait_ge(dtu_lo, g + 1)
                for k in range(KD):
                    mm = mm3(gb[:, 2, :], a_h[:, k, :], a_l[:, k, :], dtu_h[:, k, :], dtu_l[:, k, :],
                             k == 0, k == KD - 1)
                mm.then_inc(g_ps, 1)

            def spread(g, n):
                k = row(g, n)
                if n == 0:
                    pe.wait_ge(inp_lo, g + 1)
                if k >= 2:
                    pe.wait_ge(scan_ok, 2 * (k - 2) + 2)
                nc.tensor.matmul(bi[:, k % 2, :], sel[:, n:n + 1].to_broadcast([64, P]), parts[:, g % 2, :],
                                 start=True, stop=True).then_inc(ir_ok, 1)

            def xt_transpose(i, src):
                pe.wait_ge(ln_x, TT * (i + 1))
                for k in range(KD):
                    for t in range(TT):
                        mm = nc.tensor.transpose(gb[:, k, t * P:(t + 1) * P],
                                                 src[:, t, k * P:(k + 1) * P], ident[:])
                mm.then_inc(xt_ps, 1)

            def y_transpose(g):
                pe.wait_ge(acc_ok, row(g, N))
                for t in range(TT):
                    for k in range(KD):
                        mm = nc.tensor.transpose(gb[:, t // 2, (t % 2) * D + k * P:(t % 2) * D + (k + 1) * P],
                                                 acc[:, k, t * P:(t + 1) * P], ident[:])
                mm.then_inc(y_t, 1)

            def inner_columns(g):
                w = HR + E
                pe.wait_ge(xt_hi, 3 * g + 1)
                pe.wait_ge(xt_lo, 3 * g + 1)
                for t in range(TT):
                    ts = slice(t * P, (t + 1) * P)
                    for k in range(KD):
                        mm = mm3(gb[:, 2, t * w:(t + 1) * w], xt_h[:, k, ts], xt_l[:, k, ts],
                                 w_cat_h[:, k, D:], w_cat_l[:, k, D:], k == 0 and t == 0, k == KD - 1, True)
                mm.then_inc(cat_ps, 1)

            def two_tiles(t):
                return gb[:, t // 2, (t % 2) * D:(t % 2 + 1) * D]

            def base(g):
                for t in range(TT):
                    ts = slice(t * P, (t + 1) * P)
                    for k in range(KD):
                        mm = mm3(two_tiles(t), xt_h[:, k, ts], xt_l[:, k, ts], w_cat_h[:, k, 0:D],
                                 w_cat_l[:, k, 0:D], k == 0 and t % 2 == 0, False, True)
                mm.then_inc(base_ps, 1)

            def up_transpose(g):
                pe.wait_ge(hw_ok, g + 1)
                for t in range(TT):
                    mm = nc.tensor.transpose(gb[0:HR + 1, 2, t * P:(t + 1) * P], hw[:, t, :], ident[:])
                mm.then_inc(hwt_ps, 1)

            def up(g):
                pe.wait_ge(hw_hi, g + 1)
                pe.wait_ge(hw_lo, g + 1)
                for t in range(TT):
                    ts = slice(t * P, (t + 1) * P)
                    mm = mm3(two_tiles(t), hw_h[:, ts], hw_l[:, ts], w_up_h[:], w_up_l[:], False, True, True)
                mm.then_inc(up_ps, 1)

            def share_values(g):
                pe.wait_ge(xt_hi, 3 * g + 2)
                pe.wait_ge(xt_lo, 3 * g + 2)
                for k in range(KD):
                    mm = mm3(gb[:, 2, :], w_sh_h[:, k, :], w_sh_l[:, k, :], xt_h[:, k, :], xt_l[:, k, :],
                             k == 0, k == KD - 1)
                mm.then_inc(sh_ps, 1)
                for t in range(TT):
                    for k in range(KD):
                        ts = slice(t * P, (t + 1) * P)
                        mm = mm3(two_tiles(t), xt_h[:, k, ts], xt_l[:, k, ts],
                                 w_vo_h[:, k, :], w_vo_l[:, k, :], k == 0 and t % 2 == 0, k == KD - 1, True)
                mm.then_inc(v_ps, 1)

            def score_block(g, i, kk):
                c = g % CPB
                j = i * (c + 1) + kk
                if j == 0:
                    pe.wait_ge(q_lo, g + 1)
                    pe.wait_ge(k_lo, g + 1)
                    pe.wait_ge(v_ok, 2 * g + 2)
                if j >= 3:
                    pe.wait_ge(s_mx, s_base[g] + j - 2)
                w = T if kk < c else (i + 1) * P
                mm = nc.tensor.matmul(gb[:, j % 3, 0:w], q_st[0:96, i * P:(i + 1) * P],
                                      k_st[0:96, kk * T:kk * T + w], start=True, stop=True)
                if kk == c:
                    mm = nc.tensor.matmul(gb[:, j % 3, w - P:w], ident_bf[:], mask_bf[:],
                                          start=False, stop=True, skip_group_check=True)
                mm.then_inc(s_ps, 1)

            def max_transpose(g):
                pe.wait_ge(mhl_ok, 2 * g + 2)
                for i in range(TT):
                    mm = nc.tensor.transpose(gb[0:2, 2, i * P:(i + 1) * P], mhl[:, i, :].bitcast(F32), ident[:])
                mm.then_inc(mt_ps, 1)

            def scores_t(g, h, i):
                k = p_base[g][h] + i
                pe.wait_ge(mt_ok, g + 1)
                if k >= 1:
                    pe.wait_ge(p_ok, k)
                last = i == n_p[g][h] - 1
                for e in range(2):
                    kt = 2 * i + e
                    mm = nc.tensor.matmul(gb[:, 2, e * D:(e + 1) * D], k_st[:, kt * P:(kt + 1) * P],
                                          q_st[:, 2 * h * P:(2 * h + 2) * P], start=(e == 0),
                                          stop=True, skip_group_check=True)
                    if last:
                        mm = nc.tensor.matmul(gb[:, 2, e * D + e * P:e * D + (e + 1) * P],
                                              ident_bf[:], mask_t_bf[:], start=False, stop=True,
                                              skip_group_check=True)
                mm.then_inc(st_ps, 1)

            def values(g, h, i):
                k = p_base[g][h] + i
                pe.wait_ge(p_ok, k + 1)
                if h == 1 and i == 0:
                    pe.wait_ge(o_res, TT * g + 2)
                last = i == n_p[g][h] - 1
                for e in range(2):
                    kt = 2 * i + e
                    for ql in range(2):
                        if last and e == 1 and ql == 0:
                            continue
                        mm = nc.tensor.matmul(gb[:, ql, 0:D + 1],
                                              pring[:, k % 2, e * D + ql * P:e * D + (ql + 1) * P],
                                              vc[:, kt, :], start=(kt == 0),
                                              stop=last and (e == 1 or ql == 0))
                mm.then_inc(pv_ok, 1)

            def low_rank(g):
                pe.wait_ge(xt_hi, 3 * g + 3)
                pe.wait_ge(xt_lo, 3 * g + 3)
                for k in range(KD):
                    mm = mm3(gb[:, 2, :], w_la_h[:, k, :], w_la_l[:, k, :], xf_h[:, k, :], xf_l[:, k, :],
                             k == 0, k == KD - 1)
                mm.then_inc(l_ps, 1)

            def feed_forward(g, j):
                def blocks(u):
                    k = g * UNITS + u
                    half, pair = divmod(u, UNITS // 2)
                    return k, slice(half * D, (half + 1) * D), [2 * pair, 2 * pair + 1], gb[:, 3 + k % 2, :]

                if j < UNITS:
                    k, ts, ms, bank = blocks(j)
                    if k >= 2:
                        pe.wait_ge(a1_ok, k - 1)
                    if j == 0:
                        pe.wait_ge(l_hi, g + 1)
                        pe.wait_ge(l_lo, g + 1)
                    for e, m in enumerate(ms):
                        cols, out = slice(m * P, (m + 1) * P), bank[:, e * D:(e + 1) * D]
                        for kk in range(KD):
                            mm3(out, w_i_h[:, kk, cols], w_i_l[:, kk, cols], xf_h[:, kk, ts], xf_l[:, kk, ts],
                                kk == 0 and e == 0, False, True)
                        mm = nc.tensor.matmul(out, w_z0[:, cols], lr[:, ts], start=False, stop=True,
                                              skip_group_check=True)
                    mm.then_inc(z0_ps, 1)
                if 1 <= j <= UNITS:
                    k, ts, ms, bank = blocks(j - 1)
                    pe.wait_ge(a0_ok, k + 1)
                    for e, m in enumerate(ms):
                        mm = nc.tensor.matmul(bank[:, e * D:(e + 1) * D], w_zd[:, m * P:(m + 1) * P], lr[:, ts],
                                              start=False, stop=True, skip_group_check=True)
                    mm.then_inc(zd_ps, 1)
                if j >= 2:
                    k, ts, ms, bank = blocks(j - 2)
                    pe.wait_ge(mid_ok, k + 1)
                    if (j - 2) % 4 == 0 and k > 0:
                        pe.wait_ge(lf_r, 2 * g + (j - 2) // 4)
                    for e, m in enumerate(ms):
                        for t in range(2):
                            mm = nc.tensor.matmul(gb[:, 5, t * D:(t + 1) * D],
                                                  mid[:, k % 2, e * D + t * P:e * D + (t + 1) * P],
                                                  w_out[:, m, :], start=(ms[0] == 0 and e == 0 and t == 0),
                                                  stop=(ms[1] == FB - 1 and e == 1), skip_group_check=True)
                    mm.then_inc(mid_used, 1)

            pe.wait_ge(consts, 3)
            pe.wait_ge(wp_dve, 1)
            pe.wait_ge(wp_act, 3)
            pre_transpose(0)
            pre_u(0)
            pre_z(0)
            pe.wait_ge(ld_att, 6 * 16)
            pe.wait_ge(ld_ffn, 8 * 16)
            pe.wait_ge(wp_dve, 3)
            pre_input(0)
            pe.wait_ge(inp_ok, 1)
            spread(0, 0)
            pe.wait_ge(sp_max, 2)
            pe.wait_ge(bc_cp, 1)
            pe.wait_ge(sp_abs, 2)
            for k in range(KD):
                nc.tensor.matmul(gb[:, 4, 0:D], bv_rep[:, k, :], w_o[:, k, :], start=(k == 0), stop=False)
            nc.tensor.matmul(gb[:, 4, 0:D], ones[0:1, :], bo_row, start=False, stop=True).then_inc(wp_pe, 1)
            for m in range(KD):
                for k in range(KD):
                    mm = nc.tensor.matmul(gb[:, 1, m * D:(m + 1) * D], w_v_t[:, k, m * P:(m + 1) * P],
                                          w_o[:, k, :], start=(k == 0 and m == 0), stop=(k == KD - 1),
                                          skip_group_check=True)
            mm.then_inc(wp_pe, 1)
            for m in range(KD):
                mm = nc.tensor.matmul(gb[:, 2, m * P:m * P + P], lora_a[:, m * P:(m + 1) * P], sel_a128,
                                      start=(m == 0), stop=True, skip_group_check=True)
            mm.then_inc(wp_pe, 1)
            pe.wait_ge(wa, 3)
            pe.wait_ge(wp_dve, 5)
            for h in range(2):
                mm = nc.tensor.matmul(gb[0:RANKL, h, :], sel_0, lora_b[:, h * T:(h + 1) * T],
                                      start=True, stop=True)
            mm.then_inc(wp_pe, 1)
            pe.wait_ge(wp_act, 6)
            for h in range(2):
                mm = nc.tensor.matmul(gb[0:RANKL, 4 + h, :], sel_d, lora_b[:, h * T:(h + 1) * T],
                                      start=True, stop=True)
            mm.then_inc(wp_pe, 2)

            for s in range(NCH + 2):
                g, r, f, p = s, s - 1, s - 2, s + 1

                def ahead(n):
                    if g < NCH and n + 1 < N:
                        spread(g, n + 1)
                    elif n + 1 == N and g + 1 < NCH:
                        spread(g + 1, 0)

                until = pacer(s, ahead)
                main, ffn = 0 <= r < NCH, 0 <= f
                score, p0, p1, end, total = timeline(s)
                if s == 0:
                    until(9)
                    pe.wait_ge(wp_act, 9)
                    pe.wait_ge(wp_dve, 8)
                    for t, part in ((9, pre_transpose), (12, pre_u), (15, pre_z), (26, pre_input)):
                        until(t)
                        part(p)
                if main:
                    y_transpose(r)
                    until(1)
                    if ffn:
                        feed_forward(f, 0)
                        until(4)
                        feed_forward(f, 1)
                    until(8.5)
                    xt_transpose(3 * r, x13(r))
                    until(9.5)
                    if ffn:
                        feed_forward(f, 2)
                    until(13)
                    inner_columns(r)
                    base(r)
                    until(18)
                    if ffn:
                        feed_forward(f, 3)
                    until(21)
                    up_transpose(r)
                    if ffn:
                        feed_forward(f, 4)
                    until(25)
                    up(r)
                    if p < NCH:
                        until(27)
                        pe.wait_ge(ln_r, r + 1)
                        pre_transpose(p)
                        until(30)
                        pre_u(p)
                        until(32)
                        pre_z(p)
                    until(36)
                    if p < NCH:
                        pe.wait_ge(bc_cp, p + 1)
                        pe.wait_ge(sp_abs, 2 * p + 2)
                        pe.wait_ge(sp_max, 2 * p + 2)
                    xt_transpose(3 * r + 1, x2)
                    if ffn:
                        feed_forward(f, 5)
                    until(40.5)
                    share_values(r)
                    for i in range(TT):
                        for kk in range(r % CPB + 1):
                            until(44 + 0.6 * (i * (r % CPB + 1) + kk))
                            score_block(r, i, kk)
                    until(score)
                    if ffn:
                        feed_forward(f, 6)
                    max_transpose(r)
                    for h, start in ((0, p0), (1, p1)):
                        if h == 0:
                            scores_t(r, 0, 0)
                        for i in range(n_p[r][h]):
                            until(start + 2.15 * i)
                            if i + 1 < n_p[r][h]:
                                scores_t(r, h, i + 1)
                            elif h == 0:
                                scores_t(r, 1, 0)
                            values(r, h, i)
                        if h == 0 and ffn:
                            feed_forward(f, 7)
                    until(end)
                    if ffn:
                        feed_forward(f, 8)
                    if p < NCH:
                        pre_input(p)
                    until(end + 4)
                    if ffn:
                        feed_forward(f, 9)
                    until(end + 8)
                    pe.wait_ge(o_res, TT * (r + 1))
                    xt_transpose(3 * r + 2, x13(r))
                    if p < NCH:
                        pe.wait_ge(inp_ok, p + 1)
                    low_rank(r)
                elif ffn:
                    for j in range(UNITS + 2):
                        feed_forward(f, j)
                until(1e9)

        @block.vector
        def _(dve):
            V = nc.vector

            def small(ins, s_, v):
                ins.then_inc(s_, 1)
                dve.wait_ge(s_, v)

            dve.wait_ge(consts, 3)
            dve.wait_ge(ld_pre, 9 * 16)
            small(V.memset(a_rep, 0.0), wd, 1)
            dve.wait_ge(wa, 1)
            for c0 in (0, 32):
                V.tensor_scalar(a_rep[:, :, c0:c0 + N], a_neg[:], -1.0, None, ALU.mult)
            V.tensor_scalar(a_neg[:], a_neg[:], -1.0, None, ALU.mult).then_inc(wd, 1)
            V.tensor_copy(sel[:], sel_cols[:]).then_inc(wd, 1)
            dve.wait_ge(wp_act, 1)
            V.tensor_tensor(w_in_l[:], w_in_r, w_in_h[:].bitcast(F32), ALU.subtract)
            dve.wait_ge(wp_act, 3)
            V.tensor_tensor(w_pre_l[:], gb[:, 1:3, 0:D + P], w_pre_h[:].bitcast(F32),
                            ALU.subtract).then_inc(wp_dve, 1)

            def pre_x(g):
                dve.wait_ge(xs_hi, g + 1)
                V.tensor_tensor(xs_l[:].rearrange("p k t -> p (k t)"),
                                gb[:, 0:2, :].rearrange("p k t -> p (k t)"),
                                xs_h[:].bitcast(F32).rearrange("p k t -> p (k t)"),
                                ALU.subtract).then_inc(xs_lo, 1)

            def pre_max(g):
                dve.wait_ge(z_ps, g + 1)
                dve.wait_ge(sp_abs, 2 * g + 2)
                for j in range(KD):
                    V.tensor_scalar(sp_m[:, j, :], gb[:, 1 + j, :], b_dt[:, j:j + 1], 0.0,
                                    ALU.add, ALU.max).then_inc(sp_max, 1)

            def pre_dt(g):
                dve.wait_ge(sp_ln, g + 1)
                dve.wait_ge(sp_max, 2 * g + 2)
                V.tensor_tensor(sp_a[:], sp_m[:], sp_a[:], ALU.add).then_inc(sp_sum, 1)
                dve.wait_ge(sp_sum, g + 1)
                if g >= 2:
                    dve.wait_ge(bar_ok, 2 * row(g - 1, 0))
                V.tensor_scalar(dt_sb[:, g % 2, :, :], sp_a[:], DT_MAX - DT_MIN, DT_MIN,
                                ALU.mult, ALU.add).then_inc(dt_ok, 1)
                dve.wait_ge(dt_ok, g + 1)
                dve.wait_ge(u_cp, 2 * g + 2)
                V.tensor_tensor(dtu[:], dt_sb[:, g % 2, :, :], u_sb[:], ALU.mult).then_inc(dtu_ok, 1)

            def pre_ux(g):
                dve.wait_ge(dtu_ok, g + 1)
                for j in range(KD):
                    V.scalar_tensor_tensor(out=u_sb[:, j, :], in0=u_sb[:, j, :], scalar=d_skip[:, j:j + 1],
                                           in1=xs_h[:, j, :].bitcast(F32), op0=ALU.mult,
                                           op1=ALU.add).then_inc(ux_h, 1)
                dve.wait_ge(ux_h, 2 * g + 2)
                V.tensor_tensor(u_sb[:], u_sb[:], xs_l[:].bitcast(F32), ALU.add).then_inc(ux_l, 1)

            def pre_low(g):
                dve.wait_ge(dtu_hi, g + 1)
                V.tensor_tensor(dtu_l[:], dtu[:], dtu_h[:].bitcast(F32), ALU.subtract).then_inc(dtu_lo, 1)

            def pre_input(g):
                dve.wait_ge(g_ps, g + 1)
                dve.wait_ge(bc_cp, g + 1)
                V.tensor_tensor(bc_sb[0:64, :], gb[0:64, 2, :], bc_sb[0:64, :], ALU.mult).then_inc(inp_ok, 1)
                dve.wait_ge(inp_ok, g + 1)
                if g >= 2:
                    dve.wait_ge(ir_ok, row(g - 1, 0))
                V.tensor_copy(parts[:, g % 2, :], bc_sb[0:64, :]).then_inc(inp_hi, 1)
                dve.wait_ge(inp_hi, g + 1)
                V.tensor_tensor(parts[32:64, g % 2, :], bc_sb[32:64, :],
                                parts[32:64, g % 2, :].bitcast(F32), ALU.subtract).then_inc(inp_lo, 1)

            def scan(g, n):
                k = row(g, n)
                dve.wait_ge(ir_ok, k + 1)
                if k >= 4:
                    dve.wait_ge(acc_ok, k - 3)
                if g % CPB:
                    dve.wait_ge(st_ok, kept(g - 1, n))
                for j in range(KD):
                    dve.wait_ge(bar_ok, 2 * k + j + 1)
                    V.tensor_tensor_scan(hst[:, k % 4, j, :], bar[:, k % 2, j, :], bi[:, k % 2, :],
                                         state[:, j, n:n + 1] if g % CPB else 0.0,
                                         ALU.mult, ALU.add).then_inc(scan_ok, 1)

            def keep_state(g, n):
                k = row(g, n)
                dve.wait_ge(scan_ok, 2 * k + 2)
                V.tensor_copy(state[:, :, n:n + 1], hst[:, k % 4, :, T - 1:T]).then_inc(st_ok, 1)

            def accumulate(g, n):
                k = row(g, n)
                dve.wait_ge(pr_ok, k + 1)
                if n == 0:
                    dve.wait_ge(ux_l, g + 1)
                    if g >= 1:
                        dve.wait_ge(y_t, g)
                else:
                    dve.wait_ge(acc_ok, k)
                V.tensor_tensor(acc[:], u_sb[:] if n == 0 else acc[:], hst[:, k % 4, :, :],
                                ALU.add).then_inc(acc_ok, 1)

            def stats(q, src):
                for t in range(TT):
                    V.bn_stats(bnst[:, t, :], src[:, t, :]).then_inc(ln_bn, 1)
                dve.wait_ge(ln_bn, TT * (q + 1))
                for t in range(TT):
                    V.bn_aggr(mv[:, t, :], bnst[:, t, :]).then_inc(ln_mv, 1)
                dve.wait_ge(ln_mv, TT * (q + 1))
                V.tensor_scalar(veps[:], mv[:, :, 1], EPS, None, ALU.add).then_inc(ln_ve, 1)

            def stats_last(g):
                dve.wait_ge(lf_r, 2 * g + 2)
                for t in range(TT):
                    V.bn_stats(bnst_f[:, t, :], x13(g)[:, t, :]).then_inc(lf_bn, 1)
                dve.wait_ge(lf_bn, TT * (g + 1))
                for t in range(TT):
                    V.bn_aggr(mv_f[:, t, :], bnst_f[:, t, :]).then_inc(lf_mv, 1)
                dve.wait_ge(lf_mv, TT * (g + 1))
                V.tensor_scalar(veps_f[:], mv_f[:, :, 1], EPS, None, ALU.add).then_inc(lf_ve, 1)

            def norm_bias_last(g):
                dve.wait_ge(lf_rstd, g + 1)
                V.scalar_tensor_tensor(out=nbias_f[:], in0=mv_f[:, :, 0], scalar=-1.0, in1=rstd_f[:],
                                       op0=ALU.mult, op1=ALU.mult).then_inc(lf_nb, 1)

            def norm_bias(q):
                dve.wait_ge(ln_rstd, q + 1)
                V.scalar_tensor_tensor(out=nbias[:], in0=mv[:, :, 0], scalar=-1.0, in1=rstd[:],
                                       op0=ALU.mult, op1=ALU.mult).then_inc(ln_nb, 1)

            def xt_low(i, low, high):
                dve.wait_ge(xt_hi, i + 1)
                V.tensor_tensor(low[:].rearrange("p k t -> p (k t)"),
                                gb[:, 0:2, :].rearrange("p k t -> p (k t)"),
                                high[:].bitcast(F32).rearrange("p k t -> p (k t)"),
                                ALU.subtract).then_inc(xt_lo, 1)

            def two_banks(b0):
                return gb[:, b0:b0 + 2, :].rearrange("p a (t d) -> p (a t) d", d=D)

            inner = gb[:, 2, 0:TT * (HR + E)].rearrange("p (t w) -> p t w", t=TT)

            def router(g):
                v = 11 * g
                dve.wait_ge(cat_ps, g + 1)
                small(V.tensor_tensor(lg[:], inner[:, :, HR:], r_bias[:], ALU.add), rt, v + 1)
                small(V.tensor_reduce(lmax[:], lg[:], AX.X, ALU.max), rt, v + 2)
                V.tensor_tensor(ls[:], lg[:], lmax[:].unsqueeze(2).to_broadcast([P, TT, E]),
                                ALU.subtract).then_inc(lg_ok, 1)
                of_j = lg[:].unsqueeze(2).to_broadcast([P, TT, E, E])
                of_i = lg[:].unsqueeze(3).to_broadcast([P, TT, E, E])
                V.tensor_tensor(rk_gt[:], of_j, of_i, ALU.is_gt).then_inc(rt, 1)
                small(V.tensor_tensor(rk_eq[:], of_j, of_i, ALU.is_equal), rt, v + 4)
                small(V.tensor_tensor(rk_eq[:].rearrange("p t i j -> p t (i j)"),
                                      rk_eq[:].rearrange("p t i j -> p t (i j)"),
                                      tie[:].rearrange("p i j -> p (i j)").unsqueeze(1).to_broadcast([P, TT, E * E]),
                                      ALU.mult), rt, v + 5)
                small(V.tensor_tensor(rk_gt[:], rk_gt[:], rk_eq[:], ALU.add), rt, v + 6)
                small(V.tensor_reduce(rank[:], rk_gt[:], AX.X, ALU.add), rt, v + 7)
                dve.wait_ge(ex_ok, g + 1)
                small(V.scalar_tensor_tensor(out=em[:], in0=rank[:], scalar=1.5, in1=ex[:],
                                             op0=ALU.is_lt, op1=ALU.mult), rt, v + 8)
                V.tensor_reduce(e_sum[:], ex[:], AX.X, ALU.add)
                small(V.tensor_reduce(k_sum[:], em[:], AX.X, ALU.add), rt, v + 9)
                small(V.scalar_tensor_tensor(out=e_sum[:], in0=e_sum[:], scalar=1e-6, in1=k_sum[:],
                                             op0=ALU.mult, op1=ALU.add), rt, v + 10)
                small(V.reciprocal(k_sum[:], e_sum[:]), rt, v + 11)
                dve.wait_ge(consts, 12)
                V.tensor_tensor(gate[:, :, 0:E], em[:], k_sum[:].unsqueeze(2).to_broadcast([P, TT, E]),
                                ALU.mult).then_inc(lgate, 1)
                dve.wait_ge(lgate, g + 1)
                V.tensor_tensor(hw[:, :, 0:HR].rearrange("p t (e r) -> p t e r", r=R),
                                inner[:, :, 0:HR].rearrange("p t (e r) -> p t e r", r=R),
                                gate[:].unsqueeze(3).to_broadcast([P, TT, EP, R]), ALU.mult).then_inc(hw_ok, 1)

            def keys(g):
                c = g % CPB
                dve.wait_ge(q_hi, g + 1)
                dve.wait_ge(k_hi, g + 1)
                V.scalar_tensor_tensor(out=q_st[64:96, :], in0=gb[64:96, 2, :], scalar=b_sh[64:96, :],
                                       in1=q_st[64:96, :].bitcast(F32), op0=ALU.add,
                                       op1=ALU.subtract).then_inc(q_lo, 1)
                ks = k_st[32:64, c * T:(c + 1) * T]
                V.scalar_tensor_tensor(out=ks, in0=gb[32:64, 2, :], scalar=b_sh[32:64, :],
                                       in1=ks.bitcast(F32), op0=ALU.add, op1=ALU.subtract).then_inc(k_lo, 1)

            def block_max(g, i, kk):
                c = g % CPB
                j = i * (c + 1) + kk
                dve.wait_ge(s_ps, s_base[g] + j + 1)
                w = T if kk < c else (i + 1) * P
                V.tensor_reduce(smax[:, i, kk:kk + 1], gb[:, j % 3, 0:w], AX.X, ALU.max).then_inc(s_mx, 1)

            def maxima(g):
                c = g % CPB
                dve.wait_ge(s_mx, s_base[g] + n_s[g])
                small(V.tensor_reduce(m4[:], smax[:, :, 0:c + 1], AX.X, ALU.max), m_ok, g + 1)
                small(V.tensor_scalar(mhl[:, :, 0], m4[:], -1.0, None, ALU.mult), mhl_ok, 2 * g + 1)
                V.scalar_tensor_tensor(out=mhl[:, :, 1], in0=m4[:], scalar=-1.0, in1=mhl[:, :, 0].bitcast(F32),
                                       op0=ALU.mult, op1=ALU.subtract).then_inc(mhl_ok, 1)

            def finish_attention(g, h):
                dve.wait_ge(pv_ok, p_base[g][h] + n_p[g][h])
                dve.wait_ge(x2b_ok, g + 1)
                V.reciprocal(rl[:, 2 * h:2 * h + 2].unsqueeze(2), gb[:, 0:2, D:D + 1]).then_inc(rl_ok, 1)
                dve.wait_ge(rl_ok, 2 * g + h + 1)
                for ql in range(2):
                    i = 2 * h + ql
                    V.scalar_tensor_tensor(out=x2[:, i, :], in0=gb[:, ql, 0:D], scalar=rl[:, i:i + 1],
                                           in1=x2[:, i, :], op0=ALU.mult, op1=ALU.add).then_inc(o_res, 1)

            def mix(g, j):
                if not 1 <= j <= UNITS:
                    return
                k = g * UNITS + j - 1
                dve.wait_ge(a1_ok, k + 1)
                dve.wait_ge(a0_ok, k + 1)
                if k >= 2:
                    dve.wait_ge(mid_used, k - 1)
                V.scalar_tensor_tensor(out=mid[:, k % 2, :], in0=aring[:, 2 * k % 3, :], scalar=sgn01[:, 0:1],
                                       in1=aring[:, (2 * k + 1) % 3, :], op0=ALU.mult,
                                       op1=ALU.add).then_inc(mid_ok, 1)

            def residual_last(g, half):
                dve.wait_ge(mid_used, UNITS * g + 4 * (half + 1))
                x = x13(g)[:, 2 * half:2 * half + 2, :].rearrange("p t d -> p (t d)")
                V.scalar_tensor_tensor(out=x, in0=gb[:, 5, :], scalar=sgn[:, 1:2], in1=x,
                                       op0=ALU.mult, op1=ALU.add).then_inc(lf_r, 1)

            pre_x(0)
            dve.wait_ge(wd, 2)
            dve.wait_ge(wp_act, 4)
            V.tensor_tensor(a_l[:], a_rep, a_h[:].bitcast(F32), ALU.subtract).then_inc(wp_dve, 1)
            pre_max(0)
            pre_dt(0)
            pre_ux(0)
            pre_low(0)
            dve.wait_ge(ld_att, 6 * 16)
            dve.wait_ge(ld_ffn, 8 * 16)
            V.tensor_copy(bv_rep, bv_col[:].unsqueeze(2).to_broadcast([P, KD, P]))
            V.memset(sel_a128, 0.0)
            V.memset(sel_0, 0.0)
            V.tensor_scalar(sgn[:], top_v[:], 0.0, None, ALU.is_ge)
            small(V.tensor_copy(top_f[:], top_i[:]), wd, 4)
            V.tensor_scalar(sgn[:], sgn[:], 2.0, -1.0, ALU.mult, ALU.add)
            small(V.tensor_scalar(picked[:], top_f[:], expert_of[:, 0:1], None, ALU.is_equal), wd, 5)
            V.tensor_tensor(absv[:], top_v[:], sgn[:], ALU.mult)
            V.tensor_tensor(sgn01[:], sgn[:, 0:1], sgn[:, 1:2], ALU.mult)
            small(V.tensor_scalar(minus0[:], picked[:, 0:1], -1.0, None, ALU.mult), wd, 6)
            for q in range(3):
                c0 = 32 * q
                V.tensor_scalar(sel_a128[:, c0:c0 + R], pick_cols[:], picked[:, 0:1], None, ALU.mult)
                V.tensor_scalar(sel_a128[:, c0 + R:c0 + 2 * R], pick_cols[:], picked[:, 1:2], None, ALU.mult)
                V.tensor_scalar(sel_0[:, c0:c0 + R], pick_cols[:], picked[:, 0:1], None, ALU.mult)
                V.tensor_scalar(sel_d[:, c0:c0 + R], pick_cols[:], minus0[:, 0:1], None, ALU.mult)
                ins = V.tensor_scalar(sel_d[:, c0 + R:c0 + 2 * R], pick_cols[:], picked[:, 1:2], None, ALU.mult)
            ins.then_inc(wp_dve, 1)
            pre_input(0)
            V.memset(q_st[96:128, :].bitcast(F32), 0.0)
            V.memset(k_st[96:128, :].bitcast(F32), 0.0).then_inc(wd, 1)
            dve.wait_ge(wd, 7)
            V.memset(k_st[96:98, :].bitcast(F32), 1.0)
            dve.wait_ge(wa, 2)
            V.tensor_tensor(w_cat_l[:], w_cat_r, w_cat_h[:].bitcast(F32), ALU.subtract)
            dve.wait_ge(wp_act, 5)
            V.tensor_tensor(w_up_l[:], w_up_r, w_up_h[:].bitcast(F32), ALU.subtract).then_inc(wp_dve, 1)
            dve.wait_ge(wa, 3)
            V.tensor_tensor(w_vo_l[:], gb[:, 1, :].rearrange("p (k n) -> p k n", k=KD),
                            w_vo_h[:].bitcast(F32), ALU.subtract).then_inc(wp_dve, 1)
            dve.wait_ge(wa, 4)
            V.tensor_tensor(w_sh_l[:], w_sh_r, w_sh_h[:].bitcast(F32), ALU.subtract)
            dve.wait_ge(wa, 5)
            V.tensor_tensor(w_i_l[:], w_i_r, w_i_h[:].bitcast(F32), ALU.subtract)
            dve.wait_ge(wp_act, 7)
            V.tensor_tensor(w_la_l[:], gb[:, 2, 0:2 * P].rearrange("p (k n) -> p k n", k=KD),
                            w_la_h[:].bitcast(F32), ALU.subtract).then_inc(wp_dve, 1)
            dve.wait_ge(wp_act, 8)
            V.tensor_tensor(w_z0[32:64, :], gb[32:64, 0:2, :].rearrange("p k t -> p (k t)"),
                            w_z0[32:64, :].bitcast(F32), ALU.subtract).then_inc(wp_dve, 1)
            dve.wait_ge(wp_act, 9)
            V.tensor_tensor(w_zd[32:64, :], gb[32:64, 4:6, :].rearrange("p k t -> p (k t)"),
                            w_zd[32:64, :].bitcast(F32), ALU.subtract).then_inc(wp_dve, 1)

            for s in range(NCH + 2):
                g, r, f, p = s, s - 1, s - 2, s + 1

                def state_row(n):
                    if g < NCH:
                        scan(g, n)
                        if n >= 2:
                            accumulate(g, n - 2)
                        if g % CPB != CPB - 1:
                            keep_state(g, n)

                until = pacer(s, state_row)
                main, ffn = 0 <= r < NCH, 0 <= f
                score, p0, p1, end, total = timeline(s)
                if s == 0:
                    for t, part in ((11, pre_x), (18, pre_max), (22, pre_dt), (25, pre_ux), (26, pre_low),
                                    (30, pre_input)):
                        until(t)
                        part(p)
                if main:
                    dve.wait_ge(y_t, r + 1)
                    stats(3 * r, two_banks(0))
                    until(4)
                    if ffn:
                        mix(f, 1)
                    norm_bias(3 * r)
                    until(10.5)
                    xt_low(3 * r, xt_l, xt_h)
                    until(13)
                    if ffn:
                        mix(f, 2)
                    until(15.5)
                    router(r)
                    until(20)
                    if ffn:
                        mix(f, 3)
                    until(22.5)
                    dve.wait_ge(hwt_ps, r + 1)
                    dve.wait_ge(hw_hi, r + 1)
                    V.tensor_tensor(hw_l, gb[0:HR + 1, 2, :], hw_h.bitcast(F32), ALU.subtract).then_inc(hw_lo, 1)
                    if ffn:
                        mix(f, 4)
                    until(26)
                    dve.wait_ge(up_ps, r + 1)
                    V.tensor_tensor(x13(r), two_banks(0), x13(r), ALU.add).then_inc(ln_r, 1)
                    dve.wait_ge(ln_r, r + 1)
                    stats(3 * r + 1, x13(r))
                    if p < NCH:
                        until(29)
                        pre_x(p)
                    until(31)
                    norm_bias(3 * r + 1)
                    if p < NCH:
                        until(35)
                        pre_max(p)
                    until(38)
                    xt_low(3 * r + 1, xt_l, xt_h)
                    if ffn:
                        mix(f, 5)
                        residual_last(f, 0)
                    if p < NCH:
                        pre_dt(p)
                        until(42)
                        pre_ux(p)
                    until(43)
                    keys(r)
                    for i in range(TT):
                        for kk in range(r % CPB + 1):
                            until(44 + 0.6 * (i * (r % CPB + 1) + kk))
                            block_max(r, i, kk)
                    maxima(r)
                    if p < NCH:
                        pre_low(p)
                    until(p0)
                    if ffn:
                        mix(f, 6)
                    until(p1)
                    finish_attention(r, 0)
                    if ffn:
                        until(p1 + 2)
                        mix(f, 7)
                    until(end)
                    finish_attention(r, 1)
                    dve.wait_ge(o_res, TT * (r + 1))
                    stats(3 * r + 2, x2)
                    if ffn:
                        mix(f, 8)
                    until(end + 3)
                    if p < NCH:
                        pre_input(p)
                    norm_bias(3 * r + 2)
                    if ffn:
                        until(end + 6)
                        residual_last(f, 1)
                        stats_last(f)
                    until(end + 10)
                    xt_low(3 * r + 2, xf_l, xf_h)
                    until(total)
                    dve.wait_ge(l_hi, r + 1)
                    V.tensor_tensor(lr[64:96, :], gb[64:96, 2, :], lr[64:96, :].bitcast(F32),
                                    ALU.subtract).then_inc(l_lo, 1)
                elif ffn:
                    for j in range(UNITS + 1):
                        mix(f, j)
                        if j == 5:
                            residual_last(f, 0)
                    residual_last(f, 1)
                    stats_last(f)
                until(1e9)
                if g < NCH:
                    accumulate(g, N - 2)
                    accumulate(g, N - 1)
                if ffn:
                    norm_bias_last(f)


def _layout(i):
    import numpy as np

    f = {k: np.ascontiguousarray(v) for k, v in i.items() if np.asarray(v).size}

    def pad(w, at, width):
        out = np.zeros((w.shape[0], width), w.dtype)
        for c in at:
            out[:, c:c + w.shape[1]] = w
        return out

    def by_partition(v):
        return np.ascontiguousarray(v.reshape(KD, P, -1).transpose(1, 0, 2)).reshape(P, KD, -1)

    w_x = f["L0_attn_w_x"]
    idx = np.arange(P)
    eye = np.eye(R, dtype=np.float32)
    sel = np.zeros((64, N), np.float32)
    for n in range(N):
        sel[[n, 32 + n], n] = 1
    w_bc = pad(w_x[:, 64:80], (0, 32), P)
    w_bc[:, 64:80] = w_x[:, 80:96]
    sh = f["L1_attn_b_share"]
    b_sh = np.zeros((P, 1), sh.dtype)
    for c in (0, 32, 64):
        b_sh[c:c + 16, 0] = sh
    return {
        "x": f["L0_attn_x"],
        "w_in": f["L0_attn_w_in"], "w_in_t": f["L0_attn_w_in"].T,
        "w_xdt_t": w_x[:, :64].T, "w_dt": f["L0_attn_w_dt"], "w_bc": w_bc,
        "b_dt": by_partition(f["L0_attn_b_dt"])[:, :, 0], "d_skip": by_partition(f["L0_attn_Dp"])[:, :, 0],
        "a_log": by_partition(f["L0_attn_A_log"]), "sel_cols": sel,
        "w_cat": np.concatenate([f["L0_ffn_base_W"].T, f["L0_ffn_routed_A"].reshape(E * R, D).T,
                                 f["L0_ffn_shared_A"].T, f["L0_ffn_router_W"].T], 1),
        "w_up": np.concatenate([f["L0_ffn_routed_B"].transpose(0, 2, 1).reshape(E * R, D),
                                f["L0_ffn_shared_B"].T, f["L0_ffn_base_b"][None]], 0),
        "r_bias": np.broadcast_to(f["L0_ffn_router_b"], (P, TT, E)),
        "tie": np.broadcast_to(np.tril(np.ones((E, E), np.float32), -1), (P, E, E)),
        "w_sh": pad(f["L1_attn_W_share"], (0, 32, 64), P), "b_sh": b_sh,
        "w_v_t": f["L1_attn_Wv"].T, "w_o": f["L1_attn_Wo"],
        "bv": by_partition(f["L1_attn_bv"])[:, :, 0], "bo": f["L1_attn_bo"][None],
        "w_i_t": f["L1_ffn_wi_w"].T, "w_out_t": f["L1_ffn_wo_w"].T,
        "lora_a": f["L1_ffn_lora_As"].reshape(P, D),
        "lora_b": f["L1_ffn_lora_Bs"].transpose(0, 2, 1).reshape(P, FF),
        "pick_cols": eye[idx % R], "expert_of": (idx // R).astype(np.float32)[:, None],
        "top_i": np.broadcast_to(f["L1_ffn_top_k_indices"], (P, 2)),
        "top_v": np.broadcast_to(f["L1_ffn_top_k_values"], (P, 2)),
    }


def kernel(**inputs):
    import numpy as np
    import concourse.bacc as bacc
    from concourse.bass_utils import run_bass_kernel_spmd

    nc = bacc.Bacc("TRN2", target_bir_lowering=False, num_devices=1)
    arrays, args = {}, {}
    for name, v in _layout(inputs).items():
        v = np.ascontiguousarray(v)
        arrays[f"in_{name}"] = v
        args[name] = nc.dram_tensor(f"in_{name}", v.shape, mybir.dt.from_np(v.dtype), kind="ExternalInput").ap()
    args["out"] = nc.dram_tensor("out_x", (B, S, D), F32, kind="ExternalOutput").ap()
    args["c_rows"] = nc.dram_tensor("c_rows", (2, N, T), F32, kind="Internal").ap()
    program(nc, args)
    return run_bass_kernel_spmd(nc, [arrays], core_ids=[0]).results[0]["out_x"]
```

```python
from contextlib import ExitStack

import concourse.bass as bass
from concourse import mybir

F32 = mybir.dt.float32
F32R = mybir.dt.float32r
BF16 = mybir.dt.bfloat16
I32 = mybir.dt.int32
ALU = mybir.AluOpType
ACT = mybir.ActivationFunctionType
AX = mybir.AxisListType

P = 128
B, S, D = 2, 2048, 256
KD = D // P
T = 512
TT = T // P
CPB = S // T
NCH = B * CPB
N = 16
E, R = 6, 16
EP = E + 1
HR = EP * R
CAT = D + HR + E
FF = 1024
FB = FF // P
DT_MIN, DT_MAX = 0.001, 0.1
EPS = 1e-5
SCALE = 0.25
NEG = -1e38
RANKL = 96


def program(nc, a):
    with ExitStack() as ctx:
        def sb(name, shape, dt=F32):
            return ctx.enter_context(nc.sbuf_tensor(name, shape, dt))

        def sem(name):
            return ctx.enter_context(nc.semaphore(name))

        ident = sb("ident", [P, P])
        ident_bf = sb("ident_bf", [P, P], BF16)
        mask_bf = sb("mask_bf", [P, P], BF16)
        mask_t_bf = sb("mask_t_bf", [P, P], BF16)
        ones = sb("ones", [P, P])
        sel_cols = sb("sel_cols", [64, N])
        sel = sb("sel", [64, N], F32R)
        w_in_h = sb("w_in_h", [P, KD, D], F32R)
        w_in_l = sb("w_in_l", [P, KD, D], F32R)
        w_pre_h = sb("w_pre_h", [P, KD, D + P], F32R)
        w_pre_l = sb("w_pre_l", [P, KD, D + P], F32R)
        b_dt = sb("b_dt", [P, KD])
        d_skip = sb("d_skip", [P, KD])
        a_neg = sb("a_neg", [P, KD, N])
        a_h = sb("a_h", [P, KD, P], F32R)
        a_l = sb("a_l", [P, KD, P], F32R)
        w_cat_h = sb("w_cat_h", [P, KD, CAT], F32R)
        w_cat_l = sb("w_cat_l", [P, KD, CAT], F32R)
        w_up_h = sb("w_up_h", [HR + 1, D], F32R)
        w_up_l = sb("w_up_l", [HR + 1, D], F32R)
        r_bias = sb("r_bias", [P, TT, E])
        tie = sb("tie", [P, E, E])
        w_sh_h = sb("w_sh_h", [P, KD, P], F32R)
        w_sh_l = sb("w_sh_l", [P, KD, P], F32R)
        b_sh = sb("b_sh", [P, 1])
        w_vo_h = sb("w_vo_h", [P, KD, D], F32R)
        w_vo_l = sb("w_vo_l", [P, KD, D], F32R)
        bv_col = sb("bv_col", [P, KD])
        att_bias = sb("att_bias", [P, D])
        pick_cols = sb("pick_cols", [P, R])
        expert_of = sb("expert_of", [P, 1])
        top_i = sb("top_i", [P, 2], I32)
        top_f = sb("top_f", [P, 2])
        top_v = sb("top_v", [P, 2])
        picked = sb("picked", [P, 2])
        minus0 = sb("minus0", [P, 1])
        sgn = sb("sgn", [P, 2])
        absv = sb("absv", [P, 2])
        sgn01 = sb("sgn01", [P, 1])
        w_la_h = sb("w_la_h", [P, KD, P], F32R)
        w_la_l = sb("w_la_l", [P, KD, P], F32R)
        w_z0 = sb("w_z0", [RANKL, FF], F32R)
        w_zd = sb("w_zd", [RANKL, FF], F32R)
        w_i_h = sb("w_i_h", [P, KD, FF], F32R)
        w_i_l = sb("w_i_l", [P, KD, FF], F32R)
        w_out = sb("w_out", [P, FB, D])
        xs_h = sb("xs_h", [P, KD, T], F32R)
        xs_l = sb("xs_l", [P, KD, T], F32R)
        u_sb = sb("u_sb", [P, KD, T])
        dt_sb = sb("dt_sb", [P, 2, KD, T])
        sp_a = sb("sp_a", [P, KD, T])
        dtu = sp_a
        bc_sb = sb("bc_sb", [P, T])
        parts = sb("parts", [64, 2, T], F32R)
        bar = sb("bar", [P, 2, KD, T])
        hst = sb("hst", [P, 4, KD, T])
        c_rep = sb("c_rep", [P, 3, T])
        state = sb("state", [P, KD, N])
        acc = sb("acc", [P, KD, T])
        bnst = sb("bnst", [P, TT, 6])
        mv = sb("mv", [P, TT, 2])
        veps = sb("veps", [P, TT])
        rstd = sb("rstd", [P, TT])
        nmean = sb("nmean", [P, TT])
        nbias = sb("nbias", [P, TT])
        bnst_f = sb("bnst_f", [P, TT, 6])
        mv_f = sb("mv_f", [P, TT, 2])
        veps_f = sb("veps_f", [P, TT])
        rstd_f = sb("rstd_f", [P, TT])
        nmean_f = sb("nmean_f", [P, TT])
        nbias_f = sb("nbias_f", [P, TT])
        mhalf = sb("mhalf", [P, TT])
        rows_tm = sb("rows_tm", [P, 3, TT, D])
        xt_h = sb("xt_h", [P, KD, T], F32R)
        xt_l = sb("xt_l", [P, KD, T], F32R)
        xf_h = sb("xf_h", [P, KD, T], F32R)
        xf_l = sb("xf_l", [P, KD, T], F32R)
        lg = sb("lg", [P, TT, E])
        lmax = sb("lmax", [P, TT])
        ls = sb("ls", [P, TT, E])
        ex = sb("ex", [P, TT, E])
        rk_gt = sb("rk_gt", [P, TT, E, E])
        rk_eq = sb("rk_eq", [P, TT, E, E])
        rank = sb("rank", [P, TT, E])
        em = sb("em", [P, TT, E])
        e_sum = sb("e_sum", [P, TT])
        k_sum = sb("k_sum", [P, TT])
        gate = sb("gate", [P, TT, EP])
        hw = sb("hw", [P, TT, HR + 1])
        q_st = sb("q_st", [P, T], F32R)
        k_st = sb("k_st", [P, S], F32R)
        vc = sb("vc", [P, S // P, D + 1])
        smax = sb("smax", [P, TT, CPB])
        m4 = sb("m4", [P, TT])
        mhl = sb("mhl", [P, TT, 2], F32R)
        rl = sb("rl", [P, TT])
        lr = sb("lr", [RANKL, T], F32R)
        mid = sb("mid", [P, 2, T])
        aring = sb("aring", [P, 3, T])
        pring = sb("pring", [P, 2, T])
        sp_m = sb("sp_m", [P, KD, T])
        x_pre = sp_m
        x2 = rows_tm[:, 2, :, :]

        def x13(g):
            return rows_tm[:, g % 2, :, :]

        dtu_h, dtu_l = xs_h, xs_l
        hw_h, hw_l = xt_h[0:HR + 1, 0, :], xt_h[0:HR + 1, 1, :]

        vflat = vc[:, :, :].rearrange("p a b -> p (a b)")
        w_i_r = vflat[:, 0:KD * FF].rearrange("p (k f) -> p k f", k=KD)
        w_cat_r = vflat[:, KD * FF:KD * FF + KD * CAT].rearrange("p (k f) -> p k f", k=KD)
        lora_b = vflat[:, KD * (FF + CAT):KD * (FF + CAT) + FF]
        xflat = rows_tm[:, :, :, :].rearrange("p a t d -> p (a t d)")

        def cut(flat, at, blocks, width):
            return flat[:, at:at + blocks * width].rearrange("p (k n) -> p k n", k=blocks)

        w_in_r, w_in_t = cut(xflat, 0, KD, D), cut(xflat, KD * D, KD, D)
        dt_bc_r = cut(xflat, 2 * KD * D, KD, D + P)
        w_sh_r = cut(xflat, 3 * KD * D + KD * P, KD, P)
        w_v_t, w_o = cut(xflat, 4 * KD * D, KD, D), cut(xflat, 5 * KD * D, KD, D)
        mflat = aring[:, :, :].rearrange("p a t -> p (a t)")
        lora_a = mflat[:, 0:D]
        w_up_r = mflat[0:HR + 1, D:2 * D]
        bv_rep = cut(mflat, 4 * D, KD, P)
        a_rep = cut(mflat, 5 * D, KD, P)
        prflat = pring[:, :, :].rearrange("p a t -> p (a t)")
        bo_row = prflat[0:1, 0:D]
        sel_a128 = prflat[:, D:D + P]
        sel_0, sel_d = prflat[:, 2 * D:2 * D + RANKL], prflat[:, 2 * D + P:2 * D + P + RANKL]
        w_xdt_t, w_dt = mflat[0:64, 2 * D:3 * D], mflat[0:64, 3 * D:4 * D]

        bi = ctx.enter_context(nc.psum_tensor("bi", [P, 2, T], F32))
        gb = ctx.enter_context(nc.psum_tensor("gb", [P, 6, T], F32))

        ld_x = sem("ld_x")
        c_kept = sem("c_kept")
        c_in = [sem(f"c_in{i}") for i in range(3)]
        ld_pre, ld_cat, ld_att, ld_ffn = sem("ld_pre"), sem("ld_cat"), sem("ld_att"), sem("ld_ffn")
        consts = sem("consts")
        pc_ready = sem("pc_ready")
        wp_pe, wp_act, wp_dve = sem("wp_pe"), sem("wp_act"), sem("wp_dve")
        wd = sem("wd")
        wa = sem("wa")
        w_hi, w_lo = sem("w_hi"), sem("w_lo")
        xs_hi, xs_lo = sem("xs_hi"), sem("xs_lo")
        u_ps, z_ps, bc_ps, g_ps = sem("u_ps"), sem("z_ps"), sem("bc_ps"), sem("g_ps")
        u_cp, bc_cp = sem("u_cp"), sem("bc_cp")
        sp_abs, sp_exp, sp_ln = sem("sp_abs"), sem("sp_exp"), sem("sp_ln")
        sp_max, sp_sum, dt_ok = sem("sp_max"), sem("sp_sum"), sem("dt_ok")
        dtu_ok, dtu_hi, dtu_lo = sem("dtu_ok"), sem("dtu_hi"), sem("dtu_lo")
        inp_ok, inp_hi, inp_lo = sem("inp_ok"), sem("inp_hi"), sem("inp_lo")
        bar_ok = sem("bar_ok")
        ir_ok = sem("ir_ok")
        ux_h, ux_l = sem("ux_h"), sem("ux_l")
        scan_ok = sem("scan_ok")
        st_ok = sem("st_ok")
        pr_ok = sem("pr_ok")
        pair_ok = sem("pair_ok")
        acc_ok = sem("acc_ok")
        y_t = sem("y_t")
        ln_r, ln_bn, ln_mv, ln_ve = sem("ln_r"), sem("ln_bn"), sem("ln_mv"), sem("ln_ve")
        ln_rstd, ln_nb, ln_x = sem("ln_rstd"), sem("ln_nb"), sem("ln_x")
        lf_r, lf_bn, lf_mv, lf_ve = sem("lf_r"), sem("lf_bn"), sem("lf_mv"), sem("lf_ve")
        lf_rstd, lf_nb, lf_x = sem("lf_rstd"), sem("lf_nb"), sem("lf_x")
        xt_ps, xt_hi, xt_lo = sem("xt_ps"), sem("xt_hi"), sem("xt_lo")
        lgate = sem("lgate")
        base_ps = sem("base_ps")
        cat_ps, lg_ok, rt, ex_ok, hw_ok = sem("cat_ps"), sem("lg_ok"), sem("rt"), sem("ex_ok"), sem("hw_ok")
        hwt_ps, hw_hi, hw_lo, up_ps = sem("hwt_ps"), sem("hw_hi"), sem("hw_lo"), sem("up_ps")
        sh_ps, q_hi, k_hi, q_lo, k_lo = sem("sh_ps"), sem("q_hi"), sem("k_hi"), sem("q_lo"), sem("k_lo")
        v_ps, v_ok, x2b_ok = sem("v_ps"), sem("v_ok"), sem("x2b_ok")
        s_ps, s_mx = sem("s_ps"), sem("s_mx")
        m_ok, mhl_ok, mt_ps, mt_ok = sem("m_ok"), sem("mhl_ok"), sem("mt_ps"), sem("mt_ok")
        st_ps, p_ok, pv_ok = sem("st_ps"), sem("p_ok"), sem("pv_ok")
        rl_ok, o_res = sem("rl_ok"), sem("o_res")
        l_ps, l_hi, l_lo = sem("l_ps"), sem("l_hi"), sem("l_lo")
        z0_ps, zd_ps, a0_ok, a1_ok, mid_ok, mid_used = (
            sem("z0_ps"), sem("zd_ps"), sem("a0_ok"), sem("a1_ok"), sem("mid_ok"), sem("mid_used"))
        stored = sem("stored")

        n_s = [TT * (g % CPB + 1) for g in range(NCH)]
        n_p = [[(4 * (g % CPB) + 2 * h + 2) // 2 for h in range(2)] for g in range(NCH)]
        s_base = [sum(n_s[:g]) for g in range(NCH)]
        p_base = [[sum(sum(x) for x in n_p[:g]) + (n_p[g][0] if h else 0) for h in range(2)] for g in range(NCH)]

        def row(g, n):
            return g * N + n

        def kept(g, n):
            return (g - g // CPB) * N + n + 1

        UNITS = 8

        def at(c, first, last):
            return first + (last - first) * c / (CPB - 1)

        def pacer(rows, emit_row, units=(), emit_unit=None):
            items = sorted([(n, 0, n) for n in range(rows)] + [(u, 1, j) for j, u in enumerate(units)])
            assert [j for _, kind, j in items if kind] == list(range(len(units)))
            done = [0]

            def until(t, upto=0):
                while done[0] < len(items) and (items[done[0]][0] <= t or any(
                        kind and j < upto for _, kind, j in items[done[0]:])):
                    _, kind, j = items[done[0]]
                    (emit_unit if kind else emit_row)(j)
                    done[0] += 1
            return until

        block = ctx.enter_context(nc.Block())

        @block.sync
        def _(sp):
            def rows(w):
                return w.rearrange("(k p) n -> p k n", p=P)

            for dst, src in ((w_xdt_t, a["w_xdt_t"]), (w_dt, a["w_dt"]),
                             (w_in_t, rows(a["w_in_t"])), (w_in_r, rows(a["w_in"])),
                             (dt_bc_r[:, :, D:D + P], rows(a["w_bc"])), (b_dt[:], a["b_dt"]),
                             (d_skip[:], a["d_skip"]), (a_neg[:], a["a_log"]), (sel_cols[:], a["sel_cols"])):
                sp.dma_start(dst, src).then_inc(ld_pre, 16)
            for dst, src in ((w_cat_r, rows(a["w_cat"])), (w_up_r, a["w_up"]),
                             (r_bias[:], a["r_bias"]), (tie[:], a["tie"])):
                sp.dma_start(dst, src).then_inc(ld_cat, 16)
            for dst, src in ((w_sh_r, rows(a["w_sh"])), (b_sh[:], a["b_sh"]), (w_v_t, rows(a["w_v_t"])),
                             (w_o, rows(a["w_o"])), (bv_col[:], a["bv"]), (bo_row, a["bo"])):
                sp.dma_start(dst, src).then_inc(ld_att, 16)
            for dst, src in ((w_i_r, rows(a["w_i_t"])), (lora_a, a["lora_a"]), (lora_b, a["lora_b"]),
                             (pick_cols[:], a["pick_cols"]), (expert_of[:], a["expert_of"]),
                             (top_i[:], a["top_i"]), (top_v[:], a["top_v"]), (w_out[:], rows(a["w_out_t"]))):
                sp.dma_start(dst, src).then_inc(ld_ffn, 16)
            for k in range(NCH * N):
                g, n = divmod(k, N)
                if n == 0:
                    sp.wait_ge(bc_cp, g + 1)
                    sp.dma_start(a["c_rows"][g % 2], bc_sb[64:64 + N, :]).then_inc(c_kept, 16)
                    sp.wait_ge(c_kept, 16 * (g + 1))
                if k >= 3:
                    sp.wait_ge(pr_ok, k - 2)
                sp.dma_start(c_rep[:, k % 3, :], a["c_rows"][g % 2, n, :].partition_broadcast(P)
                             ).then_inc(c_in[k % 3], 16)

        @block.gpsimd
        def _(pool):
            pool.memset(ident[:], 0.0).then_inc(consts, 1)
            pool.memset(ones[:], 1.0).then_inc(consts, 1)
            pool.wait_ge(consts, 2)
            pool.affine_select(out=ident[:], in_=ident[:], compare_op=ALU.not_equal, fill=1.0, base=0,
                               pattern=[[-1, P]], channel_multiplier=1).then_inc(consts, 1)
            pool.memset(ident_bf[:], 0.0).then_inc(consts, 1)
            pool.memset(mask_bf[:], 0.0).then_inc(consts, 1)
            pool.memset(mask_t_bf[:], 0.0).then_inc(consts, 1)
            pool.memset(mhalf[:], -0.5).then_inc(consts, 1)
            pool.memset(gate[:], 1.0).then_inc(consts, 1)
            pool.memset(hw[:], 1.0).then_inc(consts, 1)
            pool.wait_ge(consts, 9)
            pool.affine_select(out=ident_bf[:], in_=ident_bf[:], compare_op=ALU.not_equal, fill=1.0, base=0,
                               pattern=[[-1, P]], channel_multiplier=1).then_inc(consts, 1)
            pool.affine_select(out=mask_bf[:], in_=mask_bf[:], compare_op=ALU.is_ge, fill=NEG, base=0,
                               pattern=[[-1, P]], channel_multiplier=1).then_inc(consts, 1)
            pool.affine_select(out=mask_t_bf[:], in_=mask_t_bf[:], compare_op=ALU.is_ge, fill=NEG, base=0,
                               pattern=[[1, P]], channel_multiplier=-1).then_inc(consts, 1)

            pool.wait_ge(consts, 12)
            pool.memset(q_st[96:128, :].bitcast(F32), 0.0).then_inc(consts, 1)
            pool.wait_ge(consts, 13)
            pool.memset(k_st[96:128, :].bitcast(F32), 0.0).then_inc(consts, 1)
            pool.wait_ge(consts, 14)
            pool.memset(k_st[96:98, :].bitcast(F32), 1.0).then_inc(consts, 1)
            pool.wait_ge(consts, 15)
            for i, (low, raw, high) in enumerate(((w_cat_l, w_cat_r, w_cat_h), (w_up_l, w_up_r, w_up_h),
                                                  (w_sh_l, w_sh_r, w_sh_h), (w_i_l, w_i_r, w_i_h))):
                pool.wait_ge(w_hi, i + 1)
                if i:
                    pool.wait_ge(w_lo, i)
                pool.tensor_tensor(low[:], raw, high[:].bitcast(F32), ALU.subtract).then_inc(w_lo, 1)

            pool.wait_ge(w_lo, 4)

            def product(g, n):
                k = row(g, n)
                if g % CPB != CPB - 1:
                    pool.wait_ge(st_ok, kept(g, n))
                else:
                    pool.wait_ge(scan_ok, 2 * k + 2)
                pool.wait_ge(c_in[k % 3], 16 * (k // 3 + 1))
                h = hst[:, k % 4, :, :]
                pool.tensor_tensor(h, h, c_rep[:, k % 3, :].unsqueeze(1).to_broadcast([P, KD, T]),
                                   ALU.mult).then_inc(pr_ok, 1)
                if n % 2:
                    pool.wait_ge(pr_ok, k + 1)
                    pool.tensor_tensor(h, hst[:, (k - 1) % 4, :, :], h, ALU.add).then_inc(pair_ok, 1)

            def pre_ux(g):
                pool.wait_ge(ux_h, 2 * g + 2)
                pool.tensor_tensor(u_sb[:], u_sb[:], xs_l[:].bitcast(F32), ALU.add).then_inc(ux_l, 1)

            def pre_low(g):
                pool.wait_ge(dtu_hi, g + 1)
                pool.tensor_tensor(dtu_l[:], dtu[:], dtu_h[:].bitcast(F32), ALU.subtract).then_inc(dtu_lo, 1)

            def norm_power(q):
                pool.wait_ge(ln_ve, q + 1)
                pool.tensor_tensor(rstd[:], veps[:], mhalf[:], ALU.pow).then_inc(ln_rstd, 1)
                pool.wait_ge(ln_rstd, q + 1)
                pool.tensor_tensor(nbias[:], nmean[:], rstd[:], ALU.mult).then_inc(ln_nb, 1)

            def norm_power_last(g):
                pool.wait_ge(lf_ve, g + 1)
                pool.tensor_tensor(rstd_f[:], veps_f[:], mhalf[:], ALU.pow).then_inc(lf_rstd, 1)
                pool.wait_ge(lf_rstd, g + 1)
                pool.tensor_tensor(nbias_f[:], nmean_f[:], rstd_f[:], ALU.mult).then_inc(lf_nb, 1)

            for s in range(NCH + 2):
                r, f, c = s - 1, s - 2, (s - 1) % CPB
                main, ffn = 0 <= r < NCH, 0 <= f
                until = pacer(N if s < NCH else 0, lambda n: product(s, n),
                              [at(c, 14.79, 15.34)] if ffn else [], lambda j: norm_power_last(f))
                if s == 0:
                    until(10)
                    pool.wait_ge(wp_pe, 8)
                    pool.memset(vc[:, :, D:D + 1], 1.0).then_inc(pc_ready, 1)
                if main:
                    until(at(c, 0.11, 0.03))
                    norm_power(3 * r)
                    until(at(c, 6.29, 5.37))
                    norm_power(3 * r + 1)
                    until(at(c, 8.54, 7.35))
                    pool.wait_ge(xt_ps, KD * (3 * r + 2))
                    pool.wait_ge(wp_act, 5)
                    pool.tensor_tensor(x2, x2, att_bias[:].unsqueeze(1).to_broadcast([P, TT, D]),
                                       ALU.add).then_inc(x2b_ok, 1)
                    if s + 1 < NCH:
                        until(at(c, 9.96, 8.17))
                        pre_ux(s + 1)
                        until(at(c, 9.85, 8.87))
                        pre_low(s + 1)
                    until(at(c, 12.88, 13.15))
                    norm_power(3 * r + 2)
                until(1e9)

        @block.scalar
        def _(act):
            def copy(out, in_):
                return nc.scalar.activation(out, in_, ACT.Copy)

            act.wait_ge(ld_pre, 9 * 16)
            nc.scalar.activation(a_neg[:], a_neg[:], ACT.Exp).then_inc(wa, 1)
            copy(w_in_h[:], w_in_r).then_inc(wp_act, 1)
            act.wait_ge(wp_pe, 1)
            copy(dt_bc_r[:, :, 0:D], gb[:, 0, :].rearrange("p (k n) -> p k n", k=KD)).then_inc(wp_act, 1)
            act.wait_ge(wp_pe, 2)
            copy(w_pre_h[:], gb[:, 1:3, 0:D + P]).then_inc(wp_act, 1)
            act.wait_ge(wd, 2)
            copy(a_h[:], a_rep).then_inc(wp_act, 1)

            def load_x(g):
                b, c = divmod(g, CPB)
                if g >= 1:
                    act.wait_ge(sp_sum, g)
                act.dma_start(x_pre[:], a["x"][b, :, c * T:(c + 1) * T].rearrange("(k p) t -> p k t", p=P)
                              ).then_inc(ld_x, 16)

            def store(g):
                b, c = divmod(g, CPB)
                act.wait_ge(lf_x, TT * (g + 1))
                act.dma_start(a["out"][b, c * T:(c + 1) * T, :].rearrange("(t p) d -> p t d", p=P),
                              x13(g)).then_inc(stored, 16)

            def pre_x(g):
                act.wait_ge(ld_x, 16 * (g + 1))
                if g >= 1:
                    act.wait_ge(g_ps, g)
                copy(xs_h[:], x_pre[:]).then_inc(xs_hi, 1)

            def pre_u(g):
                act.wait_ge(u_ps, g + 1)
                if g >= 1:
                    act.wait_ge(acc_ok, row(g - 1, 0) // 2 + 1)
                copy(u_sb[:, 0, :], gb[:, 2, :]).then_inc(u_cp, 1)
                copy(u_sb[:, 1, :], gb[:, 0, :]).then_inc(u_cp, 1)

            def pre_z(g):
                if g >= 1:
                    act.wait_ge(dtu_lo, g)
                act.wait_ge(z_ps, g + 1)
                for j in range(KD):
                    nc.scalar.activation(sp_a[:, j, :], gb[:, 1 + j, :], ACT.Abs,
                                         bias=b_dt[:, j:j + 1]).then_inc(sp_abs, 1)
                act.wait_ge(bc_ps, g + 1)
                if g >= 1:
                    act.wait_ge(inp_lo, g)
                    act.wait_ge(c_kept, 16 * g)
                copy(bc_sb[:], gb[:, 0, :]).then_inc(bc_cp, 1)

            def pre_softplus(g):
                act.wait_ge(sp_abs, 2 * g + 2)
                nc.scalar.activation(sp_a[:], sp_a[:], ACT.Exp, scale=-1.0).then_inc(sp_exp, 1)
                act.wait_ge(sp_exp, g + 1)
                nc.scalar.activation(sp_a[:], sp_a[:], ACT.Ln, bias=ones[:, 0:1]).then_inc(sp_ln, 1)

            def pre_dtu(g):
                act.wait_ge(dtu_ok, g + 1)
                act.wait_ge(bc_ps, g + 1)
                act.wait_ge(ux_l, g + 1)
                copy(dtu_h[:], dtu[:]).then_inc(dtu_hi, 1)

            def decay(g, n):
                k = row(g, n)
                act.wait_ge(dt_ok, g + 1)
                if k >= 2:
                    act.wait_ge(scan_ok, 2 * (k - 2) + 2)
                for j in range(KD):
                    nc.scalar.activation(bar[:, k % 2, j, :], dt_sb[:, g % 2, j, :], ACT.Exp,
                                         scale=a_neg[:, j, n:n + 1]).then_inc(bar_ok, 1)

            def normalize(q, out, src):
                act.wait_ge(ln_nb, q + 1)
                if q % 3 == 0 and q >= 6:
                    act.wait_ge(stored, 16 * (q // 3 - 1))
                for t in range(TT):
                    nc.scalar.activation(out[:, t, :], src[:, t, :], ACT.Identity, scale=rstd[:, t:t + 1],
                                         bias=nbias[:, t:t + 1]).then_inc(ln_x, 1)

            def normalize_last(g):
                act.wait_ge(lf_nb, g + 1)
                for t in range(TT):
                    nc.scalar.activation(x13(g)[:, t, :], x13(g)[:, t, :], ACT.Identity,
                                         scale=rstd_f[:, t:t + 1], bias=nbias_f[:, t:t + 1]).then_inc(lf_x, 1)

            def xt_high(i, out):
                for k in range(KD):
                    act.wait_ge(xt_ps, KD * i + k + 1)
                    copy(out[:, k, :], gb[:, k, :]).then_inc(xt_hi, 1)

            def keys(g):
                b, c = divmod(g, CPB)
                act.wait_ge(sh_ps, g + 1)
                nc.scalar.activation(q_st[0:96, :], gb[0:96, 2, :], ACT.Identity,
                                     bias=b_sh[0:96, :]).then_inc(q_hi, 1)
                nc.scalar.activation(k_st[0:96, c * T:(c + 1) * T], gb[0:96, 2, :], ACT.Identity,
                                     bias=b_sh[0:96, :]).then_inc(k_hi, 1)
                act.wait_ge(v_ps, g + 1)
                act.wait_ge(pc_ready, 1)
                for h in range(2):
                    copy(vc[:, 4 * c + 2 * h:4 * c + 2 * h + 2, 0:D],
                         gb[:, h, :].rearrange("p (t d) -> p t d", t=2)).then_inc(v_ok, 1)

            def max_rows(g):
                act.wait_ge(mt_ps, g + 1)
                copy(q_st[96:98, :], gb[0:2, 2, :]).then_inc(mt_ok, 1)

            def exp_pair(g, h, i):
                k = p_base[g][h] + i
                act.wait_ge(st_ps, k + 1)
                if k >= 2:
                    act.wait_ge(pv_ok, k - 1)
                nc.scalar.activation(pring[:, k % 2, :], gb[:, 2, :], ACT.Exp, scale=SCALE).then_inc(p_ok, 1)

            def relus(g, j):
                if j < UNITS:
                    k = g * UNITS + j
                    if k >= 2:
                        act.wait_ge(mid_ok, k - 1)
                    act.wait_ge(z0_ps, k + 1)
                    nc.scalar.activation(aring[:, 2 * k % 3, :], gb[:, 3 + k % 2, :], ACT.Relu,
                                         scale=absv[:, 0:1]).then_inc(a0_ok, 1)
                if 1 <= j <= UNITS:
                    k = g * UNITS + j - 1
                    if k >= 1:
                        act.wait_ge(mid_ok, k)
                    act.wait_ge(zd_ps, k + 1)
                    nc.scalar.activation(aring[:, (2 * k + 1) % 3, :], gb[:, 3 + k % 2, :], ACT.Relu,
                                         scale=absv[:, 1:2]).then_inc(a1_ok, 1)

            load_x(0)
            act.wait_ge(ld_cat, 4 * 16)
            copy(w_cat_h[:], w_cat_r).then_inc(w_hi, 1)
            copy(w_up_h[:], w_up_r).then_inc(w_hi, 1)
            act.wait_ge(ld_att, 6 * 16)
            copy(w_sh_h[:], w_sh_r).then_inc(w_hi, 1)
            pre_x(0)
            act.wait_ge(ld_ffn, 8 * 16)
            copy(w_i_h[:], w_i_r).then_inc(w_hi, 1)
            pre_u(0)
            pre_z(0)
            pre_softplus(0)
            pre_dtu(0)
            decay(0, 0)
            decay(0, 1)

            def later_weights(i):
                if i == 0:
                    act.wait_ge(wp_pe, 3)
                    copy(att_bias[:], gb[:, 4, 0:D]).then_inc(wp_act, 1)
                elif i == 1:
                    act.wait_ge(wp_pe, 4)
                    copy(w_vo_h[:], gb[:, 1, :].rearrange("p (k n) -> p k n", k=KD)).then_inc(wa, 1)
                elif i == 2:
                    act.wait_ge(wp_pe, 5)
                    copy(w_la_h[:], gb[:, 2, 0:2 * P].rearrange("p (k n) -> p k n", k=KD)).then_inc(wp_act, 1)
                elif i == 3:
                    act.wait_ge(wp_pe, 6)
                    copy(w_z0[:], gb[0:RANKL, 0:2, :].rearrange("p k t -> p (k t)")).then_inc(wp_act, 1)
                else:
                    act.wait_ge(wp_pe, 7)
                    copy(w_zd[:], gb[0:RANKL, 4:6, :].rearrange("p k t -> p (k t)")).then_inc(wp_act, 1)

            for s in range(NCH + 2):
                g, r, f, p = s, s - 1, s - 2, s + 1

                def ahead(n):
                    if g < NCH and n + 1 < N and (g or n):
                        decay(g, n + 1)
                    elif n + 1 == N and g + 1 < NCH:
                        decay(g + 1, 0)

                def unit(j):
                    if j <= UNITS:
                        relus(f, j)
                    else:
                        normalize_last(f)
                        store(f)

                main, ffn, c = 0 <= r < NCH, 0 <= f, r % CPB
                until = pacer(N, ahead, [
                    at(c, 0.2, 0.2), at(c, 0.8, 1.33), at(c, 3.1, 3.33), at(c, 4.17, 4.02), at(c, 5.47, 4.82),
                    at(c, 9.97, 7.9), at(c, 10.45, 9.62), at(c, 12.42, 11.66), at(c, 12.98, 13.6), at(c, 16.35, 16.35),
                ] if ffn else [], unit)
                if p < NCH:
                    load_x(p)
                if s == 0:
                    for i in range(5):
                        until(0.6 * i)
                        later_weights(i)
                    for t, part in ((4, pre_x), (5.6, pre_u), (6.8, pre_z), (6.74, pre_softplus), (9.6, pre_dtu)):
                        until(t)
                        part(p)
                if main:
                    until(at(c, 1.7, 2.33))
                    normalize(3 * r, x13(r), gb[:, 0:2, :].rearrange("p a (t d) -> p (a t) d", d=D))
                    until(at(c, 2.5, 2.93))
                    xt_high(3 * r, xt_h)
                    until(at(c, 4.07, 3.82))
                    act.wait_ge(lg_ok, r + 1)
                    nc.scalar.activation(ex[:], ls[:], ACT.Exp).then_inc(ex_ok, 1)
                    until(at(c, 5.37, 4.72))
                    act.wait_ge(hwt_ps, r + 1)
                    copy(hw_h, gb[0:HR + 1, 2, :]).then_inc(hw_hi, 1)
                    if p < NCH:
                        until(at(c, 7.07, 5.98))
                        pre_x(p)
                        until(at(c, 8.07, 6.6))
                        pre_u(p)
                    until(at(c, 8.18, 5.51))
                    normalize(3 * r + 1, x2, x13(r))
                    if p < NCH:
                        until(at(c, 9.56, 7.78))
                        pre_z(p)
                        pre_softplus(p)
                    until(at(c, 9.67, 7.19))
                    xt_high(3 * r + 1, xt_h)
                    until(at(c, 10.06, 8.29))
                    keys(r)
                    if p < NCH:
                        until(at(c, 10.36, 8.84))
                        pre_dtu(p)
                    until(at(c, 11.34, 9.76))
                    max_rows(r)
                    for h, start, stop in ((0, at(c, 10.44, 9.61), at(c, 12.15, 10.49)),
                                           (1, at(c, 12.35, 11.5), at(c, 12.8, 13.45))):
                        for i in range(n_p[r][h]):
                            until(start + (stop - start) * i / n_p[r][h])
                            exp_pair(r, h, i)
                    until(at(c, 14.82, 14.35))
                    normalize(3 * r + 2, x13(r), x2)
                    until(at(c, 14.61, 15.2), UNITS + 1)
                    xt_high(3 * r + 2, xf_h)
                    until(at(c, 16.2, 15.46))
                    act.wait_ge(l_ps, r + 1)
                    copy(lr[:], gb[0:RANKL, 2, :]).then_inc(l_hi, 1)
                until(1e9)
            act.wait_ge(stored, 16 * NCH)

        @block.tensor
        def _(pe):
            def mm3(out, lh, ll, rh, rl_, start, stop, skip=False):
                nc.tensor.matmul(out, lh, rh, start=start, stop=False, skip_group_check=skip)
                nc.tensor.matmul(out, ll, rh, start=False, stop=False, skip_group_check=skip)
                return nc.tensor.matmul(out, lh, rl_, start=False, stop=stop, skip_group_check=skip)

            pe.wait_ge(ld_pre, 9 * 16)
            for k in range(KD):
                mm = nc.tensor.matmul(gb[:, 0, k * D:(k + 1) * D], w_xdt_t[:, k * P:(k + 1) * P], w_dt,
                                      start=(k == 0), stop=True, skip_group_check=True)
            mm.then_inc(wp_pe, 1)
            pe.wait_ge(wp_act, 2)
            for m in range(KD):
                for k in range(KD):
                    mm = nc.tensor.matmul(gb[:, 1 + m, 0:D + P], w_in_t[:, k, m * P:(m + 1) * P],
                                          dt_bc_r[:, k, :], start=(k == 0), stop=(k == KD - 1))
            mm.then_inc(wp_pe, 1)

            def project(out, w_h, w_l, cols):
                for k in range(KD):
                    mm = mm3(out, w_h[:, k, cols], w_l[:, k, cols], xs_h[:, k, :], xs_l[:, k, :],
                             k == 0, k == KD - 1)
                return mm

            def pre_u(g):
                pe.wait_ge(xs_hi, g + 1)
                pe.wait_ge(xs_lo, g + 1)
                project(gb[:, 2, :], w_in_h, w_in_l, slice(0, P))
                project(gb[:, 0, :], w_in_h, w_in_l, slice(P, D)).then_inc(u_ps, 1)

            def pre_z(g):
                pe.wait_ge(u_cp, 2 * g + 1)
                project(gb[:, 1, :], w_pre_h, w_pre_l, slice(0, P))
                project(gb[:, 2, :], w_pre_h, w_pre_l, slice(P, D)).then_inc(z_ps, 1)
                pe.wait_ge(u_cp, 2 * g + 2)
                project(gb[:, 0, :], w_pre_h, w_pre_l, slice(D, D + P)).then_inc(bc_ps, 1)

            def pre_input(g):
                pe.wait_ge(dtu_hi, g + 1)
                pe.wait_ge(dtu_lo, g + 1)
                for k in range(KD):
                    mm = mm3(gb[:, 2, :], a_h[:, k, :], a_l[:, k, :], dtu_h[:, k, :], dtu_l[:, k, :],
                             k == 0, k == KD - 1)
                mm.then_inc(g_ps, 1)

            def spread(g, n):
                k = row(g, n)
                if n == 0:
                    pe.wait_ge(inp_lo, g + 1)
                if k >= 2:
                    pe.wait_ge(scan_ok, 2 * (k - 2) + 2)
                nc.tensor.matmul(bi[:, k % 2, :], sel[:, n:n + 1].to_broadcast([64, P]), parts[:, g % 2, :],
                                 start=True, stop=True).then_inc(ir_ok, 1)

            def xt_transpose(i, src):
                pe.wait_ge(ln_x, TT * (i + 1))
                for k in range(KD):
                    for t in range(TT):
                        mm = nc.tensor.transpose(gb[:, k, t * P:(t + 1) * P],
                                                 src[:, t, k * P:(k + 1) * P], ident[:])
                    mm.then_inc(xt_ps, 1)

            def y_transpose(g):
                pe.wait_ge(acc_ok, row(g, N) // 2)
                for t in range(TT):
                    for k in range(KD):
                        mm = nc.tensor.transpose(gb[:, t // 2, (t % 2) * D + k * P:(t % 2) * D + (k + 1) * P],
                                                 acc[:, k, t * P:(t + 1) * P], ident[:])
                mm.then_inc(y_t, 1)

            def inner_columns(g):
                w = HR + E
                pe.wait_ge(xt_hi, KD * (3 * g + 1))
                pe.wait_ge(xt_lo, KD * (3 * g + 1))
                for t in range(TT):
                    ts = slice(t * P, (t + 1) * P)
                    for k in range(KD):
                        mm = mm3(gb[:, 2, t * w:(t + 1) * w], xt_h[:, k, ts], xt_l[:, k, ts],
                                 w_cat_h[:, k, D:], w_cat_l[:, k, D:], k == 0 and t == 0, k == KD - 1, True)
                mm.then_inc(cat_ps, 1)

            def two_tiles(t):
                return gb[:, t // 2, (t % 2) * D:(t % 2 + 1) * D]

            def base(g):
                for t in range(TT):
                    ts = slice(t * P, (t + 1) * P)
                    for k in range(KD):
                        mm = mm3(two_tiles(t), xt_h[:, k, ts], xt_l[:, k, ts], w_cat_h[:, k, 0:D],
                                 w_cat_l[:, k, 0:D], k == 0 and t % 2 == 0, False, True)
                mm.then_inc(base_ps, 1)

            def up_transpose(g):
                pe.wait_ge(hw_ok, g + 1)
                for t in range(TT):
                    mm = nc.tensor.transpose(gb[0:HR + 1, 2, t * P:(t + 1) * P], hw[:, t, :], ident[:])
                mm.then_inc(hwt_ps, 1)

            def up(g):
                pe.wait_ge(hw_hi, g + 1)
                pe.wait_ge(hw_lo, g + 1)
                for t in range(TT):
                    ts = slice(t * P, (t + 1) * P)
                    mm = mm3(two_tiles(t), hw_h[:, ts], hw_l[:, ts], w_up_h[:], w_up_l[:], False, True, True)
                mm.then_inc(up_ps, 1)

            def share_values(g):
                pe.wait_ge(xt_hi, KD * (3 * g + 2))
                pe.wait_ge(xt_lo, KD * (3 * g + 2))
                for k in range(KD):
                    mm = mm3(gb[:, 2, :], w_sh_h[:, k, :], w_sh_l[:, k, :], xt_h[:, k, :], xt_l[:, k, :],
                             k == 0, k == KD - 1)
                mm.then_inc(sh_ps, 1)
                for t in range(TT):
                    for k in range(KD):
                        ts = slice(t * P, (t + 1) * P)
                        mm = mm3(two_tiles(t), xt_h[:, k, ts], xt_l[:, k, ts],
                                 w_vo_h[:, k, :], w_vo_l[:, k, :], k == 0 and t % 2 == 0, k == KD - 1, True)
                mm.then_inc(v_ps, 1)

            def score_block(g, i, kk):
                c = g % CPB
                j = i * (c + 1) + kk
                if j == 0:
                    pe.wait_ge(q_lo, g + 1)
                    pe.wait_ge(k_lo, g + 1)
                    pe.wait_ge(v_ok, 2 * g + 2)
                if j >= 3:
                    pe.wait_ge(s_mx, s_base[g] + j - 2)
                w = T if kk < c else (i + 1) * P
                mm = nc.tensor.matmul(gb[:, j % 3, 0:w], q_st[0:96, i * P:(i + 1) * P],
                                      k_st[0:96, kk * T:kk * T + w], start=True, stop=True)
                if kk == c:
                    mm = nc.tensor.matmul(gb[:, j % 3, w - P:w], ident_bf[:], mask_bf[:],
                                          start=False, stop=True, skip_group_check=True)
                mm.then_inc(s_ps, 1)

            def max_transpose(g):
                pe.wait_ge(mhl_ok, 2 * g + 2)
                for i in range(TT):
                    mm = nc.tensor.transpose(gb[0:2, 2, i * P:(i + 1) * P], mhl[:, i, :].bitcast(F32), ident[:])
                mm.then_inc(mt_ps, 1)

            def scores_t(g, h, i):
                k = p_base[g][h] + i
                pe.wait_ge(mt_ok, g + 1)
                if k >= 1:
                    pe.wait_ge(p_ok, k)
                last = i == n_p[g][h] - 1
                for e in range(2):
                    kt = 2 * i + e
                    mm = nc.tensor.matmul(gb[:, 2, e * D:(e + 1) * D], k_st[:, kt * P:(kt + 1) * P],
                                          q_st[:, 2 * h * P:(2 * h + 2) * P], start=(e == 0),
                                          stop=True, skip_group_check=True)
                    if last:
                        mm = nc.tensor.matmul(gb[:, 2, e * D + e * P:e * D + (e + 1) * P],
                                              ident_bf[:], mask_t_bf[:], start=False, stop=True,
                                              skip_group_check=True)
                mm.then_inc(st_ps, 1)

            def values(g, h, i):
                k = p_base[g][h] + i
                pe.wait_ge(p_ok, k + 1)
                if h == 1 and i == 0:
                    pe.wait_ge(o_res, TT * g + 2)
                last = i == n_p[g][h] - 1
                for e in range(2):
                    kt = 2 * i + e
                    for ql in range(2):
                        if last and e == 1 and ql == 0:
                            continue
                        mm = nc.tensor.matmul(gb[:, ql, 0:D + 1],
                                              pring[:, k % 2, e * D + ql * P:e * D + (ql + 1) * P],
                                              vc[:, kt, :], start=(kt == 0),
                                              stop=last and (e == 1 or ql == 0))
                mm.then_inc(pv_ok, 1)

            def low_rank(g):
                pe.wait_ge(xt_hi, KD * (3 * g + 3))
                pe.wait_ge(xt_lo, KD * (3 * g + 3))
                for k in range(KD):
                    mm = mm3(gb[:, 2, :], w_la_h[:, k, :], w_la_l[:, k, :], xf_h[:, k, :], xf_l[:, k, :],
                             k == 0, k == KD - 1)
                mm.then_inc(l_ps, 1)

            def feed_forward(g, j):
                def blocks(u):
                    k = g * UNITS + u
                    half, pair = divmod(u, UNITS // 2)
                    return k, slice(half * D, (half + 1) * D), [2 * pair, 2 * pair + 1], gb[:, 3 + k % 2, :]

                if j < UNITS:
                    k, ts, ms, bank = blocks(j)
                    if k >= 2:
                        pe.wait_ge(a1_ok, k - 1)
                    if j == 0:
                        pe.wait_ge(l_hi, g + 1)
                        pe.wait_ge(l_lo, g + 1)
                    for e, m in enumerate(ms):
                        cols, out = slice(m * P, (m + 1) * P), bank[:, e * D:(e + 1) * D]
                        for kk in range(KD):
                            mm3(out, w_i_h[:, kk, cols], w_i_l[:, kk, cols], xf_h[:, kk, ts], xf_l[:, kk, ts],
                                kk == 0 and e == 0, False, True)
                        mm = nc.tensor.matmul(out, w_z0[:, cols], lr[:, ts], start=False, stop=True,
                                              skip_group_check=True)
                    mm.then_inc(z0_ps, 1)
                if 1 <= j <= UNITS:
                    k, ts, ms, bank = blocks(j - 1)
                    pe.wait_ge(a0_ok, k + 1)
                    for e, m in enumerate(ms):
                        mm = nc.tensor.matmul(bank[:, e * D:(e + 1) * D], w_zd[:, m * P:(m + 1) * P], lr[:, ts],
                                              start=False, stop=True, skip_group_check=True)
                    mm.then_inc(zd_ps, 1)
                if j >= 2:
                    k, ts, ms, bank = blocks(j - 2)
                    pe.wait_ge(mid_ok, k + 1)
                    if (j - 2) % 4 == 0 and k > 0:
                        pe.wait_ge(lf_r, 2 * g + (j - 2) // 4)
                    for e, m in enumerate(ms):
                        for t in range(2):
                            mm = nc.tensor.matmul(gb[:, 5, t * D:(t + 1) * D],
                                                  mid[:, k % 2, e * D + t * P:e * D + (t + 1) * P],
                                                  w_out[:, m, :], start=(ms[0] == 0 and e == 0 and t == 0),
                                                  stop=(ms[1] == FB - 1 and e == 1), skip_group_check=True)
                    mm.then_inc(mid_used, 1)

            pe.wait_ge(consts, 3)
            pe.wait_ge(wp_dve, 1)
            pe.wait_ge(wp_act, 3)
            pre_u(0)
            pre_z(0)
            pe.wait_ge(ld_att, 6 * 16)
            pe.wait_ge(ld_ffn, 8 * 16)
            pre_input(0)
            pe.wait_ge(inp_ok, 1)
            spread(0, 0)

            def later_weights(i):
                if i == 0:
                    pe.wait_ge(wp_dve, 3)
                    pe.wait_ge(sp_max, 2)
                    pe.wait_ge(bc_cp, 1)
                    pe.wait_ge(sp_abs, 2)
                    for k in range(KD):
                        nc.tensor.matmul(gb[:, 4, 0:D], bv_rep[:, k, :], w_o[:, k, :], start=(k == 0), stop=False)
                    nc.tensor.matmul(gb[:, 4, 0:D], ones[0:1, :], bo_row, start=False, stop=True
                                     ).then_inc(wp_pe, 1)
                elif i == 1:
                    for m in range(KD):
                        for k in range(KD):
                            mm = nc.tensor.matmul(gb[:, 1, m * D:(m + 1) * D], w_v_t[:, k, m * P:(m + 1) * P],
                                                  w_o[:, k, :], start=(k == 0 and m == 0), stop=(k == KD - 1),
                                                  skip_group_check=True)
                    mm.then_inc(wp_pe, 1)
                elif i == 2:
                    for m in range(KD):
                        mm = nc.tensor.matmul(gb[:, 2, m * P:m * P + P], lora_a[:, m * P:(m + 1) * P], sel_a128,
                                              start=(m == 0), stop=True, skip_group_check=True)
                    mm.then_inc(wp_pe, 1)
                elif i == 3:
                    pe.wait_ge(wa, 2)
                    pe.wait_ge(wp_dve, 4)
                    for h in range(2):
                        mm = nc.tensor.matmul(gb[0:RANKL, h, :], sel_0, lora_b[:, h * T:(h + 1) * T],
                                              start=True, stop=True)
                    mm.then_inc(wp_pe, 1)
                else:
                    pe.wait_ge(wp_act, 5)
                    for h in range(2):
                        mm = nc.tensor.matmul(gb[0:RANKL, 4 + h, :], sel_d, lora_b[:, h * T:(h + 1) * T],
                                              start=True, stop=True)
                    mm.then_inc(wp_pe, 2)

            for s in range(NCH + 2):
                g, r, f, p = s, s - 1, s - 2, s + 1

                def ahead(n):
                    if g < NCH and n + 1 < N:
                        spread(g, n + 1)
                    elif n + 1 == N and g + 1 < NCH:
                        spread(g + 1, 0)

                main, ffn, c = 0 <= r < NCH, 0 <= f, r % CPB
                until = pacer(N, ahead, [
                    at(c, 0.44, 0.44), at(c, 1.31, 0.94), at(c, 2.3, 1.73), at(c, 4.21, 3.36), at(c, 5.69, 4.18),
                    at(c, 9.85, 7.07), at(c, 10.63, 9.94), at(c, 12.87, 11.51), at(c, 13.74, 13.37), at(c, 14.23, 14.02),
                ] if ffn else [], lambda j: feed_forward(f, j))
                if s == 0:
                    for i in range(5):
                        until(0.6 * i)
                        later_weights(i)
                    until(3.6)
                    pe.wait_ge(wp_act, 8)
                    pe.wait_ge(wp_dve, 7)
                    pe.wait_ge(w_lo, 4)
                    for t, part in ((4.8, pre_u), (6, pre_z), (12.07, pre_input)):
                        until(t)
                        part(p)
                if main:
                    until(at(c, 1.61, 1.27))
                    y_transpose(r)
                    until(at(c, 2.64, 2.17))
                    xt_transpose(3 * r, x13(r))
                    until(at(c, 3.74, 3.11))
                    inner_columns(r)
                    base(r)
                    until(at(c, 5.21, 4.08))
                    up_transpose(r)
                    until(at(c, 5.96, 4.23))
                    up(r)
                    if p < NCH:
                        until(at(c, 6.57, 5.14))
                        pe.wait_ge(ln_r, r + 1)
                        until(at(c, 7.1, 5.6))
                        pre_u(p)
                        until(at(c, 8.86, 6.81))
                        pre_z(p)
                    until(at(c, 9.87, 7.1))
                    if p < NCH:
                        pe.wait_ge(bc_cp, p + 1)
                        pe.wait_ge(sp_abs, 2 * p + 2)
                        pe.wait_ge(sp_max, 2 * p + 2)
                    xt_transpose(3 * r + 1, x2)
                    until(at(c, 10.26, 8.22))
                    share_values(r)
                    for i in range(TT):
                        for kk in range(c + 1):
                            until(at(c, 10.48, 8.49) + at(c, 0.05, 0.83) * (i * (c + 1) + kk) / n_s[r])
                            score_block(r, i, kk)
                    until(at(c, 10.73, 9.95))
                    max_transpose(r)
                    for h, start, stop in ((0, at(c, 12.93, 9.95), at(c, 12.77, 10.6)),
                                           (1, at(c, 13.18, 11.53), at(c, 12.68, 13.31))):
                        if h == 0:
                            scores_t(r, 0, 0)
                        for i in range(n_p[r][h]):
                            until(start + (stop - start) * i / n_p[r][h])
                            if i + 1 < n_p[r][h]:
                                scores_t(r, h, i + 1)
                            elif h == 0:
                                scores_t(r, 1, 0)
                            values(r, h, i)
                    if p < NCH:
                        until(at(c, 13.7, 13.47))
                        pre_input(p)
                    until(at(c, 14.36, 14.4))
                    pe.wait_ge(o_res, TT * (r + 1))
                    xt_transpose(3 * r + 2, x13(r))
                    if p < NCH:
                        pe.wait_ge(inp_ok, p + 1)
                    until(at(c, 15.4, 15.27))
                    low_rank(r)
                until(1e9)

        @block.vector
        def _(dve):
            V = nc.vector

            def small(ins, s_, v):
                ins.then_inc(s_, 1)
                dve.wait_ge(s_, v)

            dve.wait_ge(consts, 3)
            dve.wait_ge(ld_pre, 9 * 16)
            small(V.memset(a_rep, 0.0), wd, 1)
            dve.wait_ge(wa, 1)
            for c0 in (0, 32):
                V.tensor_scalar(a_rep[:, :, c0:c0 + N], a_neg[:], -1.0, None, ALU.mult)
            V.tensor_scalar(a_neg[:], a_neg[:], -1.0, None, ALU.mult).then_inc(wd, 1)
            V.tensor_copy(sel[:], sel_cols[:]).then_inc(wd, 1)
            dve.wait_ge(wp_act, 1)
            V.tensor_tensor(w_in_l[:], w_in_r, w_in_h[:].bitcast(F32), ALU.subtract)
            dve.wait_ge(wp_act, 3)
            V.tensor_tensor(w_pre_l[:], gb[:, 1:3, 0:D + P], w_pre_h[:].bitcast(F32),
                            ALU.subtract).then_inc(wp_dve, 1)

            def pre_x(g):
                dve.wait_ge(xs_hi, g + 1)
                V.tensor_tensor(xs_l[:], x_pre[:], xs_h[:].bitcast(F32), ALU.subtract).then_inc(xs_lo, 1)

            def pre_max(g):
                dve.wait_ge(z_ps, g + 1)
                dve.wait_ge(sp_abs, 2 * g + 2)
                for j in range(KD):
                    V.tensor_scalar(sp_m[:, j, :], gb[:, 1 + j, :], b_dt[:, j:j + 1], 0.0,
                                    ALU.add, ALU.max).then_inc(sp_max, 1)

            def pre_dt(g):
                dve.wait_ge(sp_ln, g + 1)
                dve.wait_ge(sp_max, 2 * g + 2)
                V.tensor_tensor(sp_a[:], sp_m[:], sp_a[:], ALU.add).then_inc(sp_sum, 1)
                dve.wait_ge(sp_sum, g + 1)
                if g >= 2:
                    dve.wait_ge(bar_ok, 2 * row(g - 1, 0))
                V.tensor_scalar(dt_sb[:, g % 2, :, :], sp_a[:], DT_MAX - DT_MIN, DT_MIN,
                                ALU.mult, ALU.add).then_inc(dt_ok, 1)
                dve.wait_ge(dt_ok, g + 1)
                dve.wait_ge(u_cp, 2 * g + 2)
                V.tensor_tensor(dtu[:], dt_sb[:, g % 2, :, :], u_sb[:], ALU.mult).then_inc(dtu_ok, 1)

            def pre_ux(g):
                dve.wait_ge(dtu_ok, g + 1)
                for j in range(KD):
                    V.scalar_tensor_tensor(out=u_sb[:, j, :], in0=u_sb[:, j, :], scalar=d_skip[:, j:j + 1],
                                           in1=xs_h[:, j, :].bitcast(F32), op0=ALU.mult,
                                           op1=ALU.add).then_inc(ux_h, 1)
                if g <= 1:
                    dve.wait_ge(ux_h, 2 * g + 2)
                    V.tensor_tensor(u_sb[:], u_sb[:], xs_l[:].bitcast(F32), ALU.add).then_inc(ux_l, 1)

            def pre_low(g):
                dve.wait_ge(dtu_hi, g + 1)
                V.tensor_tensor(dtu_l[:], dtu[:], dtu_h[:].bitcast(F32), ALU.subtract).then_inc(dtu_lo, 1)

            def pre_input(g):
                dve.wait_ge(g_ps, g + 1)
                dve.wait_ge(bc_cp, g + 1)
                V.tensor_tensor(bc_sb[0:64, :], gb[0:64, 2, :], bc_sb[0:64, :], ALU.mult).then_inc(inp_ok, 1)
                dve.wait_ge(inp_ok, g + 1)
                if g >= 2:
                    dve.wait_ge(ir_ok, row(g - 1, 0))
                V.tensor_copy(parts[:, g % 2, :], bc_sb[0:64, :]).then_inc(inp_hi, 1)
                dve.wait_ge(inp_hi, g + 1)
                V.tensor_tensor(parts[32:64, g % 2, :], bc_sb[32:64, :],
                                parts[32:64, g % 2, :].bitcast(F32), ALU.subtract).then_inc(inp_lo, 1)

            def scan(g, n):
                k = row(g, n)
                dve.wait_ge(ir_ok, k + 1)
                if k >= 4:
                    dve.wait_ge(acc_ok if k % 2 else pair_ok, (k - 4) // 2 + 1)
                if g % CPB:
                    dve.wait_ge(st_ok, kept(g - 1, n))
                for j in range(KD):
                    dve.wait_ge(bar_ok, 2 * k + j + 1)
                    V.tensor_tensor_scan(hst[:, k % 4, j, :], bar[:, k % 2, j, :], bi[:, k % 2, :],
                                         state[:, j, n:n + 1] if g % CPB else 0.0,
                                         ALU.mult, ALU.add).then_inc(scan_ok, 1)

            def keep_state(g, n):
                k = row(g, n)
                dve.wait_ge(scan_ok, 2 * k + 2)
                V.tensor_copy(state[:, :, n:n + 1], hst[:, k % 4, :, T - 1:T]).then_inc(st_ok, 1)

            def accumulate(g, m):
                k = row(g, 2 * m) // 2
                dve.wait_ge(pair_ok, k + 1)
                if m == 0:
                    dve.wait_ge(ux_l, g + 1)
                    if g >= 1:
                        dve.wait_ge(y_t, g)
                else:
                    dve.wait_ge(acc_ok, k)
                V.tensor_tensor(acc[:], u_sb[:] if m == 0 else acc[:], hst[:, (2 * k + 1) % 4, :, :],
                                ALU.add).then_inc(acc_ok, 1)

            def stats(q, src):
                for t in range(TT):
                    V.bn_stats(bnst[:, t, :], src[:, t, :]).then_inc(ln_bn, 1)
                dve.wait_ge(ln_bn, TT * (q + 1))
                for t in range(TT):
                    V.bn_aggr(mv[:, t, :], bnst[:, t, :]).then_inc(ln_mv, 1)
                dve.wait_ge(ln_mv, TT * (q + 1))
                V.tensor_scalar(nmean[:], mv[:, :, 0], -1.0, None, ALU.mult)
                V.tensor_scalar(veps[:], mv[:, :, 1], EPS, None, ALU.add).then_inc(ln_ve, 1)

            def stats_last(g):
                dve.wait_ge(lf_r, 2 * g + 2)
                for t in range(TT):
                    V.bn_stats(bnst_f[:, t, :], x13(g)[:, t, :]).then_inc(lf_bn, 1)
                dve.wait_ge(lf_bn, TT * (g + 1))
                for t in range(TT):
                    V.bn_aggr(mv_f[:, t, :], bnst_f[:, t, :]).then_inc(lf_mv, 1)
                dve.wait_ge(lf_mv, TT * (g + 1))
                V.tensor_scalar(nmean_f[:], mv_f[:, :, 0], -1.0, None, ALU.mult)
                V.tensor_scalar(veps_f[:], mv_f[:, :, 1], EPS, None, ALU.add).then_inc(lf_ve, 1)

            def xt_low(i, low, high):
                for k in range(KD):
                    dve.wait_ge(xt_hi, KD * i + k + 1)
                    V.tensor_tensor(low[:, k, :], gb[:, k, :], high[:, k, :].bitcast(F32),
                                    ALU.subtract).then_inc(xt_lo, 1)

            def two_banks(b0):
                return gb[:, b0:b0 + 2, :].rearrange("p a (t d) -> p (a t) d", d=D)

            inner = gb[:, 2, 0:TT * (HR + E)].rearrange("p (t w) -> p t w", t=TT)

            def router(g):
                v = 11 * g
                dve.wait_ge(cat_ps, g + 1)
                small(V.tensor_tensor(lg[:], inner[:, :, HR:], r_bias[:], ALU.add), rt, v + 1)
                small(V.tensor_reduce(lmax[:], lg[:], AX.X, ALU.max), rt, v + 2)
                V.tensor_tensor(ls[:], lg[:], lmax[:].unsqueeze(2).to_broadcast([P, TT, E]),
                                ALU.subtract).then_inc(lg_ok, 1)
                of_j = lg[:].unsqueeze(2).to_broadcast([P, TT, E, E])
                of_i = lg[:].unsqueeze(3).to_broadcast([P, TT, E, E])
                V.tensor_tensor(rk_gt[:], of_j, of_i, ALU.is_gt).then_inc(rt, 1)
                small(V.tensor_tensor(rk_eq[:], of_j, of_i, ALU.is_equal), rt, v + 4)
                small(V.tensor_tensor(rk_eq[:].rearrange("p t i j -> p t (i j)"),
                                      rk_eq[:].rearrange("p t i j -> p t (i j)"),
                                      tie[:].rearrange("p i j -> p (i j)").unsqueeze(1).to_broadcast([P, TT, E * E]),
                                      ALU.mult), rt, v + 5)
                small(V.tensor_tensor(rk_gt[:], rk_gt[:], rk_eq[:], ALU.add), rt, v + 6)
                small(V.tensor_reduce(rank[:], rk_gt[:], AX.X, ALU.add), rt, v + 7)
                dve.wait_ge(ex_ok, g + 1)
                small(V.scalar_tensor_tensor(out=em[:], in0=rank[:], scalar=1.5, in1=ex[:],
                                             op0=ALU.is_lt, op1=ALU.mult), rt, v + 8)
                V.tensor_reduce(e_sum[:], ex[:], AX.X, ALU.add)
                small(V.tensor_reduce(k_sum[:], em[:], AX.X, ALU.add), rt, v + 9)
                small(V.scalar_tensor_tensor(out=e_sum[:], in0=e_sum[:], scalar=1e-6, in1=k_sum[:],
                                             op0=ALU.mult, op1=ALU.add), rt, v + 10)
                small(V.reciprocal(k_sum[:], e_sum[:]), rt, v + 11)
                dve.wait_ge(consts, 12)
                V.tensor_tensor(gate[:, :, 0:E], em[:], k_sum[:].unsqueeze(2).to_broadcast([P, TT, E]),
                                ALU.mult).then_inc(lgate, 1)
                dve.wait_ge(lgate, g + 1)
                V.tensor_tensor(hw[:, :, 0:HR].rearrange("p t (e r) -> p t e r", r=R),
                                inner[:, :, 0:HR].rearrange("p t (e r) -> p t e r", r=R),
                                gate[:].unsqueeze(3).to_broadcast([P, TT, EP, R]), ALU.mult).then_inc(hw_ok, 1)

            def keys(g):
                c = g % CPB
                dve.wait_ge(q_hi, g + 1)
                dve.wait_ge(k_hi, g + 1)
                V.scalar_tensor_tensor(out=q_st[64:96, :], in0=gb[64:96, 2, :], scalar=b_sh[64:96, :],
                                       in1=q_st[64:96, :].bitcast(F32), op0=ALU.add,
                                       op1=ALU.subtract).then_inc(q_lo, 1)
                ks = k_st[32:64, c * T:(c + 1) * T]
                V.scalar_tensor_tensor(out=ks, in0=gb[32:64, 2, :], scalar=b_sh[32:64, :],
                                       in1=ks.bitcast(F32), op0=ALU.add, op1=ALU.subtract).then_inc(k_lo, 1)

            def block_max(g, i, kk):
                c = g % CPB
                j = i * (c + 1) + kk
                dve.wait_ge(s_ps, s_base[g] + j + 1)
                w = T if kk < c else (i + 1) * P
                V.tensor_reduce(smax[:, i, kk:kk + 1], gb[:, j % 3, 0:w], AX.X, ALU.max).then_inc(s_mx, 1)

            def maxima(g):
                c = g % CPB
                dve.wait_ge(s_mx, s_base[g] + n_s[g])
                small(V.tensor_reduce(m4[:], smax[:, :, 0:c + 1], AX.X, ALU.max), m_ok, g + 1)
                small(V.tensor_scalar(mhl[:, :, 0], m4[:], -1.0, None, ALU.mult), mhl_ok, 2 * g + 1)
                V.scalar_tensor_tensor(out=mhl[:, :, 1], in0=m4[:], scalar=-1.0, in1=mhl[:, :, 0].bitcast(F32),
                                       op0=ALU.mult, op1=ALU.subtract).then_inc(mhl_ok, 1)

            def finish_attention(g, h):
                dve.wait_ge(pv_ok, p_base[g][h] + n_p[g][h])
                dve.wait_ge(x2b_ok, g + 1)
                V.reciprocal(rl[:, 2 * h:2 * h + 2].unsqueeze(2), gb[:, 0:2, D:D + 1]).then_inc(rl_ok, 1)
                dve.wait_ge(rl_ok, 2 * g + h + 1)
                for ql in range(2):
                    i = 2 * h + ql
                    V.scalar_tensor_tensor(out=x2[:, i, :], in0=gb[:, ql, 0:D], scalar=rl[:, i:i + 1],
                                           in1=x2[:, i, :], op0=ALU.mult, op1=ALU.add).then_inc(o_res, 1)

            def mix(g, j):
                if not 1 <= j <= UNITS:
                    return
                k = g * UNITS + j - 1
                dve.wait_ge(a1_ok, k + 1)
                dve.wait_ge(a0_ok, k + 1)
                if k >= 2:
                    dve.wait_ge(mid_used, k - 1)
                V.scalar_tensor_tensor(out=mid[:, k % 2, :], in0=aring[:, 2 * k % 3, :], scalar=sgn01[:, 0:1],
                                       in1=aring[:, (2 * k + 1) % 3, :], op0=ALU.mult,
                                       op1=ALU.add).then_inc(mid_ok, 1)

            def residual_last(g, half):
                dve.wait_ge(mid_used, UNITS * g + 4 * (half + 1))
                x = x13(g)[:, 2 * half:2 * half + 2, :].rearrange("p t d -> p (t d)")
                V.scalar_tensor_tensor(out=x, in0=gb[:, 5, :], scalar=sgn[:, 1:2], in1=x,
                                       op0=ALU.mult, op1=ALU.add).then_inc(lf_r, 1)

            pre_x(0)
            dve.wait_ge(wd, 2)
            dve.wait_ge(wp_act, 4)
            V.tensor_tensor(a_l[:], a_rep, a_h[:].bitcast(F32), ALU.subtract).then_inc(wp_dve, 1)
            pre_max(0)
            pre_dt(0)
            pre_ux(0)
            pre_low(0)
            dve.wait_ge(ld_att, 6 * 16)
            dve.wait_ge(ld_ffn, 8 * 16)
            V.tensor_copy(bv_rep, bv_col[:].unsqueeze(2).to_broadcast([P, KD, P]))
            V.memset(sel_a128, 0.0)
            V.memset(sel_0, 0.0)
            V.tensor_scalar(sgn[:], top_v[:], 0.0, None, ALU.is_ge)
            small(V.tensor_copy(top_f[:], top_i[:]), wd, 4)
            V.tensor_scalar(sgn[:], sgn[:], 2.0, -1.0, ALU.mult, ALU.add)
            small(V.tensor_scalar(picked[:], top_f[:], expert_of[:, 0:1], None, ALU.is_equal), wd, 5)
            V.tensor_tensor(absv[:], top_v[:], sgn[:], ALU.mult)
            V.tensor_tensor(sgn01[:], sgn[:, 0:1], sgn[:, 1:2], ALU.mult)
            small(V.tensor_scalar(minus0[:], picked[:, 0:1], -1.0, None, ALU.mult), wd, 6)
            for q in range(3):
                c0 = 32 * q
                V.tensor_scalar(sel_a128[:, c0:c0 + R], pick_cols[:], picked[:, 0:1], None, ALU.mult)
                V.tensor_scalar(sel_a128[:, c0 + R:c0 + 2 * R], pick_cols[:], picked[:, 1:2], None, ALU.mult)
                V.tensor_scalar(sel_0[:, c0:c0 + R], pick_cols[:], picked[:, 0:1], None, ALU.mult)
                V.tensor_scalar(sel_d[:, c0:c0 + R], pick_cols[:], minus0[:, 0:1], None, ALU.mult)
                ins = V.tensor_scalar(sel_d[:, c0 + R:c0 + 2 * R], pick_cols[:], picked[:, 1:2], None, ALU.mult)
            ins.then_inc(wp_dve, 1)
            pre_input(0)

            def later_weights(i):
                if i == 1:
                    dve.wait_ge(wa, 2)
                    V.tensor_tensor(w_vo_l[:], gb[:, 1, :].rearrange("p (k n) -> p k n", k=KD),
                                    w_vo_h[:].bitcast(F32), ALU.subtract).then_inc(wp_dve, 1)
                elif i == 2:
                    dve.wait_ge(wp_act, 6)
                    V.tensor_tensor(w_la_l[:], gb[:, 2, 0:2 * P].rearrange("p (k n) -> p k n", k=KD),
                                    w_la_h[:].bitcast(F32), ALU.subtract).then_inc(wp_dve, 1)
                elif i == 3:
                    dve.wait_ge(wp_act, 7)
                    V.tensor_tensor(w_z0[32:64, :], gb[32:64, 0:2, :].rearrange("p k t -> p (k t)"),
                                    w_z0[32:64, :].bitcast(F32), ALU.subtract).then_inc(wp_dve, 1)
                elif i == 4:
                    dve.wait_ge(wp_act, 8)
                    V.tensor_tensor(w_zd[32:64, :], gb[32:64, 4:6, :].rearrange("p k t -> p (k t)"),
                                    w_zd[32:64, :].bitcast(F32), ALU.subtract).then_inc(wp_dve, 1)

            for s in range(NCH + 2):
                g, r, f, p = s, s - 1, s - 2, s + 1

                def state_row(n):
                    if g < NCH:
                        scan(g, n)
                    if n % 2 and n >= 3:
                        accumulate(g, n // 2 - 1)
                    elif n == 1 and g >= 1:
                        accumulate(g - 1, N // 2 - 1)
                    if g < NCH and g % CPB != CPB - 1:
                        keep_state(g, n)

                def unit(j):
                    if j <= UNITS:
                        mix(f, j)
                        if j == 5:
                            residual_last(f, 0)
                    else:
                        residual_last(f, 1)
                        stats_last(f)

                main, ffn, c = 0 <= r < NCH, 0 <= f, r % CPB
                until = pacer(N if g < NCH else 2 if g == NCH else 0, state_row, [
                    at(c, 0.2, 0.2), at(c, 1.66, 1.66), at(c, 3.2, 3), at(c, 4.37, 3.61), at(c, 6.8, 6.68),
                    at(c, 9.97, 8.59), at(c, 10.34, 9.85), at(c, 13.14, 11.98), at(c, 13.55, 13.55), at(c, 15.52, 15.52),
                ] if ffn else [], unit)
                if s == 0:
                    for i in range(5):
                        until(0.83 * i + 0.5)
                        later_weights(i)
                    for t, part in ((3.56, pre_x), (7.2, pre_max), (3.07, pre_dt), (9.75, pre_ux), (10.4, pre_low),
                                    (12, pre_input)):
                        until(t)
                        part(p)
                if main:
                    until(at(c, 1.2, 1.2))
                    dve.wait_ge(y_t, r + 1)
                    stats(3 * r, two_banks(0))
                    until(at(c, 2.7, 2.5))
                    xt_low(3 * r, xt_l, xt_h)
                    until(at(c, 3.68, 3.09))
                    router(r)
                    until(at(c, 5.15, 4.45))
                    dve.wait_ge(hwt_ps, r + 1)
                    dve.wait_ge(hw_hi, r + 1)
                    V.tensor_tensor(hw_l, gb[0:HR + 1, 2, :], hw_h.bitcast(F32), ALU.subtract).then_inc(hw_lo, 1)
                    until(at(c, 6.15, 5.19))
                    dve.wait_ge(up_ps, r + 1)
                    V.tensor_tensor(x13(r), two_banks(0), x13(r), ALU.add).then_inc(ln_r, 1)
                    dve.wait_ge(ln_r, r + 1)
                    stats(3 * r + 1, x13(r))
                    if p < NCH:
                        until(at(c, 5.58, 5.02))
                        pre_x(p)
                        until(at(c, 9.4, 6.79))
                        pre_max(p)
                    until(at(c, 9.72, 7.65))
                    xt_low(3 * r + 1, xt_l, xt_h)
                    if p < NCH:
                        until(at(c, 9.23, 6.23))
                        pre_dt(p)
                        until(at(c, 9.11, 6.69))
                        pre_ux(p)
                    until(at(c, 9.66, 8.68))
                    keys(r)
                    for i in range(TT):
                        for kk in range(c + 1):
                            until(at(c, 9.29, 9.01) + at(c, 0.37, 0.67) * (i * (c + 1) + kk) / n_s[r])
                            block_max(r, i, kk)
                    maxima(r)
                    until(at(c, 12.45, 10.48))
                    finish_attention(r, 0)
                    until(at(c, 13.3, 13.45))
                    finish_attention(r, 1)
                    dve.wait_ge(o_res, TT * (r + 1))
                    stats(3 * r + 2, x2)
                    if p < NCH:
                        until(at(c, 14.15, 14.05))
                        pre_input(p)
                    until(at(c, 15.25, 15.25), UNITS + 1)
                    xt_low(3 * r + 2, xf_l, xf_h)
                    until(at(c, 15.75, 15.75))
                    dve.wait_ge(l_hi, r + 1)
                    V.tensor_tensor(lr[64:96, :], gb[64:96, 2, :], lr[64:96, :].bitcast(F32),
                                    ALU.subtract).then_inc(l_lo, 1)
                until(1e9)


def _layout(i):
    import numpy as np

    f = {k: np.ascontiguousarray(v) for k, v in i.items() if np.asarray(v).size}

    def pad(w, at, width):
        out = np.zeros((w.shape[0], width), w.dtype)
        for c in at:
            out[:, c:c + w.shape[1]] = w
        return out

    def by_partition(v):
        return np.ascontiguousarray(v.reshape(KD, P, -1).transpose(1, 0, 2)).reshape(P, KD, -1)

    w_x = f["L0_attn_w_x"]
    idx = np.arange(P)
    eye = np.eye(R, dtype=np.float32)
    sel = np.zeros((64, N), np.float32)
    for n in range(N):
        sel[[n, 32 + n], n] = 1
    w_bc = pad(w_x[:, 64:80], (0, 32), P)
    w_bc[:, 64:80] = w_x[:, 80:96]
    sh = f["L1_attn_b_share"]
    b_sh = np.zeros((P, 1), sh.dtype)
    for c in (0, 32, 64):
        b_sh[c:c + 16, 0] = sh
    return {
        "x": f["L0_attn_x"].transpose(0, 2, 1),
        "w_in": f["L0_attn_w_in"], "w_in_t": f["L0_attn_w_in"].T,
        "w_xdt_t": w_x[:, :64].T, "w_dt": f["L0_attn_w_dt"], "w_bc": w_bc,
        "b_dt": by_partition(f["L0_attn_b_dt"])[:, :, 0], "d_skip": by_partition(f["L0_attn_Dp"])[:, :, 0],
        "a_log": by_partition(f["L0_attn_A_log"]), "sel_cols": sel,
        "w_cat": np.concatenate([f["L0_ffn_base_W"].T, f["L0_ffn_routed_A"].reshape(E * R, D).T,
                                 f["L0_ffn_shared_A"].T, f["L0_ffn_router_W"].T], 1),
        "w_up": np.concatenate([f["L0_ffn_routed_B"].transpose(0, 2, 1).reshape(E * R, D),
                                f["L0_ffn_shared_B"].T, f["L0_ffn_base_b"][None]], 0),
        "r_bias": np.broadcast_to(f["L0_ffn_router_b"], (P, TT, E)),
        "tie": np.broadcast_to(np.tril(np.ones((E, E), np.float32), -1), (P, E, E)),
        "w_sh": pad(f["L1_attn_W_share"], (0, 32, 64), P), "b_sh": b_sh,
        "w_v_t": f["L1_attn_Wv"].T, "w_o": f["L1_attn_Wo"],
        "bv": by_partition(f["L1_attn_bv"])[:, :, 0], "bo": f["L1_attn_bo"][None],
        "w_i_t": f["L1_ffn_wi_w"].T, "w_out_t": f["L1_ffn_wo_w"].T,
        "lora_a": f["L1_ffn_lora_As"].reshape(P, D),
        "lora_b": f["L1_ffn_lora_Bs"].transpose(0, 2, 1).reshape(P, FF),
        "pick_cols": eye[idx % R], "expert_of": (idx // R).astype(np.float32)[:, None],
        "top_i": np.broadcast_to(f["L1_ffn_top_k_indices"], (P, 2)),
        "top_v": np.broadcast_to(f["L1_ffn_top_k_values"], (P, 2)),
    }


def kernel(**inputs):
    import numpy as np
    import concourse.bacc as bacc
    from concourse.bass_utils import run_bass_kernel_spmd

    nc = bacc.Bacc("TRN2", target_bir_lowering=False, num_devices=1)
    arrays, args = {}, {}
    for name, v in _layout(inputs).items():
        v = np.ascontiguousarray(v)
        arrays[f"in_{name}"] = v
        args[name] = nc.dram_tensor(f"in_{name}", v.shape, mybir.dt.from_np(v.dtype), kind="ExternalInput").ap()
    args["out"] = nc.dram_tensor("out_x", (B, S, D), F32, kind="ExternalOutput").ap()
    args["c_rows"] = nc.dram_tensor("c_rows", (2, N, T), F32, kind="Internal").ap()
    program(nc, args)
    return run_bass_kernel_spmd(nc, [arrays], core_ids=[0]).results[0]["out_x"]
```
